# Optimizing a Trainium2 kernel written in Bass

```python
import numpy as np
import jax
import jax.numpy as jnp

def _softmax(x, axis=-1):
    return jax.nn.softmax(x, axis=axis)

def _gelu(x):
    return jax.nn.gelu(x, approximate=True)

def _silu(x):
    return jax.nn.silu(x)

def _sigmoid(x):
    return jax.nn.sigmoid(x)

def _layernorm(x, axis=-1, eps=1e-05):
    m = jnp.mean(x, axis=axis, keepdims=True)
    v = jnp.var(x, axis=axis, keepdims=True)
    return (x - m) / jnp.sqrt(v + eps)

def _scatter_add(tgt, idx, src, axis=0):
    return tgt.at[idx].add(src)

def _segment_sum(src, seg, n):
    return jax.ops.segment_sum(src, seg, n)
kernel_name = 'mk_seq_preln_d1_jaxref_r4_7a17e5'

def setup_inputs(seed: int=0):
    np.random.seed(seed)
    _w = jnp.asarray

    def _L0_attn_setup():
        import jax, jax.numpy as jnp
        import numpy as np
        from jax import lax
        N_HEADS = 16
        EPS = 1e-06
        CHUNK = 128

        def causal_dot_product(q, k, v):
            B, H, L, D = q.shape
            M = v.shape[-1]
            nc = L // CHUNK
            qc = q.reshape(B, H, nc, CHUNK, D).transpose(2, 0, 1, 3, 4)
            kc = k.reshape(B, H, nc, CHUNK, D).transpose(2, 0, 1, 3, 4)
            vc = v.reshape(B, H, nc, CHUNK, M).transpose(2, 0, 1, 3, 4)

            def step(kv_carry, inp):
                qb, kb, vb = inp
                kv = jnp.einsum('bhcd,bhcm->bhcdm', kb, vb)
                kv_cum = jnp.cumsum(kv, axis=2) + kv_carry[:, :, None]
                out = jnp.einsum('bhcd,bhcdm->bhcm', qb, kv_cum)
                return (kv_cum[:, :, -1], out)
            init = jnp.zeros((B, H, D, M), q.dtype)
            _, outs = lax.scan(step, init, (qc, kc, vc))
            return outs.transpose(1, 2, 0, 3, 4).reshape(B, H, L, M)

        def flow_attention_causal(x, Wq, bq, Wk, bk, Wv, bv, Wo, bo):
            B, L, _ = x.shape
            d_model = Wq.shape[1]
            H = N_HEADS
            q = (x @ Wq + bq).reshape(B, L, H, -1).transpose(0, 2, 1, 3)
            k = (x @ Wk + bk).reshape(B, L, H, -1).transpose(0, 2, 1, 3)
            v = (x @ Wv + bv).reshape(B, L, H, -1).transpose(0, 2, 1, 3)
            q = jax.nn.sigmoid(q)
            k = jax.nn.sigmoid(k)
            sink_incoming = 1.0 / jnp.einsum('bhld,bhld->bhl', q + EPS, jnp.cumsum(k, axis=2) + EPS)
            source_outgoing = 1.0 / jnp.einsum('bhld,bhld->bhl', k + EPS, jnp.cumsum(q, axis=2) + EPS)
            normal = (jnp.arange(L, dtype=x.dtype) + 1.0)[None, None, :]
            sink_incoming = sink_incoming * normal
            source_outgoing = source_outgoing * normal
            conserved_sink = jnp.einsum('bhld,bhld->bhl', q + EPS, jnp.cumsum(k * source_outgoing[..., None], axis=2) + EPS) / normal
            conserved_source = jnp.einsum('bhld,bhld->bhl', k + EPS, jnp.cumsum(q * sink_incoming[..., None], axis=2) + EPS) / normal
            sink_allocation = jax.nn.sigmoid(conserved_sink)
            cs = jnp.exp(conserved_source)
            source_competition = cs / jnp.cumsum(cs, axis=-1) * normal
            out = causal_dot_product(q * (sink_incoming / normal)[..., None], k, v * source_competition[..., None]) * sink_allocation[..., None]
            out = out.transpose(0, 2, 1, 3).reshape(B, L, d_model)
            return out @ Wo + bo
        key = jax.random.key(seed)
        ks = jax.random.split(key, 9)
        B, L, d_model = (4, 1024, 256)
        s = 0.02
        return {'x': jax.random.normal(ks[0], (B, L, d_model), dtype=jnp.float32), 'Wq': jax.random.normal(ks[1], (d_model, d_model), dtype=jnp.float32) * s, 'bq': jnp.zeros((d_model,), dtype=jnp.float32), 'Wk': jax.random.normal(ks[2], (d_model, d_model), dtype=jnp.float32) * s, 'bk': jnp.zeros((d_model,), dtype=jnp.float32), 'Wv': jax.random.normal(ks[3], (d_model, d_model), dtype=jnp.float32) * s, 'bv': jnp.zeros((d_model,), dtype=jnp.float32), 'Wo': jax.random.normal(ks[4], (d_model, d_model), dtype=jnp.float32) * s, 'bo': jnp.zeros((d_model,), dtype=jnp.float32)}
    _L0_attn_in = _L0_attn_setup()

    def _L0_ffn_setup():
        import jax, jax.numpy as jnp
        import numpy as np
        DIM = 256
        DEPTH = 2
        HEADS = 8
        DIM_HEAD = 64
        WINDOW = 128
        INNER = HEADS * DIM_HEAD
        HID = int(DIM * 4 * 2 / 3)
        B, N = (2, 2048)
        QK_SCALE = 8.0

        def shift_token(t):
            t1, t2 = jnp.split(t, 2, axis=-1)
            t2 = jnp.pad(t2, ((0, 0), (1, 0), (0, 0)))[:, :-1]
            return jnp.concatenate([t1, t2], axis=-1)

        def l2norm(t):
            return t / jnp.clip(jnp.linalg.norm(t, axis=-1, keepdims=True), 1e-12)

        def rotate_half(x):
            x1, x2 = jnp.split(x, 2, axis=-1)
            return jnp.concatenate([-x2, x1], axis=-1)

        def rotary_xpos(q, k):
            n = q.shape[-2]
            half_idx = jnp.arange(0, DIM_HEAD, 2, dtype=jnp.float32)
            inv_freq = 1.0 / 10000.0 ** (half_idx / DIM_HEAD)
            t = jnp.arange(n, dtype=jnp.float32)
            freqs = t[:, None] * inv_freq[None, :]
            freqs = jnp.concatenate([freqs, freqs], axis=-1)
            base = (half_idx + 0.4 * DIM_HEAD) / (1.4 * DIM_HEAD)
            power = (t - n // 2) / float(WINDOW // 2)
            scale = base[None, :] ** power[:, None]
            scale = jnp.concatenate([scale, scale], axis=-1)
            cos, sin = (jnp.cos(freqs), jnp.sin(freqs))
            q = q * cos * scale + rotate_half(q) * sin * scale
            k = k * cos / scale + rotate_half(k) * sin / scale
            return (q, k)

        def local_attention(q, k, v):
            b, h, n, d = q.shape
            w = n // WINDOW
            bq = q.reshape(b, h, w, WINDOW, d) * QK_SCALE
            bk = k.reshape(b, h, w, WINDOW, d)
            bv = v.reshape(b, h, w, WINDOW, d)

            def look_around(t):
                p = jnp.pad(t, ((0, 0), (0, 0), (1, 0), (0, 0), (0, 0)))
                return jnp.concatenate([p[:, :, :w], p[:, :, 1:]], axis=3)
            bk, bv = (look_around(bk), look_around(bv))
            bt = jnp.arange(n).reshape(w, WINDOW)
            btp = jnp.pad(bt, ((1, 0), (0, 0)), constant_values=-1)
            btk = jnp.concatenate([btp[:w], btp[1:]], axis=1)
            sim = jnp.einsum('bhwid,bhwjd->bhwij', bq, bk)
            i = bt[:, :, None]
            j = btk[:, None, :]
            mask = (i < j) | (i > j + WINDOW) | (j == -1)
            sim = jnp.where(mask, -jnp.finfo(sim.dtype).max, sim)
            attn = jax.nn.softmax(sim, axis=-1)
            out = jnp.einsum('bhwij,bhwjd->bhwid', attn, bv)
            return out.reshape(b, h, n, d)

        def _layer(x, wqkv, qs, ksc, wo, lg, lb, w1, b1, w2, b2):
            b, n, _ = x.shape
            h = shift_token(x)
            qkv = h @ wqkv
            q, k, v = jnp.split(qkv, 3, axis=-1)
            to_heads = lambda t: t.reshape(b, n, HEADS, DIM_HEAD).transpose(0, 2, 1, 3)
            q, k, v = (to_heads(q), to_heads(k), to_heads(v))
            q = l2norm(q) * qs
            k = l2norm(k) * ksc
            q, k = rotary_xpos(q, k)
            o = local_attention(q, k, v)
            o = o.transpose(0, 2, 1, 3).reshape(b, n, INNER)
            x = x + o @ wo
            h = shift_token(x)
            mu = h.mean(-1, keepdims=True)
            var = h.var(-1, keepdims=True)
            h = (h - mu) / jnp.sqrt(var + 1e-05) * lg + lb
            h = h @ w1 + b1
            a, g = jnp.split(h, 2, axis=-1)
            h = a * jax.nn.gelu(g, approximate=False)
            x = x + h @ w2 + b2
            return x
        key = jax.random.key(seed)
        ks = jax.random.split(key, 6)
        return {'x': jax.random.normal(ks[0], (B, N, DIM), jnp.float32), 'wqkv': jax.random.normal(ks[1], (DEPTH, DIM, 3 * INNER), jnp.float32) * 0.02, 'q_scale': jnp.ones((DEPTH, DIM_HEAD), jnp.float32), 'k_scale': jnp.ones((DEPTH, DIM_HEAD), jnp.float32), 'wo': jax.random.normal(ks[2], (DEPTH, INNER, DIM), jnp.float32) * 0.02, 'ln_g': jnp.ones((DEPTH, DIM), jnp.float32), 'ln_b': jnp.zeros((DEPTH, DIM), jnp.float32), 'w1': jax.random.normal(ks[3], (DEPTH, DIM, 2 * HID), jnp.float32) * 0.02, 'b1': jnp.zeros((DEPTH, 2 * HID), jnp.float32), 'w2': jax.random.normal(ks[4], (DEPTH, HID, DIM), jnp.float32) * 0.02, 'b2': jnp.zeros((DEPTH, DIM), jnp.float32)}
    _L0_ffn_in = _L0_ffn_setup()
    _d = {'L0_attn_x': _L0_attn_in['x'], 'L0_attn_Wq': _L0_attn_in['Wq'], 'L0_attn_bq': _L0_attn_in['bq'], 'L0_attn_Wk': _L0_attn_in['Wk'], 'L0_attn_bk': _L0_attn_in['bk'], 'L0_attn_Wv': _L0_attn_in['Wv'], 'L0_attn_bv': _L0_attn_in['bv'], 'L0_attn_Wo': _L0_attn_in['Wo'], 'L0_attn_bo': _L0_attn_in['bo'], 'L0_ffn_wqkv': _L0_ffn_in['wqkv'], 'L0_ffn_q_scale': _L0_ffn_in['q_scale'], 'L0_ffn_k_scale': _L0_ffn_in['k_scale'], 'L0_ffn_wo': _L0_ffn_in['wo'], 'L0_ffn_ln_g': _L0_ffn_in['ln_g'], 'L0_ffn_ln_b': _L0_ffn_in['ln_b'], 'L0_ffn_w1': _L0_ffn_in['w1'], 'L0_ffn_b1': _L0_ffn_in['b1'], 'L0_ffn_w2': _L0_ffn_in['w2'], 'L0_ffn_b2': _L0_ffn_in['b2']}
    _x0 = _d['L0_attn_x']
    _d['L0_attn_x'] = jax.random.normal(jax.random.fold_in(jax.random.key(seed), 1), (2, 2048, 256), dtype=_x0.dtype)
    del _x0
    return _d

def reference(L0_attn_x, L0_attn_Wq, L0_attn_bq, L0_attn_Wk, L0_attn_bk, L0_attn_Wv, L0_attn_bv, L0_attn_Wo, L0_attn_bo, L0_ffn_wqkv, L0_ffn_q_scale, L0_ffn_k_scale, L0_ffn_wo, L0_ffn_ln_g, L0_ffn_ln_b, L0_ffn_w1, L0_ffn_b1, L0_ffn_w2, L0_ffn_b2):

    def _L0_attn_ref(x, Wq, bq, Wk, bk, Wv, bv, Wo, bo):
        import jax, jax.numpy as jnp
        import numpy as np
        from jax import lax
        N_HEADS = 16
        EPS = 1e-06
        CHUNK = 128

        def causal_dot_product(q, k, v):
            B, H, L, D = q.shape
            M = v.shape[-1]
            nc = L // CHUNK
            qc = q.reshape(B, H, nc, CHUNK, D).transpose(2, 0, 1, 3, 4)
            kc = k.reshape(B, H, nc, CHUNK, D).transpose(2, 0, 1, 3, 4)
            vc = v.reshape(B, H, nc, CHUNK, M).transpose(2, 0, 1, 3, 4)

            def step(kv_carry, inp):
                qb, kb, vb = inp
                kv = jnp.einsum('bhcd,bhcm->bhcdm', kb, vb)
                kv_cum = jnp.cumsum(kv, axis=2) + kv_carry[:, :, None]
                out = jnp.einsum('bhcd,bhcdm->bhcm', qb, kv_cum)
                return (kv_cum[:, :, -1], out)
            init = jnp.zeros((B, H, D, M), q.dtype)
            _, outs = lax.scan(step, init, (qc, kc, vc))
            return outs.transpose(1, 2, 0, 3, 4).reshape(B, H, L, M)

        def flow_attention_causal(x, Wq, bq, Wk, bk, Wv, bv, Wo, bo):
            B, L, _ = x.shape
            d_model = Wq.shape[1]
            H = N_HEADS
            q = (x @ Wq + bq).reshape(B, L, H, -1).transpose(0, 2, 1, 3)
            k = (x @ Wk + bk).reshape(B, L, H, -1).transpose(0, 2, 1, 3)
            v = (x @ Wv + bv).reshape(B, L, H, -1).transpose(0, 2, 1, 3)
            q = jax.nn.sigmoid(q)
            k = jax.nn.sigmoid(k)
            sink_incoming = 1.0 / jnp.einsum('bhld,bhld->bhl', q + EPS, jnp.cumsum(k, axis=2) + EPS)
            source_outgoing = 1.0 / jnp.einsum('bhld,bhld->bhl', k + EPS, jnp.cumsum(q, axis=2) + EPS)
            normal = (jnp.arange(L, dtype=x.dtype) + 1.0)[None, None, :]
            sink_incoming = sink_incoming * normal
            source_outgoing = source_outgoing * normal
            conserved_sink = jnp.einsum('bhld,bhld->bhl', q + EPS, jnp.cumsum(k * source_outgoing[..., None], axis=2) + EPS) / normal
            conserved_source = jnp.einsum('bhld,bhld->bhl', k + EPS, jnp.cumsum(q * sink_incoming[..., None], axis=2) + EPS) / normal
            sink_allocation = jax.nn.sigmoid(conserved_sink)
            cs = jnp.exp(conserved_source)
            source_competition = cs / jnp.cumsum(cs, axis=-1) * normal
            out = causal_dot_product(q * (sink_incoming / normal)[..., None], k, v * source_competition[..., None]) * sink_allocation[..., None]
            out = out.transpose(0, 2, 1, 3).reshape(B, L, d_model)
            return out @ Wo + bo
        return flow_attention_causal(x, Wq, bq, Wk, bk, Wv, bv, Wo, bo)

    def _L0_ffn_ref(x, wqkv, q_scale, k_scale, wo, ln_g, ln_b, w1, b1, w2, b2):
        import jax, jax.numpy as jnp
        import numpy as np
        DIM = 256
        DEPTH = 2
        HEADS = 8
        DIM_HEAD = 64
        WINDOW = 128
        INNER = HEADS * DIM_HEAD
        HID = int(DIM * 4 * 2 / 3)
        B, N = (2, 2048)
        QK_SCALE = 8.0

        def shift_token(t):
            t1, t2 = jnp.split(t, 2, axis=-1)
            t2 = jnp.pad(t2, ((0, 0), (1, 0), (0, 0)))[:, :-1]
            return jnp.concatenate([t1, t2], axis=-1)

        def l2norm(t):
            return t / jnp.clip(jnp.linalg.norm(t, axis=-1, keepdims=True), 1e-12)

        def rotate_half(x):
            x1, x2 = jnp.split(x, 2, axis=-1)
            return jnp.concatenate([-x2, x1], axis=-1)

        def rotary_xpos(q, k):
            n = q.shape[-2]
            half_idx = jnp.arange(0, DIM_HEAD, 2, dtype=jnp.float32)
            inv_freq = 1.0 / 10000.0 ** (half_idx / DIM_HEAD)
            t = jnp.arange(n, dtype=jnp.float32)
            freqs = t[:, None] * inv_freq[None, :]
            freqs = jnp.concatenate([freqs, freqs], axis=-1)
            base = (half_idx + 0.4 * DIM_HEAD) / (1.4 * DIM_HEAD)
            power = (t - n // 2) / float(WINDOW // 2)
            scale = base[None, :] ** power[:, None]
            scale = jnp.concatenate([scale, scale], axis=-1)
            cos, sin = (jnp.cos(freqs), jnp.sin(freqs))
            q = q * cos * scale + rotate_half(q) * sin * scale
            k = k * cos / scale + rotate_half(k) * sin / scale
            return (q, k)

        def local_attention(q, k, v):
            b, h, n, d = q.shape
            w = n // WINDOW
            bq = q.reshape(b, h, w, WINDOW, d) * QK_SCALE
            bk = k.reshape(b, h, w, WINDOW, d)
            bv = v.reshape(b, h, w, WINDOW, d)

            def look_around(t):
                p = jnp.pad(t, ((0, 0), (0, 0), (1, 0), (0, 0), (0, 0)))
                return jnp.concatenate([p[:, :, :w], p[:, :, 1:]], axis=3)
            bk, bv = (look_around(bk), look_around(bv))
            bt = jnp.arange(n).reshape(w, WINDOW)
            btp = jnp.pad(bt, ((1, 0), (0, 0)), constant_values=-1)
            btk = jnp.concatenate([btp[:w], btp[1:]], axis=1)
            sim = jnp.einsum('bhwid,bhwjd->bhwij', bq, bk)
            i = bt[:, :, None]
            j = btk[:, None, :]
            mask = (i < j) | (i > j + WINDOW) | (j == -1)
            sim = jnp.where(mask, -jnp.finfo(sim.dtype).max, sim)
            attn = jax.nn.softmax(sim, axis=-1)
            out = jnp.einsum('bhwij,bhwjd->bhwid', attn, bv)
            return out.reshape(b, h, n, d)

        def _layer(x, wqkv, qs, ksc, wo, lg, lb, w1, b1, w2, b2):
            b, n, _ = x.shape
            h = shift_token(x)
            qkv = h @ wqkv
            q, k, v = jnp.split(qkv, 3, axis=-1)
            to_heads = lambda t: t.reshape(b, n, HEADS, DIM_HEAD).transpose(0, 2, 1, 3)
            q, k, v = (to_heads(q), to_heads(k), to_heads(v))
            q = l2norm(q) * qs
            k = l2norm(k) * ksc
            q, k = rotary_xpos(q, k)
            o = local_attention(q, k, v)
            o = o.transpose(0, 2, 1, 3).reshape(b, n, INNER)
            x = x + o @ wo
            h = shift_token(x)
            mu = h.mean(-1, keepdims=True)
            var = h.var(-1, keepdims=True)
            h = (h - mu) / jnp.sqrt(var + 1e-05) * lg + lb
            h = h @ w1 + b1
            a, g = jnp.split(h, 2, axis=-1)
            h = a * jax.nn.gelu(g, approximate=False)
            x = x + h @ w2 + b2
            return x
        for l in range(DEPTH):
            x = _layer(x, wqkv[l], q_scale[l], k_scale[l], wo[l], ln_g[l], ln_b[l], w1[l], b1[l], w2[l], b2[l])
        return x
    x = L0_attn_x
    x = x + _L0_attn_ref(_layernorm(x, axis=-1), L0_attn_Wq, L0_attn_bq, L0_attn_Wk, L0_attn_bk, L0_attn_Wv, L0_attn_bv, L0_attn_Wo, L0_attn_bo)
    x = x + _L0_ffn_ref(_layernorm(x, axis=-1), L0_ffn_wqkv, L0_ffn_q_scale, L0_ffn_k_scale, L0_ffn_wo, L0_ffn_ln_g, L0_ffn_ln_b, L0_ffn_w1, L0_ffn_b1, L0_ffn_w2, L0_ffn_b2)
    return x

_drawn_inputs = setup_inputs


def setup_inputs(seed=0):
    import zlib

    import numpy as np

    out = dict(_drawn_inputs(seed))
    spreads = {'L0_attn_bq': (0.0, 0.8),
     'L0_attn_bk': (0.0, 0.8),
     'L0_attn_bv': (0.0, 0.338),
     'L0_attn_bo': (0.0, 0.1),
     'L0_ffn_q_scale': (1.0, 0.6),
     'L0_ffn_k_scale': (1.0, 0.6),
     'L0_ffn_ln_g': (1.0, 0.6),
     'L0_ffn_ln_b': (0.0, 0.8),
     'L0_ffn_b1': (0.0, 0.8),
     'L0_ffn_b2': (0.0, 0.1)}
    factors = {'L0_attn_Wq': 8.0,
     'L0_attn_Wk': 8.0,
     'L0_attn_Wv': 8.0,
     'L0_ffn_wqkv': 3.188,
     'L0_ffn_wo': 3.034}
    for name, (base, spread) in spreads.items():
        noise = np.random.default_rng([zlib.crc32(name.encode()), seed]).standard_normal(out[name].shape)
        drawn = base * np.exp(spread * noise) if base else spread * noise
        out[name] = jnp.asarray(drawn.astype(out[name].dtype))
    for name, factor in factors.items():
        out[name] = (out[name] * factor).astype(out[name].dtype)
    return out
```

```python
from contextlib import ExitStack

import concourse.bass as bass
import numpy as np
from concourse import mybir

F32 = mybir.dt.float32
F32R = mybir.dt.float32r
BF16 = mybir.dt.bfloat16
ALU = mybir.AluOpType
ACT = mybir.ActivationFunctionType
AX = mybir.AxisListType

P = 128
D = 256
DC = D // P
B = 2
HEADS = 8
DH = 64
INNER = HEADS * DH
HALF = DH // 2
HID = int(D * 4 * 2 / 3)
NF = 6
FS = -(-HID // NF)
FLAST = HID - (NF - 1) * FS
FC = [FS] * (NF - 1) + [FLAST]
WINDOW = 128
QK_SCALE = 8.0
LN_EPS = 1e-5
FH = 16
FD = D // FH
FLOW_EPS = 1e-6
NEG = -3.0e38


def position_tables(n):
    f = np.float32
    half = np.arange(0, DH, 2, dtype=f)
    inv_freq = (f(1.0) / f(10000.0) ** (half / f(DH))).astype(f)
    t = np.arange(n, dtype=f)
    fr = t[:, None] * inv_freq[None, :]
    base = (half + f(0.4 * DH)) / f(1.4 * DH)
    power = (t - f(n // 2)) / f(WINDOW // 2)
    scale = base[None, :] ** power[:, None]
    cos, sin = np.cos(fr), np.sin(fr)
    out = np.empty((n, 4, 2, HALF), f)
    for kind, s in ((0, scale * f(QK_SCALE)), (1, f(1.0) / scale)):
        out[:, kind, 0] = out[:, kind, 1] = cos * s
        out[:, 2 + kind, 0] = -sin * s
        out[:, 2 + kind, 1] = sin * s
    return out.reshape(n, 4, DH)


def window_masks():
    i = np.arange(P)[:, None]
    j = np.arange(P)[None, :]
    own = np.where(j <= i, 0.0, NEG)
    front = np.where(j >= i, 0.0, NEG)
    none = np.full((P, P), NEG)
    one = np.stack([np.stack([own, front]), np.stack([front, own]), np.stack([own, none])])
    m = np.broadcast_to(one.transpose(2, 0, 1, 3)[:, :, None], (P, 3, 2, 2, P))
    return np.ascontiguousarray(m).astype(np.float32).reshape(P, -1)


def flow_masks():
    f = np.arange(P)
    tri = (f[:, None] <= f[None, :]).astype(np.float32)
    head_sum = (f[:, None] // FD == np.arange(P // FD)[None, :]).astype(np.float32)
    block = (f[:, None] // FD == f[None, :] // FD).astype(np.float32)
    odd = (f[:, None] // FD % 2).astype(np.float32)
    return np.concatenate([tri, head_sum, block, odd, np.ones((P, P), np.float32)], axis=1)


def head_spread():
    out = np.zeros((2 * FH, 2 * DC, P), np.float32)
    for a in range(2):
        for c in range(DC):
            for f in range(P):
                out[a * FH + c * (P // FD) + f // FD, a * DC + c, f] = 1
    return out


def counts(nt):
    n = (np.arange(nt)[None, :] * P + np.arange(P)[:, None] + 1).astype(np.float32)
    return np.stack([n, 1 / n], axis=1)


def flow_block(nc, x, nt, w, x_dram, x1_dram):
    with ExitStack() as ctx:
        def sb(name, shape, dt=F32):
            return ctx.enter_context(nc.sbuf_tensor("f_" + name, shape, dt))

        def sem(name):
            return ctx.enter_context(nc.semaphore("f_" + name))

        psum = ctx.enter_context(nc.psum_tensor("f_psum", [P, 8, 512], F32))
        G = P // FD
        NP = B * P

        raw = sb("raw", [P, DC, 3 * D])
        wqkv = sb("wqkv", [P, 2, DC, 3 * D], F32R)
        wo = sb("wo", [P, DC, D])
        bqk = sb("bqk", [P, 2, DC])
        bv = sb("bv", [P, D])
        bo = sb("bo", [P, D])
        ident = sb("ident", [P, P])
        consts = sb("consts", [P, 3 * P + G + 1])
        tri = consts[:, 0:P]
        head_sum = consts[:, P:P + G]
        block_of = consts[:, P + G:2 * P + G]
        odd = consts[:, 2 * P + G:2 * P + G + 1]
        ones = consts[:, 2 * P + G + 1:3 * P + G + 1]
        spread = sb("spread", [2 * FH, 2 * DC, P])
        count = sb("count", [P, 2, nt])
        mhalf = sb("mhalf", [P, 2])
        euler = sb("euler", [P, B * FH])

        stats = sb("stats", [P, 2, B, 6])
        mv = sb("mv", [P, 2, B, 2])
        ve = sb("ve", [P, 2, B])
        rstd = sb("rstd", [P, 2, B])
        hn = sb("hn", [P, B, D])
        hT = sb("hT", [P, 2, DC, NP], F32R)
        qk = sb("qk", [P, 2 * DC, B, P])
        qk_back = sb("qk_back", [P, 2 * DC, B, P])
        q_odd = sb("q_odd", [P, DC, B, P])
        cum = sb("cum", [P, 2 * DC, B, P])
        carry = sb("carry", [P, 2, 2 * DC, B])
        wtd = sb("wtd", [P, 2 * DC, B, P])
        prod = sb("prod", [P, 2 * DC, B, P])
        recip = sb("recip", [P, B, 2, FH])
        recip_n = sb("recip_n", [P, B, 2, FH])
        rT = sb("rT", [2 * FH, B, P])
        r_q = sb("r_q", [P, B, FH])
        cons = sb("cons", [P, 2, B, FH])
        alloc = sb("alloc", [P, B, FH])
        fac = sb("fac", [P, B, FH])
        cs = sb("cs", [P, B, FH])
        cs_sum = sb("cs_sum", [P, B, FH])
        rcs = sb("rcs", [P, B, FH])
        comp = sb("comp", [P, B, FH])
        vb = sb("vb", [P, B, D])
        vs = sb("vs", [P, B, D])
        k_tok = sb("k_tok", [P, B, D])
        st = sb("st", [P, B, 4, 512])
        s_new = sb("s_new", [P, B, D])
        state = sb("state", [P, B, D])
        o = sb("o", [P, B, D])
        oT = sb("oT", [P, DC, B, P])
        x1 = sb("x1", [P, B, D])

        names = """in_const w_high w_ready reset stats_in mv_in ve_in rstd_in hn_in hT_ps hT_high
            hT_low qk_ps v_ps qk_sig v_kept cum1 carry1 prod1 sums1 recip1 recip_n1 rT_ps rT_kept
            spread_ps weighted cum2 carry2 prod2 sums2 cons_done alloc_done fac_done cs_done
            cs_cum cs_added rcs_done comp_done vs_done rq_kept kt_ps kt_kept st_ps st_kept o_ps
            o_kept s_ps s_masked s_added qk_copied q_odd_done oT_ps oT_kept wo_ps bo_added x1_done
            stats_x1 mv_x1 ve_x1 rstd_x1 x_normed""".split()
        S = {n: sem(n) for n in names}
        in_x = [sem(f"in_x{b}") for b in range(B)]
        out_x1 = sem("out_x1")

        def run(step):
            def go(eng):
                step(0, True, False)
                with eng.Fori(1, nt) as t:
                    step(t, True, True)
                step(nt, False, True)
            return go

        block = ctx.enter_context(nc.Block())
        NCONST = 16 * 12

        def plain(eng):
            eng.wait_ge(S["in_const"], NCONST)

        @block.sync
        def _(sp):
            sp.dma_start(x[:, 0, 0, :], x_dram[0, 0:P]).then_inc(in_x[0], 16)
            sp.dma_start(x[:, 1, 0, :], x_dram[1, 0:P]).then_inc(in_x[1], 16)
            n = S["in_const"]
            for j, m in enumerate(("Wq", "Wk", "Wv")):
                sp.dma_start(raw[:, :, j * D:(j + 1) * D], w[m].rearrange("(c p) n -> p c n", p=P)).then_inc(n, 16)
            sp.dma_start(ident[:], w["ident"]).then_inc(n, 16)
            for j, m in enumerate(("bq", "bk")):
                sp.dma_start(bqk[:, j], w[m].rearrange("(c p) -> p c", p=P), allow_slow_non_contiguous=True).then_inc(n, 16)
            sp.dma_start(bv[:], w["bv"].rearrange("(a d) -> a d", a=1).partition_broadcast(P)).then_inc(n, 16)
            sp.dma_start(bo[:], w["bo"].rearrange("(a d) -> a d", a=1).partition_broadcast(P)).then_inc(n, 16)
            sp.dma_start(consts[:], w["flow_masks"]).then_inc(n, 16)
            sp.dma_start(spread[:], w["head_spread"]).then_inc(n, 16)
            sp.dma_start(count[:], w["counts"]).then_inc(n, 16)
            sp.dma_start(wo[:], w["Wo"].rearrange("(c p) n -> p c n", p=P)).then_inc(n, 16)

            with sp.Fori(1, nt) as t:
                for b in range(B):
                    plain(sp)
                    sp.wait_ge(in_x[b], 16 * t)
                    sp.dma_start(x[:, b, t, :], x_dram[b, bass.ds(t * P, P)]).then_inc(in_x[b], 16)
            with sp.Fori(0, nt) as t:
                plain(sp)
                sp.wait_ge(S["x1_done"], t + 1)
                sp.dma_start(x1_dram[:, bass.ds(t * P, P), :].rearrange("b p d -> p b d"), x1[:]).then_inc(out_x1, 16)
            sp.wait_ge(out_x1, 16 * nt)

        @block.tensor
        def _(pe):
            def hT_stage(t):
                pe.wait_ge(S["hn_in"], t + 1)
                for c in range(DC):
                    for b in range(B):
                        mm = nc.tensor.transpose(psum[:, 7, (c * B + b) * P:(c * B + b + 1) * P], hn[:, b, c * P:(c + 1) * P], ident[:])
                mm.then_inc(S["hT_ps"], 1)

            def qk_stage(t):
                pe.wait_ge(S["hT_low"], t + 1)
                for g in range(2 * DC):
                    n = 0
                    for c in range(DC):
                        for m, a in ((0, 0), (0, 1), (1, 0)):
                            mm = nc.tensor.matmul(psum[:, 4 + g // 2, (g % 2) * NP:(g % 2 + 1) * NP], wqkv[:, m, c, g * P:(g + 1) * P],
                                                  hT[:, a, c, :], start=(n == 0), stop=(n == 5))
                            n += 1
                mm.then_inc(S["qk_ps"], 1)

            def v_stage(t):
                for b in range(B):
                    n = 0
                    for c in range(DC):
                        for a, m in ((0, 0), (0, 1), (1, 0)):
                            mm = nc.tensor.matmul(psum[:, 6, b * D:(b + 1) * D], hT[:, a, c, b * P:(b + 1) * P], wqkv[:, m, c, 2 * D:3 * D],
                                                  start=(n == 0), stop=(n == 5))
                            n += 1
                mm.then_inc(S["v_ps"], 1)

            def head_sums(t, ready, made):
                pe.wait_ge(S[ready], t + 1)
                for b in range(B):
                    for g in range(2 * DC):
                        n = (b * 2 * DC + g) * G
                        mm = nc.tensor.matmul(psum[:, 4, n:n + G], prod[:, g, b, :], head_sum, start=True, stop=True)
                mm.then_inc(S[made], 1)

            def rT_stage(t):
                pe.wait_ge(S["recip_n1"], t + 1)
                for b in range(B):
                    mm = nc.tensor.transpose(psum[0:2 * FH, 5, b * P:(b + 1) * P], recip_n[:, b].rearrange("p a h -> p (a h)"), ident[:])
                mm.then_inc(S["rT_ps"], 1)

            def spread_stage(t):
                pe.wait_ge(S["rT_kept"], t + 1)
                for g in range(2 * DC):
                    mm = nc.tensor.matmul(psum[:, 4 + g // 2, (g % 2) * NP:(g % 2 + 1) * NP], spread[:, g, :],
                                          rT[:].rearrange("p b n -> p (b n)"), start=True, stop=True)
                mm.then_inc(S["spread_ps"], 1)

            def scores(t, b):
                for k in range(4):
                    for r in range(4):
                        c, par = k // 2, k % 2
                        rows = slice(32 * r, 32 * r + (32 if par else 16))
                        q = q_odd[rows, c, b, :] if par else qk_back[rows, c, b, :]
                        mm = nc.tensor.matmul(psum[:, r, k * P:(k + 1) * P], qk_back[rows, DC + c, b, :], q, start=True, stop=True)
                mm.then_inc(S["st_ps"], 1)

            def kt_stage(t):
                for b in range(B):
                    for c in range(DC):
                        mm = nc.tensor.transpose(psum[:, 7, (b * DC + c) * P:(b * DC + c + 1) * P], qk_back[:, DC + c, b, :], ident[:])
                mm.then_inc(S["kt_ps"], 1)

            def cs_stage(t):
                pe.wait_ge(S["cs_done"], t + 1)
                out = psum[:, 7, 0:B * FH]
                nc.tensor.matmul(out, tri, cs[:].rearrange("p b h -> p (b h)"), start=True, stop=False)
                pe.wait_ge(S["cs_added"], t + 2)
                nc.tensor.matmul(out, ones, cs_sum[:].rearrange("p b h -> p (b h)"), start=False, stop=True).then_inc(S["cs_cum"], 1)

            def values(t, b):
                pe.wait_ge(S["s_added"], t + 1)
                for c in range(DC):
                    nc.tensor.matmul(psum[:, 6, b * D + c * P:b * D + (c + 1) * P], qk_back[:, c, b, :], state[:, b, c * P:(c + 1) * P],
                                     start=(c == 0), stop=False, skip_group_check=True)
                pe.wait_ge(S["st_kept"], 2 * t + b + 1)
                pe.wait_ge(S["vs_done"], t + 1)
                for r in range(4):
                    for k in range(4):
                        h = (k // 2) * G + 2 * r + k % 2
                        cols = b * D + h * FD
                        mm = nc.tensor.matmul(psum[:, 6, cols:cols + FD], st[:, b, r, k * P:(k + 1) * P], vs[:, b, h * FD:(h + 1) * FD],
                                              start=False, stop=True, skip_group_check=True)
                mm.then_inc(S["o_ps"], 1)

            def state_stage(t):
                for b in range(B):
                    for c in range(DC):
                        cols = slice(c * P, (c + 1) * P)
                        mm = nc.tensor.matmul(psum[:, 7, b * D + c * P:b * D + (c + 1) * P], k_tok[:, b, cols], vs[:, b, cols], start=True, stop=True)
                mm.then_inc(S["s_ps"], 1)

            def oT_stage(t):
                pe.wait_ge(S["o_kept"], 2 * t + 2)
                for c in range(DC):
                    for b in range(B):
                        mm = nc.tensor.transpose(psum[:, 7, (c * B + b) * P:(c * B + b + 1) * P], o[:, b, c * P:(c + 1) * P], ident[:])
                mm.then_inc(S["oT_ps"], 1)

            def wo_stage(t):
                pe.wait_ge(S["oT_kept"], t + 1)
                for b in range(B):
                    for c in range(DC):
                        mm = nc.tensor.matmul(psum[:, 6, b * D:(b + 1) * D], oT[:, c, b, :], wo[:, c, :], start=(c == 0), stop=(c == DC - 1))
                mm.then_inc(S["wo_ps"], 1)

            pe.wait_ge(S["in_const"], NCONST)
            pe.wait_ge(S["w_ready"], 1)

            def step(t, front, back):
                u = t - 1
                if front:
                    if back:
                        pe.wait_ge(S["x1_done"], u)
                    hT_stage(t)
                if back:
                    pe.wait_ge(S["qk_copied"], u + 1)
                    pe.wait_ge(S["q_odd_done"], u + 1)
                    pe.wait_ge(S["st_kept"], 2 * u)
                    scores(u, 0)
                if front:
                    if back:
                        pe.wait_ge(S["cons_done"], t)
                    qk_stage(t)
                if back:
                    if front:
                        pe.wait_ge(S["hT_low"], t + 1)
                    kt_stage(u)
                if front:
                    if back:
                        pe.wait_ge(S["x1_done"], u)
                    v_stage(t)
                if back:
                    pe.wait_ge(S["kt_kept"], u + 1)
                    cs_stage(u)
                    pe.wait_ge(S["st_kept"], 2 * u + 1)
                    scores(u, 1)
                if front:
                    head_sums(t, "prod1", "sums1")
                if back:
                    if front:
                        pe.wait_ge(S["v_kept"], t + 1)
                    else:
                        pe.wait_ge(S["x1_done"], u)
                    values(u, 0)
                if front:
                    rT_stage(t)
                if back:
                    pe.wait_ge(S["o_kept"], 2 * u + 1)
                    values(u, 1)
                if front:
                    spread_stage(t)
                if back:
                    pe.wait_ge(S["rcs_done"], u + 1)
                    state_stage(u)
                    pe.wait_ge(S["s_masked"], u + 1)
                    oT_stage(u)
                if front:
                    head_sums(t, "prod2", "sums2")
                if back:
                    wo_stage(u)

            run(step)(pe)

        @block.scalar
        def _(act):
            act.wait_ge(S["in_const"], NCONST)
            nc.scalar.copy(wqkv[:, 0].rearrange("p c n -> p (c n)"), raw[:].rearrange("p c n -> p (c n)")).then_inc(S["w_high"], 1)

            def step(t, front, back):
                u = t - 1
                if front:
                    act.wait_ge(S["hT_ps"], t + 1)
                    if back:
                        act.wait_ge(S["v_ps"], t)
                    nc.scalar.copy(hT[:, 0].rearrange("p c n -> p (c n)"), psum[:, 7, :]).then_inc(S["hT_high"], 1)
                    act.wait_ge(S["qk_ps"], t + 1)
                    if back:
                        act.wait_ge(S["prod2"], t)
                        act.wait_ge(S["qk_copied"], t)
                    for g in range(2 * DC):
                        a = nc.scalar.activation(qk[:, g].rearrange("p b n -> p (b n)"), psum[:, 4 + g // 2, (g % 2) * NP:(g % 2 + 1) * NP],
                                                 ACT.Sigmoid, bias=bqk[:, g // DC, g % DC:g % DC + 1], scale=1.0)
                    a.then_inc(S["qk_sig"], 1)
                if back:
                    act.wait_ge(S["kt_ps"], u + 1)
                    nc.scalar.copy(k_tok[:].rearrange("p b n -> p (b n)"), psum[:, 7, :]).then_inc(S["kt_kept"], 1)
                    act.wait_ge(S["cons_done"], u + 1)
                    nc.scalar.activation(alloc[:], cons[:, 0], ACT.Sigmoid).then_inc(S["alloc_done"], 1)
                if front:
                    act.wait_ge(S["rT_ps"], t + 1)
                    nc.scalar.copy(rT[:].rearrange("p b n -> p (b n)"), psum[0:2 * FH, 5, 0:NP]).then_inc(S["rT_kept"], 1)
                if back:
                    act.wait_ge(S["oT_ps"], u + 1)
                    nc.scalar.copy(oT[:].rearrange("p c b n -> p (c b n)"), psum[:, 7, :]).then_inc(S["oT_kept"], 1)
                if front:
                    act.wait_ge(S["qk_sig"], t + 1)
                    if back:
                        act.wait_ge(S["o_ps"], 2 * u + 2)
                        act.wait_ge(S["q_odd_done"], t)
                    nc.scalar.copy(qk_back[:].rearrange("p g b n -> p (g b n)"), qk[:].rearrange("p g b n -> p (g b n)")).then_inc(S["qk_copied"], 1)

            run(step)(act)

        @block.vector
        def _(dve):
            def chain(ins, name, n):
                ins.then_inc(S[name], 1)
                dve.wait_ge(S[name], n)

            def norm_stats(src, b, i, tag, n):
                nc.vector.bn_stats(stats[:, i, b], src).then_inc(S["stats_" + tag], 1)

            def norm_in(t):
                for b in range(B):
                    plain(dve)
                    dve.wait_ge(in_x[b], 16 * (t + 1))
                    a = nc.vector.bn_stats(stats[:, 0, b], x[:, b, t, :])
                a.then_inc(S["stats_in"], 1)
                norm_rest("in", 0, t)
                for b in range(B):
                    a = nc.vector.tensor_scalar(hn[:, b], x[:, b, t, :], mv[:, 0, b, 0:1], rstd[:, 0, b:b + 1], ALU.subtract, ALU.mult)
                a.then_inc(S["hn_in"], 1)

            def norm_rest(tag, i, t):
                plain(dve)
                dve.wait_ge(S["stats_" + tag], t + 1)
                for b in range(B):
                    a = nc.vector.bn_aggr(mv[:, i, b], stats[:, i, b])
                a.then_inc(S["mv_" + tag], 1)
                dve.wait_ge(S["mv_" + tag], t + 1)
                nc.vector.tensor_scalar(ve[:, i], mv[:, i, :, 1], LN_EPS, None, ALU.add).then_inc(S["ve_" + tag], 1)
                dve.wait_ge(S["rstd_" + tag], t + 1)

            def scans(t, i, src, name):
                dve.wait_ge(S["reset"], 4)
                for g in range(2 * DC):
                    for b in range(B):
                        a = nc.vector.tensor_tensor_scan(cum[:, g, b, :], ones, src[:, g, b, :], carry[:, i, g, b:b + 1], ALU.mult, ALU.add)
                a.then_inc(S[name], 1)
                dve.wait_ge(S[name], t + 1)
                nc.vector.tensor_copy(carry[:, i], cum[:, :, :, P - 1]).then_inc(S["carry1" if i == 0 else "carry2"], 1)

            def products(t, name):
                for a in range(2):
                    f = lambda v, n: v[:, n * DC:(n + 1) * DC].rearrange("p c b n -> p (c b n)")
                    ins = nc.vector.scalar_tensor_tensor(f(prod, a), f(qk, a), FLOW_EPS, f(cum, 1 - a), ALU.add, ALU.mult)
                ins.then_inc(S[name], 1)

            dve.wait_ge(S["w_high"], 1)
            nc.vector.tensor_tensor(wqkv[:, 1].rearrange("p c n -> p (c n)"), raw[:].rearrange("p c n -> p (c n)"),
                                    wqkv[:, 0].rearrange("p c n -> p (c n)").bitcast(F32), ALU.subtract).then_inc(S["w_ready"], 1)
            nc.vector.memset(carry[:], FLOW_EPS).then_inc(S["reset"], 1)
            norm_in(0)

            def mask_scores(u, b):
                dve.wait_ge(S["st_ps"], 2 * u + b + 1)
                nc.vector.tensor_tensor(st[:, b].rearrange("p r (k i) -> p (r k) i", k=4), psum[:, 0:4, :].rearrange("p r (k i) -> p (r k) i", k=4),
                                        tri.rearrange("p (o i) -> p o i", o=1).broadcast_to((P, 16, P)), ALU.mult).then_inc(S["st_kept"], 1)

            def keep_o(u, b):
                if b == 0:
                    dve.wait_ge(S["fac_done"], u + 1)
                    if not (isinstance(u, int) and u == 0):
                        dve.wait_ge(S["oT_ps"], u)
                dve.wait_ge(S["o_ps"], 2 * u + b + 1)
                nc.vector.tensor_tensor(o[:, b].rearrange("p (h d) -> p h d", d=FD), psum[:, 6, b * D:(b + 1) * D].rearrange("p (h d) -> p h d", d=FD),
                                        fac[:, b].rearrange("p (h o) -> p h o", o=1).broadcast_to((P, FH, FD)), ALU.mult).then_inc(S["o_kept"], 1)

            def step(t, front, back):
                u = t - 1
                if front:
                    dve.wait_ge(S["hT_high"], t + 1)
                    nc.vector.tensor_tensor(hT[:, 1].rearrange("p c n -> p (c n)"), psum[:, 7, :],
                                            hT[:, 0].rearrange("p c n -> p (c n)").bitcast(F32), ALU.subtract).then_inc(S["hT_low"], 1)
                if back:
                    mask_scores(u, 0)
                    dve.wait_ge(S["cs_cum"], u + 1)
                    nc.vector.reciprocal(rcs[:].rearrange("p b h -> p (b h)"), psum[:, 7, 0:B * FH]).then_inc(S["rcs_done"], 1)
                    dve.wait_ge(S["rcs_done"], u + 1)
                    nc.vector.scalar_tensor_tensor(comp[:], cs[:], count[:, 0, bass.ds(u, 1)], rcs[:], ALU.mult, ALU.mult).then_inc(S["comp_done"], 1)
                    dve.wait_ge(S["alloc_done"], u + 1)
                    nc.vector.tensor_tensor(fac[:], alloc[:], r_q[:], ALU.mult).then_inc(S["fac_done"], 1)
                if front:
                    dve.wait_ge(S["v_ps"], t + 1)
                    if back:
                        dve.wait_ge(S["vs_done"], t)
                    nc.vector.tensor_tensor(vb[:], psum[:, 6, :].rearrange("p (b d) -> p b d", b=B),
                                            bv[:].rearrange("p (o d) -> p o d", o=1).broadcast_to((P, B, D)), ALU.add).then_inc(S["v_kept"], 1)
                    dve.wait_ge(S["qk_sig"], t + 1)
                    if back:
                        dve.wait_ge(S["carry1"], t)
                    scans(t, 0, qk, "cum1")
                    if back:
                        dve.wait_ge(S["sums2"], t)
                    products(t, "prod1")
                if back:
                    mask_scores(u, 1)
                if front:
                    dve.wait_ge(S["sums1"], t + 1)
                    if back:
                        dve.wait_ge(S["fac_done"], t)
                    nc.vector.reciprocal(recip[:].rearrange("p b a h -> p (b a h)"), psum[:, 4, 0:2 * B * FH]).then_inc(S["recip1"], 1)
                    dve.wait_ge(S["recip1"], t + 1)
                    nc.vector.tensor_scalar(recip_n[:].rearrange("p b a h -> p (b a h)"), recip[:].rearrange("p b a h -> p (b a h)"),
                                            count[:, 0, bass.ds(t, 1)], None, ALU.mult).then_inc(S["recip_n1"], 1)
                    nc.vector.tensor_copy(r_q[:], recip[:, :, 0, :]).then_inc(S["rq_kept"], 1)
                if back:
                    keep_o(u, 0)
                if front:
                    dve.wait_ge(S["spread_ps"], t + 1)
                    nc.vector.tensor_tensor(wtd[:].rearrange("p g b n -> p (g b n)"), psum[:, 4:6, :].rearrange("p a n -> p (a n)"),
                                            qk[:].rearrange("p g b n -> p (g b n)"), ALU.mult).then_inc(S["weighted"], 1)
                    dve.wait_ge(S["weighted"], t + 1)
                    dve.wait_ge(S["prod1"], t + 1)
                    dve.wait_ge(S["carry1"], t + 1)
                    if back:
                        dve.wait_ge(S["carry2"], t)
                    scans(t, 1, wtd, "cum2")
                    dve.wait_ge(S["sums1"], t + 1)
                    products(t, "prod2")
                if back:
                    keep_o(u, 1)
                    dve.wait_ge(S["s_ps"], u + 1)
                    nc.vector.tensor_tensor(s_new[:].rearrange("p b (c f) -> p (b c) f", f=P), psum[:, 7, :].rearrange("p (a f) -> p a f", f=P),
                                            block_of.rearrange("p (o f) -> p o f", o=1).broadcast_to((P, B * DC, P)), ALU.mult).then_inc(S["s_masked"], 1)
                if front:
                    dve.wait_ge(S["sums2"], t + 1)
                    if back:
                        dve.wait_ge(S["alloc_done"], t)
                        dve.wait_ge(S["cs_done"], t)
                    nc.vector.tensor_scalar(cons[:].rearrange("p a b h -> p b a h"), psum[:, 4, 0:2 * B * FH].rearrange("p (b a h) -> p b a h", b=B, a=2),
                                            count[:, 1, bass.ds(t, 1)], None, ALU.mult).then_inc(S["cons_done"], 1)
                if front:
                    dve.wait_ge(S["qk_copied"], t + 1)
                    nc.vector.tensor_scalar(q_odd[:].rearrange("p c b n -> p (c b n)"), qk_back[:, 0:DC].rearrange("p c b n -> p (c b n)"),
                                            odd, None, ALU.mult).then_inc(S["q_odd_done"], 1)
                if back:
                    dve.wait_ge(S["wo_ps"], u + 1)
                    dve.wait_ge(S["bo_added"], u + 1)
                    if not (isinstance(t, int) and t <= 1):
                        dve.wait_ge(out_x1, 16 * u)
                    nc.vector.tensor_tensor(x1[:], psum[:, 6, :].rearrange("p (b d) -> p b d", b=B), x[:, :, u, :], ALU.add).then_inc(S["x1_done"], 1)
                    dve.wait_ge(S["x1_done"], u + 1)
                    for b in range(B):
                        a = nc.vector.bn_stats(stats[:, 1, b], x1[:, b])
                    a.then_inc(S["stats_x1"], 1)
                    norm_rest("x1", 1, u)
                    for b in range(B):
                        a = nc.vector.tensor_scalar(x[:, b, u, :], x1[:, b], mv[:, 1, b, 0:1], rstd[:, 1, b:b + 1], ALU.subtract, ALU.mult)
                    a.then_inc(S["x_normed"], 1)
                if front:
                    pass

            def vstep(t, front, back):
                step(t, front, back)
                if front and not (isinstance(t, int) and t == nt - 1):
                    pass

            step(0, True, False)
            norm_in(1)
            with dve.Fori(1, nt - 1) as t:
                step(t, True, True)
                norm_in(t + 1)
            step(nt - 1, True, True)
            step(nt, False, True)

        @block.gpsimd
        def _(pool):
            nc.gpsimd.memset(mhalf[:], -0.5).then_inc(S["reset"], 1)
            nc.gpsimd.memset(euler[:], float(np.e)).then_inc(S["reset"], 1)
            nc.gpsimd.memset(cs[:], 0.0).then_inc(S["reset"], 1)
            nc.gpsimd.memset(cs_sum[:], 0.0).then_inc(S["cs_added"], 1)
            nc.gpsimd.memset(state[:], 0.0).then_inc(S["s_added"], 1)
            pool.wait_ge(S["reset"], 4)
            pool.wait_ge(S["cs_added"], 1)
            pool.wait_ge(S["s_added"], 1)
            pool.wait_ge(S["in_const"], NCONST)

            def rstd_(tag, i, t):
                pool.wait_ge(S["ve_" + tag], t + 1)
                nc.gpsimd.tensor_tensor(rstd[:, i], ve[:, i], mhalf[:], ALU.pow).then_inc(S["rstd_" + tag], 1)

            def step(t, front, back, more):
                u = t - 1
                if back:
                    pool.wait_ge(S["cons_done"], u + 1)
                    pool.wait_ge(S["cs_cum"], u)
                    pool.wait_ge(S["comp_done"], u)
                    nc.gpsimd.tensor_tensor(cs_sum[:], cs_sum[:], cs[:], ALU.add).then_inc(S["cs_added"], 1)
                    pool.wait_ge(S["cs_added"], u + 2)
                    nc.gpsimd.tensor_tensor(cs[:].rearrange("p b h -> p (b h)"), euler[:], cons[:, 1].rearrange("p b h -> p (b h)"), ALU.pow).then_inc(S["cs_done"], 1)
                    pool.wait_ge(S["comp_done"], u + 1)
                    pool.wait_ge(S["s_ps"], u)
                    nc.gpsimd.tensor_tensor(vs[:].rearrange("p b (h d) -> p (b h) d", d=FD), vb[:].rearrange("p b (h d) -> p (b h) d", d=FD),
                                            comp[:].rearrange("p b (h o) -> p (b h) o", o=1).broadcast_to((P, B * FH, FD)), ALU.mult).then_inc(S["vs_done"], 1)
                    nc.gpsimd.tensor_tensor(x[:, :, u, :], x[:, :, u, :], bo[:].rearrange("p (o d) -> p o d", o=1).broadcast_to((P, B, D)),
                                            ALU.add).then_inc(S["bo_added"], 1)
                    pool.wait_ge(S["s_masked"], u + 1)
                    pool.wait_ge(S["o_ps"], 2 * u + 2)
                    nc.gpsimd.tensor_tensor(state[:], state[:], s_new[:], ALU.add).then_inc(S["s_added"], 1)
                    rstd_("x1", 1, u)
                if more:
                    rstd_("in", 0, t + 1)

            rstd_("in", 0, 0)
            step(0, True, False, True)
            with pool.Fori(1, nt - 1) as t:
                step(t, True, True, True)
            step(nt - 1, True, True, False)
            step(nt, False, True, False)


def layers_block(nc, x, nt, depth, w):
    with ExitStack() as ctx:
        def sb(name, shape, dt=F32):
            return ctx.enter_context(nc.sbuf_tensor(name, shape, dt))

        def sem(name):
            return ctx.enter_context(nc.semaphore(name))

        psum = ctx.enter_context(nc.psum_tensor("psum", [P, 8, 512], F32))
        sc_ps = psum[:, 0:4, :]

        wqkv = sb("wqkv", [P, 2, DC, 3 * INNER], F32R)
        w1 = sb("w1", [P, 2, DC, 2 * HID], F32R)
        raw = sb("raw", [P, DC, 3 * INNER])
        wo = sb("wo", [P, INNER // P, D])
        w2 = sb("w2", [P, NF, D])
        b1 = sb("b1", [P, 2, NF])
        b2 = sb("b2", [P, D])
        lng = sb("lng", [P, DC])
        lnb = sb("lnb", [P, DC])
        qks = sb("qks", [P, 4, DH])
        tab = sb("tab", [P, nt, 4, DH])
        mask = sb("mask", [P, 3, 512], BF16)
        ident = sb("ident", [P, P])
        ident_bf = sb("ident_bf", [P, P], BF16)

        xst = sb("xst", [P, B, D])
        hT = sb("hT", [P, B, 2, DC, P + 2], F32R)
        t1 = sb("t1", [P, B, 2 * INNER])
        t2 = sb("t2", [P, B, 2 * INNER])
        sq = sb("sq", [P, 2 * INNER])
        ss = sb("ss", [P, B, 2 * HEADS])
        rn = sb("rn", [P, B, 2 * HEADS])
        zeros = sb("zeros", [P, D])
        mhalf = sb("mhalf", [P, 2 * HEADS])
        qT = sb("qT", [P, HEADS // 2, P])
        kT = sb("kT", [P, B, HEADS // 2, 2, P])
        v = sb("v", [P, B, 2, INNER])
        nmax = sb("nmax", [P, HEADS])
        psm = sb("psm", [P, HEADS])
        rsm = sb("rsm", [P, HEADS])
        probs = sb("probs", [P, HEADS, 2, P])
        probsT = sb("probsT", [P, 4, 512])
        o = sb("o", [P, INNER])
        oT = sb("oT", [P, INNER // P, P])
        hs = sb("hs", [P, B, P])
        lastrow = sb("lastrow", [1, B, P])
        stats = sb("stats", [P, B, 12])
        mv = sb("mv", [P, B, 2])
        ve = sb("ve", [P, B])
        rstd = sb("rstd", [P, B])
        hn = sb("hn", [P, B, D])
        h2T = sb("h2T", [P, 2, DC, B * P], F32R)
        gate = sb("gate", [P, 2, B * P])
        hid = sb("hid", [P, NF, B * P])

        in_const = sem("in_const")
        in_wqkv = sem("in_wqkv")
        in_w1 = sem("in_w1")
        in_small = sem("in_small")
        in_tab = sem("in_tab")
        const_ready = sem("const_ready")
        half_ready = sem("half_ready")
        wqkv_ready = sem("wqkv_ready")
        wqkv_high = sem("wqkv_high")
        w1_ready = sem("w1_ready")
        w1_high = sem("w1_high")
        w1_bias_mm = sem("w1_bias_mm")
        b1_ready = sem("b1_ready")
        tab_ready = sem("tab_ready")
        state_reset = sem("state_reset")
        layer_done = sem("layer_done")
        x_staged = sem("x_staged")
        xT_ps = sem("xT_ps")
        col_carried = sem("col_carried")
        hT_high = sem("hT_high")
        hT_low = sem("hT_low")
        qk_ps = sem("qk_ps")
        v_ps = sem("v_ps")
        v_kept = sem("v_kept")
        squares = sem("squares")
        rot_parts = sem("rot_parts")
        sumsq = sem("sumsq")
        sumsq_raw = sem("sumsq_raw")
        rnorm = sem("rnorm")
        rot_sum = sem("rot_sum")
        qk_final = sem("qk_final")
        qkT_ps = sem("qkT_ps")
        qT_kept = sem("qT_kept")
        kT_kept = sem("kT_kept")
        scores_ps = sem("scores_ps")
        max_found = sem("max_found")
        exp_done = sem("exp_done")
        pT_ps = sem("pT_ps")
        pT_act = sem("pT_act")
        pT_dve = sem("pT_dve")
        o_ps = sem("o_ps")
        rsum = sem("rsum")
        o_kept = sem("o_kept")
        oT_ps = sem("oT_ps")
        oT_kept = sem("oT_kept")
        wo_ps = sem("wo_ps")
        x_attn = sem("x_attn")
        row_copied = sem("row_copied")
        in_row = [sem(f"in_row{b}") for b in range(B)]
        in_hs = [sem(f"in_hs{b}") for b in range(B)]
        stats_done = sem("stats_done")
        mv_done = sem("mv_done")
        ve_done = sem("ve_done")
        rstd_done = sem("rstd_done")
        hn_done = sem("hn_done")
        b2_added = sem("b2_added")
        h2T_ps = sem("h2T_ps")
        h2T_high = sem("h2T_high")
        h2T_low = sem("h2T_low")
        up_ps = sem("up_ps")
        gelu_done = sem("gelu_done")
        hid_done = sem("hid_done")
        down_ps = sem("down_ps")
        x_ffn = sem("x_ffn")
        out_sent = sem("out_sent")

        def plain(eng):
            eng.wait_ge(in_const, 32)

        def place(h):
            return (h % 2) * (HEADS // 2) + h // 2

        def done(l, t, b):
            return l * (B * nt) + t * B + b + 1

        def fdone(l, t):
            return l * nt + t + 1

        def rdone(l, t, r):
            return (l * nt + t) * NF + r + 1

        def run(eng, start, step, ffn_tail, end=None):
            with eng.Fori(0, depth) as l:
                start(l)
                step(l, 0, True, False)
                with eng.Fori(1, nt - 1) as t:
                    step(l, t, False, False)
                step(l, nt - 1, False, True)
                ffn_tail(l, nt - 1)
                if end is not None:
                    end(l)

        block = ctx.enter_context(nc.Block())

        @block.sync
        def _(sp):
            sp.dma_start(ident[:], w["ident"]).then_inc(in_const, 16)
            sp.dma_start(probs[:].rearrange("p h s j -> p (h s j)")[:, 0:1536], w["masks"]).then_inc(in_const, 16)

            def start(l):
                plain(sp)
                sp.wait_ge(layer_done, l)
                sp.dma_start(raw[:], w["wqkv"][bass.ds(l, 1)].rearrange("a (c p) n -> p (a c) n", p=P)).then_inc(in_wqkv, 16)
                sp.dma_start(tab[:], w["tables"].rearrange("(t p) k d -> p t k d", p=P)).then_inc(in_tab, 16)
                for n, s in ((0, "q_scale"), (1, "k_scale")):
                    row = w[s][bass.ds(l, 1)]
                    sp.dma_start(qks[:, n], row.partition_broadcast(P)).then_inc(in_small, 16)
                    sp.dma_start(qks[:, 2 + n, 0:HALF], row[:, HALF:DH].partition_broadcast(P)).then_inc(in_small, 16)
                    sp.dma_start(qks[:, 2 + n, HALF:DH], row[:, 0:HALF].partition_broadcast(P)).then_inc(in_small, 16)
                sp.dma_start(b2[:], w["b2"][bass.ds(l, 1)].partition_broadcast(P)).then_inc(in_small, 16)
                sp.dma_start(lng[:], w["ln_g"][bass.ds(l, 1)].rearrange("a (c p) -> p (a c)", p=P), allow_slow_non_contiguous=True).then_inc(in_small, 16)
                sp.dma_start(lnb[:], w["ln_b"][bass.ds(l, 1)].rearrange("a (c p) -> p (a c)", p=P), allow_slow_non_contiguous=True).then_inc(in_small, 16)
                for g in range(2):
                    row = w["b1"][bass.ds(l, 1), g * HID:(g + 1) * HID]
                    sp.dma_start(b1[0:FS, g, 0:NF - 1], row[:, 0:(NF - 1) * FS].rearrange("a (f p) -> p (a f)", p=FS), allow_slow_non_contiguous=True).then_inc(in_small, 16)
                    sp.dma_start(b1[0:FLAST, g, NF - 1:NF], row[:, (NF - 1) * FS:HID].rearrange("a (f p) -> p (a f)", p=FLAST), allow_slow_non_contiguous=True).then_inc(in_small, 16)
                sp.dma_start(wo[:], w["wo"][bass.ds(l, 1)].rearrange("a (c p) n -> p (a c) n", p=P)).then_inc(in_small, 16)
                sp.dma_start(w2[0:FS, 0:NF - 1, :], w["w2"][bass.ds(l, 1), 0:(NF - 1) * FS].rearrange("a (f p) n -> p (a f) n", p=FS)).then_inc(in_small, 16)
                sp.dma_start(w2[0:FLAST, NF - 1, :], w["w2"][bass.ds(l, 1), (NF - 1) * FS:HID].rearrange("a p n -> (a p) n")).then_inc(in_small, 16)
                sp.wait_ge(wqkv_ready, l + 1)
                sp.dma_start(raw[:, :, 0:2 * HID], w["w1"][bass.ds(l, 1)].rearrange("a (c p) n -> p (a c) n", p=P)).then_inc(in_w1, 16)

            def shift(l, t, b):
                n = done(l, t, b)
                n = n if isinstance(n, int) else sp.snap(n)
                plain(sp)
                sp.wait_ge(x_attn, n)
                sp.wait_ge(row_copied, n)
                sp.dma_start(lastrow[0:1, b], x[P - 1:P, b, t, P:D]).then_inc(in_row[b], 16)
                sp.dma_start(hs[1:P, b], x[0:P - 1, b, t, P:D]).then_inc(in_hs[b], 16)

            def step(l, t, first, last):
                shift(l, t, 0)
                shift(l, t, 1)

            run(sp, start, step, lambda l, t: None)

        @block.tensor
        def _(pe):
            def transposed_x(l, t, b, bank):
                pe.wait_ge(x_staged, done(l, t, b))
                for c in range(DC):
                    mm = nc.tensor.transpose(psum[:, bank, c * P:(c + 1) * P], xst[:, b, c * P:(c + 1) * P], ident[:])
                mm.then_inc(xT_ps, 1)

            def project(b, j, bank):
                n = 0
                for c in range(DC):
                    for a, m in ((0, 0), (0, 1), (1, 0)):
                        mm = nc.tensor.matmul(psum[:, bank, :], hT[:, b, a, c, 1 - c:1 - c + P],
                                              wqkv[:, m, c, j * INNER:(j + 1) * INNER], start=(n == 0), stop=(n == 5))
                        n += 1
                return mm

            def qk(l, t, b, bank):
                pe.wait_ge(hT_low, done(l, t, b))
                project(b, 0, bank)
                project(b, 1, bank + 1).then_inc(qk_ps, 1)

            def vproj(l, t, b, bank):
                project(b, 2, bank).then_inc(v_ps, 1)

            def qkT(l, t, b):
                pe.wait_ge(qk_final, done(l, t, b))
                for n in range(HEADS):
                    mm = nc.tensor.transpose(psum[:, 5 + n // 4, (n % 4) * P:(n % 4 + 1) * P], t1[:, b, n * P:(n + 1) * P], ident[:])
                mm.then_inc(qkT_ps, 1)

            def scores(l, t, b, kind):
                pe.wait_ge(qT_kept, done(l, t, b))
                pe.wait_ge(kT_kept, done(l, t, b))
                for k in range(4):
                    nc.tensor.matmul(psum[:, k, :], ident_bf[:], mask[:, kind, :], start=True, stop=True)
                for h in range(HEADS):
                    r = (h % 2) * DH
                    n = place(h)
                    mm = nc.tensor.matmul(psum[:, n // 2, (n % 2) * 256:(n % 2 + 1) * 256], qT[r:r + DH, h // 2, :],
                                          kT[r:r + DH, b, h // 2], start=False, stop=True, skip_group_check=True)
                mm.then_inc(scores_ps, 1)

            def probsT_(l, t, b):
                pe.wait_ge(exp_done, done(l, t, b))
                for n in range(2 * HEADS):
                    mm = nc.tensor.transpose(psum[:, n // 4, (n % 4) * P:(n % 4 + 1) * P], probs[:, n // 2, n % 2, :], ident[:])
                    if n == 7:
                        mm.then_inc(pT_ps, 1)
                mm.then_inc(pT_ps, 1)

            def values(l, t, b, bank):
                pe.wait_ge(pT_act, done(l, t, b))
                pe.wait_ge(pT_dve, done(l, t, b))
                pe.wait_ge(v_kept, done(l, t, b))
                for h in range(HEADS):
                    for s in range(2):
                        n = 2 * place(h) + s
                        mm = nc.tensor.matmul(psum[:, bank, h * DH:(h + 1) * DH], probsT[:, n // 4, (n % 4) * P:(n % 4 + 1) * P],
                                              v[:, b, s, h * DH:(h + 1) * DH], start=(s == 0), stop=(s == 1))
                mm.then_inc(o_ps, 1)

            def transposed_o(l, t, b, bank):
                pe.wait_ge(o_kept, done(l, t, b))
                for c in range(INNER // P):
                    mm = nc.tensor.transpose(psum[:, bank, c * P:(c + 1) * P], o[:, c * P:(c + 1) * P], ident[:])
                mm.then_inc(oT_ps, 1)

            def out_proj(l, t, b, bank):
                pe.wait_ge(oT_kept, done(l, t, b))
                for c in range(INNER // P):
                    mm = nc.tensor.matmul(psum[:, bank, 0:D], oT[:, c, :], wo[:, c, :], start=(c == 0), stop=(c == INNER // P - 1))
                mm.then_inc(wo_ps, 1)

            def transposed_h(l, t):
                pe.wait_ge(hn_done, done(l, t, 1))
                for c in range(DC):
                    for b in range(B):
                        mm = nc.tensor.transpose(psum[:, 7, (c * B + b) * P:(c * B + b + 1) * P], hn[:, b, c * P:(c + 1) * P], ident[:])
                mm.then_inc(h2T_ps, 1)

            def up(l, t, r):
                n = FC[r]
                for g in range(2):
                    k = 0
                    for c in range(DC):
                        for m, a in ((0, 0), (0, 1), (1, 0)):
                            f0 = g * HID + r * FS
                            mm = nc.tensor.matmul(psum[0:n, 4 + r % 3, g * 256:(g + 1) * 256], w1[:, m, c, f0:f0 + n],
                                                  h2T[:, a, c, :], start=(k == 0), stop=(k == 5))
                            k += 1
                mm.then_inc(up_ps, 1)

            def down(l, t, b):
                pe.wait_ge(hid_done, rdone(l, t, NF - 1))
                for f in range(NF):
                    n = FC[f]
                    mm = nc.tensor.matmul(psum[:, 5 + b, 0:D], hid[0:n, f, b * P:(b + 1) * P], w2[0:n, f, :],
                                          start=(f == 0), stop=(f == NF - 1))
                mm.then_inc(down_ps, 1)

            def start(l):
                pe.wait_ge(wqkv_ready, l + 1)
                pe.wait_ge(const_ready, 2)
                transposed_x(l, 0, 0, 4)
                qk(l, 0, 0, 5)
                vproj(l, 0, 0, 7)
                transposed_x(l, 0, 1, 3)
                qk(l, 0, 1, 0)
                vproj(l, 0, 1, 2)
                qkT(l, 0, 0)

            def ffn_first(l, t):
                transposed_h(l, t)
                pe.wait_ge(h2T_low, fdone(l, t))
                for r in range(3):
                    up(l, t, r)

            def ffn_rest(l, t):
                for r in range(3, NF):
                    pe.wait_ge(hid_done, rdone(l, t, r - 3))
                    up(l, t, r)

            def step(l, t, first, last):
                pe.wait_ge(rot_parts, done(l, t, 1))
                pe.wait_ge(squares, done(l, t, 1))
                pe.wait_ge(v_kept, done(l, t, 1))
                scores(l, t, 0, 2 if first else t % 2)
                qkT(l, t, 1)
                pe.wait_ge(qT_kept, done(l, t, 1))
                pe.wait_ge(kT_kept, done(l, t, 1))
                if first:
                    pe.wait_ge(in_w1, 16 * (l + 1))
                    for g in range(2):
                        for f in range(NF):
                            for c in range(DC):
                                f0 = g * HID + f * FS
                                mm = nc.tensor.matmul(psum[0:FC[f], 4, g * NF + f:g * NF + f + 1], raw[:, c, f0:f0 + FC[f]],
                                                      lnb[:, c:c + 1], start=(c == 0), stop=(c == DC - 1))
                    mm.then_inc(w1_bias_mm, 1)
                else:
                    ffn_first(l, t - 1)
                probsT_(l, t, 0)
                if not first:
                    ffn_rest(l, t - 1)
                values(l, t, 0, 7)
                scores(l, t, 1, 2 if first else t % 2)
                if first:
                    pe.wait_ge(b1_ready, l + 1)
                else:
                    pe.wait_ge(hid_done, rdone(l, t - 1, 3))
                transposed_o(l, t, 0, 4)
                if not first:
                    down(l, t - 1, 0)
                    down(l, t - 1, 1)
                probsT_(l, t, 1)
                out_proj(l, t, 0, 7)
                pe.wait_ge(pT_act, done(l, t, 1))
                pe.wait_ge(pT_dve, done(l, t, 1))
                if not first:
                    pe.wait_ge(x_ffn, done(l, t - 1, 1))
                if not last:
                    transposed_x(l, t + 1, 0, 4)
                    qk(l, t + 1, 0, 5)
                    pe.wait_ge(x_attn, done(l, t, 0))
                    vproj(l, t + 1, 0, 7)
                values(l, t, 1, 4)
                if not last:
                    transposed_x(l, t + 1, 1, 3)
                    qk(l, t + 1, 1, 0)
                transposed_o(l, t, 1, 4)
                if not last:
                    vproj(l, t + 1, 1, 2)
                    pe.wait_ge(v_kept, done(l, t + 1, 0))
                else:
                    pe.wait_ge(x_attn, done(l, t, 0))
                out_proj(l, t, 1, 7)
                if not last:
                    qkT(l, t + 1, 0)

            def ffn_tail(l, t):
                ffn_first(l, t)
                ffn_rest(l, t)
                down(l, t, 0)
                down(l, t, 1)

            run(pe, start, step, ffn_tail)

        @block.scalar
        def _(act):
            act.wait_ge(in_const, 32)
            nc.scalar.copy(ident_bf[:], ident[:]).then_inc(const_ready, 1)
            nc.scalar.copy(mask[:].rearrange("p k n -> p (k n)"), probs[:].rearrange("p h s j -> p (h s j)")[:, 0:1536]).then_inc(const_ready, 1)

            def high(l, t, b, bank):
                act.wait_ge(xT_ps, done(l, t, b))
                act.wait_ge(col_carried, done(l, t, b))
                nc.scalar.copy(hT[:, b, 0, :, 1:P + 1], psum[:, bank, 0:D].rearrange("p (c n) -> p c n", c=DC)).then_inc(hT_high, 1)

            def square(l, t, b, bank):
                act.wait_ge(qk_ps, done(l, t, b))
                if not (isinstance(t, int) and t == 0 and b == 0):
                    act.wait_ge(sumsq_raw, done(l, t, b) - 1)
                nc.scalar.activation(sq[:], psum[:, bank:bank + 2, :].rearrange("p a n -> p (a n)"), ACT.Square).then_inc(squares, 1)

            def keep_v(l, t, b, bank):
                act.wait_ge(v_ps, done(l, t, b))
                if not (isinstance(t, int) and t == 0):
                    act.wait_ge(o_ps, done(l, t - 1, b))
                nc.scalar.copy(v[:, b, t % 2, :], psum[:, bank, :]).then_inc(v_kept, 1)

            def keep_qT(l, t, b):
                act.wait_ge(qkT_ps, done(l, t, b))
                nc.scalar.copy(qT[:].rearrange("p c n -> p (c n)"), psum[:, 5, :]).then_inc(qT_kept, 1)

            def exps(l, t, b):
                act.wait_ge(max_found, done(l, t, b))
                for h in range(HEADS):
                    a = nc.scalar.activation(probs[:, h].rearrange("p s j -> p (s j)"), psum[:, h // 2, (h % 2) * 256:(h % 2 + 1) * 256],
                                             ACT.Exp, bias=nmax[:, h:h + 1], scale=1.0, accum_out=psm[:, h:h + 1])
                a.then_inc(exp_done, 1)

            def keep_pT(l, t, b):
                act.wait_ge(pT_ps, 2 * done(l, t, b) - 1)
                nc.scalar.copy(probsT[:, 0:2].rearrange("p a n -> p (a n)"), psum[:, 0:2, :].rearrange("p a n -> p (a n)")).then_inc(pT_act, 1)

            def keep_oT(l, t, b, bank):
                act.wait_ge(oT_ps, done(l, t, b))
                nc.scalar.copy(oT[:].rearrange("p c n -> p (c n)"), psum[:, bank, :]).then_inc(oT_kept, 1)

            def high2(l, t):
                act.wait_ge(h2T_ps, fdone(l, t))
                nc.scalar.copy(h2T[:, 0].rearrange("p c n -> p (c n)"), psum[:, 7, :]).then_inc(h2T_high, 1)

            def gelu(l, t, r):
                act.wait_ge(up_ps, rdone(l, t, r))
                n = FC[r]
                if r >= 2:
                    act.wait_ge(hid_done, rdone(l, t, r - 2))
                nc.scalar.activation(gate[0:n, r % 2, :], psum[0:n, 4 + r % 3, 256:512], ACT.Gelu, bias=b1[0:n, 1, r:r + 1]).then_inc(gelu_done, 1)

            def start(l):
                act.wait_ge(layer_done, l)
                act.wait_ge(in_wqkv, 16 * (l + 1))
                nc.scalar.copy(wqkv[:, 0].rearrange("p c n -> p (c n)"), raw[:].rearrange("p c n -> p (c n)")).then_inc(wqkv_high, 1)
                act.wait_ge(state_reset, l + 1)
                high(l, 0, 0, 4)
                square(l, 0, 0, 5)
                keep_v(l, 0, 0, 7)
                high(l, 0, 1, 3)
                square(l, 0, 1, 0)
                keep_v(l, 0, 1, 2)
                keep_qT(l, 0, 0)

            def step(l, t, first, last):
                keep_qT(l, t, 1)
                if first:
                    act.wait_ge(in_w1, 16 * (l + 1))
                    act.wait_ge(in_small, 16 * 16 * (l + 1))
                    for c in range(DC):
                        nc.scalar.activation(w1[:, 0, c, :], raw[:, c, 0:2 * HID], ACT.Copy, scale=lng[:, c:c + 1]).then_inc(w1_high, 1)
                else:
                    high2(l, t - 1)
                exps(l, t, 0)
                if not first:
                    for r in range(3):
                        gelu(l, t - 1, r)
                keep_pT(l, t, 0)
                if not first:
                    for r in range(3, NF):
                        gelu(l, t - 1, r)
                keep_oT(l, t, 0, 4)
                exps(l, t, 1)
                keep_pT(l, t, 1)
                if not last:
                    high(l, t + 1, 0, 4)
                    square(l, t + 1, 0, 5)
                    keep_v(l, t + 1, 0, 7)
                    high(l, t + 1, 1, 3)
                    square(l, t + 1, 1, 0)
                keep_oT(l, t, 1, 4)
                if not last:
                    keep_v(l, t + 1, 1, 2)
                    keep_qT(l, t + 1, 0)

            def ffn_tail(l, t):
                high2(l, t)
                act.wait_ge(b1_ready, l + 1)
                for r in range(NF):
                    gelu(l, t, r)

            run(act, start, step, ffn_tail)

        @block.vector
        def _(dve):
            def low(l, t, b, bank):
                dve.wait_ge(hT_high, done(l, t, b))
                nc.vector.tensor_tensor(hT[:, b, 1, :, 1:P + 1], psum[:, bank, 0:D].rearrange("p (c n) -> p c n", c=DC),
                                        hT[:, b, 0, :, 1:P + 1].bitcast(F32), ALU.subtract).then_inc(hT_low, 1)

            def rotate(l, t, b, bank):
                dve.wait_ge(squares, done(l, t, b))
                q = psum[:, bank:bank + 2, :].rearrange("p a (h d) -> p a h d", h=HEADS)
                o1 = t1[:, b].rearrange("p (a h d) -> p a h d", a=2, h=HEADS)
                o2 = t2[:, b].rearrange("p (a h d) -> p a h d", a=2, h=HEADS)
                ta = tab[:, t, 0:2].rearrange("p a (o d) -> p a o d", o=1).broadcast_to((P, 2, HEADS, DH))
                tb = tab[:, t, 2:4].rearrange("p a (o d) -> p a o d", o=1).broadcast_to((P, 2, HEADS, DH))
                nc.vector.tensor_tensor(o1, q, ta, ALU.mult)
                nc.vector.tensor_tensor(o2[:, :, :, 0:HALF], q[:, :, :, HALF:DH], tb[:, :, :, 0:HALF], ALU.mult)
                nc.vector.tensor_tensor(o2[:, :, :, HALF:DH], q[:, :, :, 0:HALF], tb[:, :, :, HALF:DH], ALU.mult).then_inc(rot_parts, 1)

            def sum_squares(l, t, b):
                dve.wait_ge(squares, done(l, t, b))
                nc.vector.tensor_reduce(ss[:, b], sq[:].rearrange("p (h d) -> p h d", d=DH), AX.X, ALU.add).then_inc(sumsq_raw, 1)
                dve.wait_ge(sumsq_raw, done(l, t, b))
                nc.vector.tensor_scalar(ss[:, b], ss[:, b], 1e-24, None, ALU.max).then_inc(sumsq, 1)

            def scale_qk(l, t, b):
                dve.wait_ge(rnorm, done(l, t, b))
                dve.wait_ge(rot_sum, done(l, t, b))
                v1 = t1[:, b].rearrange("p (h d) -> p h d", d=DH)
                rb = rn[:, b].rearrange("p (h o) -> p h o", o=1).broadcast_to((P, 2 * HEADS, DH))
                nc.vector.tensor_tensor(v1, v1, rb, ALU.mult).then_inc(qk_final, 1)

            def keep_kT(l, t, b):
                dve.wait_ge(qkT_ps, done(l, t, b))
                nc.vector.tensor_copy(kT[:, b, :, t % 2, :], psum[:, 6, :].rearrange("p (c n) -> p c n", n=P)).then_inc(kT_kept, 1)

            def maxima(l, t, b):
                dve.wait_ge(scores_ps, done(l, t, b))
                nc.vector.tensor_reduce(nmax[:], sc_ps.rearrange("p k (h j) -> p (k h) j", h=2), AX.X, ALU.max, negate=True).then_inc(max_found, 1)

            def keep_pT(l, t, b):
                dve.wait_ge(pT_ps, 2 * done(l, t, b))
                nc.vector.tensor_copy(probsT[:, 2:4].rearrange("p a n -> p (a n)"), psum[:, 2:4, :].rearrange("p a n -> p (a n)")).then_inc(pT_dve, 1)

            def normalise_o(l, t, b, bank):
                dve.wait_ge(exp_done, done(l, t, b))
                nc.vector.reciprocal(rsm[:], psm[:]).then_inc(rsum, 1)
                dve.wait_ge(rsum, done(l, t, b))
                dve.wait_ge(o_ps, done(l, t, b))
                rb = rsm[:].rearrange("p (a c o) -> p c a o", a=2, o=1).broadcast_to((P, HEADS // 2, 2, DH))
                nc.vector.tensor_tensor(o[:].rearrange("p (c a d) -> p c a d", a=2, d=DH), psum[:, bank, :].rearrange("p (c a d) -> p c a d", a=2, d=DH), rb,
                                        ALU.mult).then_inc(o_kept, 1)

            def add_attn(l, t, b):
                dve.wait_ge(wo_ps, done(l, t, b))
                nc.vector.tensor_tensor(x[:, b, t, :], psum[:, 7, 0:D], x[:, b, t, :], ALU.add).then_inc(x_attn, 1)

            def ln_stats(l, t, b):
                plain(dve)
                dve.wait_ge(x_attn, done(l, t, b))
                nc.vector.bn_stats(stats[:, b, 0:6], x[:, b, t, 0:P])
                dve.wait_ge(in_hs[b], 16 * fdone(l, t))
                dve.wait_ge(row_copied, done(l, t, b))
                nc.vector.bn_stats(stats[:, b, 6:12], hs[:, b]).then_inc(stats_done, 1)
                plain(dve)
                dve.wait_ge(stats_done, done(l, t, b))
                nc.vector.bn_aggr(mv[:, b], stats[:, b]).then_inc(mv_done, 1)
                dve.wait_ge(mv_done, done(l, t, b))
                nc.vector.tensor_scalar(ve[:, b:b + 1], mv[:, b, 1:2], LN_EPS, None, ALU.add).then_inc(ve_done, 1)

            def ln_apply(l, t, b):
                dve.wait_ge(rstd_done, done(l, t, b))
                nc.vector.tensor_scalar(hn[:, b, 0:P], x[:, b, t, 0:P], mv[:, b, 0:1], rstd[:, b:b + 1], ALU.subtract, ALU.mult)
                nc.vector.tensor_scalar(hn[:, b, P:D], hs[:, b], mv[:, b, 0:1], rstd[:, b:b + 1], ALU.subtract, ALU.mult).then_inc(hn_done, 1)

            def low2(l, t):
                dve.wait_ge(h2T_high, fdone(l, t))
                nc.vector.tensor_tensor(h2T[:, 1].rearrange("p c n -> p (c n)"), psum[:, 7, :],
                                        h2T[:, 0].rearrange("p c n -> p (c n)").bitcast(F32), ALU.subtract).then_inc(h2T_low, 1)

            def gated(l, t, r):
                dve.wait_ge(gelu_done, rdone(l, t, r))
                n = FC[r]
                nc.vector.scalar_tensor_tensor(hid[0:n, r, :], psum[0:n, 4 + r % 3, 0:256], b1[0:n, 0, r:r + 1], gate[0:n, r % 2, :],
                                               ALU.add, ALU.mult).then_inc(hid_done, 1)

            def add_ffn(l, t, b):
                dve.wait_ge(down_ps, done(l, t, b))
                dve.wait_ge(b2_added, done(l, t, b))
                nc.vector.tensor_tensor(x[:, b, t, :], psum[:, 5 + b, 0:D], x[:, b, t, :], ALU.add).then_inc(x_ffn, 1)

            def start(l):
                dve.wait_ge(in_wqkv, 16 * (l + 1))
                dve.wait_ge(wqkv_high, l + 1)
                nc.vector.tensor_tensor(wqkv[:, 1].rearrange("p c n -> p (c n)"), raw[:].rearrange("p c n -> p (c n)"),
                                        wqkv[:, 0].rearrange("p c n -> p (c n)").bitcast(F32), ALU.subtract).then_inc(wqkv_ready, 1)
                dve.wait_ge(in_tab, 16 * (l + 1))
                dve.wait_ge(in_small, 16 * 16 * (l + 1))
                for n in range(4):
                    tb = tab[:, :, n, :]
                    nc.vector.tensor_tensor(tb, tb, qks[:, n:n + 1, :].broadcast_to((P, nt, DH)), ALU.mult).then_inc(tab_ready, 1)
                dve.wait_ge(tab_ready, 4 * (l + 1))
                low(l, 0, 0, 4)
                rotate(l, 0, 0, 5)
                sum_squares(l, 0, 0)
                low(l, 0, 1, 3)
                scale_qk(l, 0, 0)
                rotate(l, 0, 1, 0)
                sum_squares(l, 0, 1)
                keep_kT(l, 0, 0)
                scale_qk(l, 0, 1)

            def step(l, t, first, last):
                if not first:
                    ln_stats(l, t - 1, 1)
                maxima(l, t, 0)
                if not first:
                    ln_apply(l, t - 1, 1)
                keep_kT(l, t, 1)
                if first:
                    dve.wait_ge(w1_high, DC * (l + 1))
                    for c in range(DC):
                        a = nc.vector.scalar_tensor_tensor(w1[:, 1, c, :], raw[:, c, 0:2 * HID], lng[:, c:c + 1], w1[:, 0, c, :].bitcast(F32),
                                                           ALU.mult, ALU.subtract)
                    a.then_inc(w1_ready, 1)
                    dve.wait_ge(w1_bias_mm, l + 1)
                    b1v = b1[:].rearrange("p g f -> p (g f)")
                    for g in range(2):
                        nc.vector.tensor_tensor(b1[0:FS, g, 0:NF - 1], psum[0:FS, 4, g * NF:g * NF + NF - 1], b1[0:FS, g, 0:NF - 1], ALU.add)
                        a = nc.vector.tensor_tensor(b1[0:FLAST, g, NF - 1:NF], psum[0:FLAST, 4, g * NF + NF - 1:g * NF + NF],
                                                    b1[0:FLAST, g, NF - 1:NF], ALU.add)
                    a.then_inc(b1_ready, 1)
                else:
                    low2(l, t - 1)
                    for r in range(3):
                        gated(l, t - 1, r)
                keep_pT(l, t, 0)
                if not first:
                    for r in range(3, NF):
                        gated(l, t - 1, r)
                normalise_o(l, t, 0, 7)
                maxima(l, t, 1)
                if not first:
                    add_ffn(l, t - 1, 0)
                    add_ffn(l, t - 1, 1)
                keep_pT(l, t, 1)
                add_attn(l, t, 0)
                if not last:
                    low(l, t + 1, 0, 4)
                    rotate(l, t + 1, 0, 5)
                    sum_squares(l, t + 1, 0)
                ln_stats(l, t, 0)
                ln_apply(l, t, 0)
                normalise_o(l, t, 1, 4)
                if not last:
                    low(l, t + 1, 1, 3)
                    scale_qk(l, t + 1, 0)
                    rotate(l, t + 1, 1, 0)
                    sum_squares(l, t + 1, 1)
                add_attn(l, t, 1)
                if not last:
                    keep_kT(l, t + 1, 0)
                    scale_qk(l, t + 1, 1)

            def ffn_tail(l, t):
                ln_stats(l, t, 1)
                ln_apply(l, t, 1)
                low2(l, t)
                for r in range(NF):
                    gated(l, t, r)
                add_ffn(l, t, 0)
                dve.wait_ge(down_ps, done(l, t, 1))
                dve.wait_ge(b2_added, done(l, t, 1))
                nc.vector.tensor_tensor(x[:, 1, t, :], psum[:, 6, 0:D], x[:, 1, t, :], ALU.add).then_inc(x_ffn, 1)
                dve.wait_ge(x_ffn, done(l, t, 1))
                nc.vector.memset(rsm[:], 0.0).then_inc(layer_done, 1)

            run(dve, start, step, ffn_tail)

        @block.gpsimd
        def _(pool):
            nc.gpsimd.memset(mhalf[:], -0.5).then_inc(half_ready, 1)
            nc.gpsimd.memset(zeros[:], 0.0).then_inc(half_ready, 1)
            pool.wait_ge(half_ready, 2)

            def stage(l, t, b, first):
                if not first:
                    pool.wait_ge(xT_ps, done(l, t - 1, b))
                nc.gpsimd.tensor_tensor(xst[:, b], x[:, b, t, :], zeros[:], ALU.add).then_inc(x_staged, 1)
                if not first:
                    pool.wait_ge(v_ps, done(l, t - 1, b))
                    pool.wait_ge(hT_low, done(l, t - 1, b))
                nc.gpsimd.tensor_tensor(hT[:, b, :, 1, 0:1], hT[:, b, :, 1, P:P + 1].bitcast(F32),
                                        zeros[:, 0:2].rearrange("p (a o) -> p a o", o=1), ALU.add).then_inc(col_carried, 1)

            def qk_norm(l, t, b):
                pool.wait_ge(sumsq, done(l, t, b))
                nc.gpsimd.tensor_tensor(rn[:, b], ss[:, b], mhalf[:], ALU.pow).then_inc(rnorm, 1)
                pool.wait_ge(rot_parts, done(l, t, b))
                nc.gpsimd.tensor_tensor(t1[:, b], t1[:, b], t2[:, b], ALU.add).then_inc(rot_sum, 1)

            def row(l, t, b, first):
                if not first:
                    pool.wait_ge(hn_done, done(l, t - 1, b))
                    pool.wait_ge(in_row[b], 16 * fdone(l, t - 1))
                nc.gpsimd.tensor_tensor(hs[0:1, b], lastrow[0:1, b], zeros[0:1, 0:P], ALU.add).then_inc(row_copied, 1)

            def ln_rstd(l, t, b):
                pool.wait_ge(ve_done, done(l, t, b))
                nc.gpsimd.tensor_tensor(rstd[:, b:b + 1], ve[:, b:b + 1], mhalf[:, 0:1], ALU.pow).then_inc(rstd_done, 1)

            def add_b2(l, t, b):
                pool.wait_ge(hn_done, done(l, t, b))
                pool.wait_ge(in_row[b], 16 * fdone(l, t))
                nc.gpsimd.tensor_tensor(x[:, b, t, :], x[:, b, t, :], b2[:], ALU.add).then_inc(b2_added, 1)

            def start(l):
                plain(pool)
                pool.wait_ge(layer_done, l)
                nc.gpsimd.memset(hT[:, :, :, 1, P:P + 1].bitcast(F32), 0.0)
                nc.gpsimd.memset(lastrow[:], 0.0)
                nc.gpsimd.memset(kT[:, :, :, 1, :], 0.0)
                nc.gpsimd.memset(v[:, :, 1, :], 0.0).then_inc(state_reset, 1)
                pool.wait_ge(state_reset, l + 1)
                stage(l, 0, 0, True)
                stage(l, 0, 1, True)
                qk_norm(l, 0, 0)
                qk_norm(l, 0, 1)

            def step(l, t, first, last):
                if not first:
                    ln_rstd(l, t - 1, 1)
                row(l, t, 0, first)
                row(l, t, 1, first)
                if not first:
                    add_b2(l, t - 1, 1)
                if not last:
                    stage(l, t + 1, 0, False)
                    stage(l, t + 1, 1, False)
                    qk_norm(l, t + 1, 0)
                ln_rstd(l, t, 0)
                add_b2(l, t, 0)
                if not last:
                    qk_norm(l, t + 1, 1)

            def ffn_tail(l, t):
                ln_rstd(l, t, 1)
                add_b2(l, t, 1)

            run(pool, start, step, ffn_tail)


def sum_block(nc, x, nt, x1_dram, out_dram):
    with ExitStack() as ctx:
        step = 2
        pieces = [(b, t) for t in range(0, nt, step) for b in range(B)]
        x1 = ctx.enter_context(nc.sbuf_tensor("s_x1", [P, B, nt, D], F32))
        loaded = [ctx.enter_context(nc.semaphore(f"s_loaded{i}")) for i in range(len(pieces))]
        summed = ctx.enter_context(nc.semaphore("s_summed"))
        stored = ctx.enter_context(nc.semaphore("s_stored"))
        block = ctx.enter_context(nc.Block())

        def rows(dram, b, t):
            return dram[b, t * P:(t + step) * P].rearrange("(t p) d -> p t d", p=P)

        @block.sync
        def _(sp):
            for i, (b, t) in enumerate(pieces):
                sp.dma_start(x1[:, b, t:t + step], rows(x1_dram, b, t)).then_inc(loaded[i], 16)

        @block.vector
        def _(dve):
            for i, (b, t) in enumerate(pieces):
                dve.wait_ge(loaded[i], 16)
                xs = x[:, b, t:t + step]
                nc.vector.tensor_tensor(xs, xs, x1[:, b, t:t + step], ALU.add).then_inc(summed, 1)

        @block.scalar
        def _(act):
            for i, (b, t) in enumerate(pieces):
                act.wait_ge(summed, i + 1)
                act.dma_start(rows(out_dram, b, t), x[:, b, t:t + step]).then_inc(stored, 16)
            act.wait_ge(stored, 16 * len(pieces))


def build_program(nc, ins, out):
    _, n, _ = ins["x"].shape
    nt = n // P
    depth = ins["wqkv"].shape[0]
    x1_dram = nc.dram_tensor("x1_scratch", (B, n, D), F32).ap()
    with ExitStack() as ctx:
        x = ctx.enter_context(nc.sbuf_tensor("x", [P, B, nt, D], F32))
        flow_block(nc, x, nt, ins, ins["x"], x1_dram)
        layers_block(nc, x, nt, depth, ins)
        sum_block(nc, x, nt, x1_dram, out)


_ATTN = ["x", "Wq", "bq", "Wk", "bk", "Wv", "bv", "Wo", "bo"]
_FFN = ["wqkv", "q_scale", "k_scale", "wo", "ln_g", "ln_b", "w1", "b1", "w2", "b2"]


def kernel(**inputs):
    import concourse.bacc as bacc
    from concourse.bass_utils import run_bass_kernel_spmd

    arrays = {n: np.ascontiguousarray(inputs["L0_attn_" + n]) for n in _ATTN}
    arrays |= {n: np.ascontiguousarray(inputs["L0_ffn_" + n]) for n in _FFN}
    n = arrays["x"].shape[1]
    arrays |= {
        "ident": np.eye(P, dtype=np.float32),
        "tables": position_tables(n),
        "masks": window_masks(),
        "flow_masks": flow_masks(),
        "head_spread": head_spread(),
        "counts": counts(n // P),
    }
    nc = bacc.Bacc("TRN2", target_bir_lowering=False, num_devices=1)
    ins = {k: nc.dram_tensor(f"in_{k}", a.shape, mybir.dt.from_np(a.dtype), kind="ExternalInput").ap() for k, a in arrays.items()}
    out = nc.dram_tensor("out", arrays["x"].shape, F32, kind="ExternalOutput").ap()
    build_program(nc, ins, out)
    r = run_bass_kernel_spmd(nc, [{f"in_{k}": a for k, a in arrays.items()}], core_ids=[0])
    return r.results[0]["out"]
```

```python
from contextlib import ExitStack

import concourse.bass as bass
import numpy as np
from concourse import mybir

F32 = mybir.dt.float32
F32R = mybir.dt.float32r
BF16 = mybir.dt.bfloat16
ALU = mybir.AluOpType
ACT = mybir.ActivationFunctionType
AX = mybir.AxisListType

P = 128
D = 256
DC = D // P
B = 2
HEADS = 8
DH = 64
INNER = HEADS * DH
HALF = DH // 2
HID = int(D * 4 * 2 / 3)
NF = 6
FS = -(-HID // NF)
FLAST = HID - (NF - 1) * FS
FC = [FS] * (NF - 1) + [FLAST]
WINDOW = 128
QK_SCALE = 8.0
LN_EPS = 1e-5
FH = 16
FD = D // FH
FLOW_EPS = 1e-6
NEG = -3.0e38


def position_tables(n):
    f = np.float32
    half = np.arange(0, DH, 2, dtype=f)
    inv_freq = (f(1.0) / f(10000.0) ** (half / f(DH))).astype(f)
    t = np.arange(n, dtype=f)
    fr = t[:, None] * inv_freq[None, :]
    base = (half + f(0.4 * DH)) / f(1.4 * DH)
    power = (t - f(n // 2)) / f(WINDOW // 2)
    scale = base[None, :] ** power[:, None]
    cos, sin = np.cos(fr), np.sin(fr)
    out = np.empty((n, 4, 2, HALF), f)
    for kind, s in ((0, scale * f(QK_SCALE)), (1, f(1.0) / scale)):
        out[:, kind, 0] = out[:, kind, 1] = cos * s
        out[:, 2 + kind, 0] = -sin * s
        out[:, 2 + kind, 1] = sin * s
    return out.reshape(n, 4, DH)


def window_masks():
    i = np.arange(P)[:, None]
    j = np.arange(P)[None, :]
    own = np.where(j <= i, 0.0, NEG)
    front = np.where(j >= i, 0.0, NEG)
    none = np.full((P, P), NEG)
    one = np.stack([np.stack([own, front]), np.stack([front, own]), np.stack([own, none])])
    m = np.broadcast_to(one.transpose(2, 0, 1, 3)[:, :, None], (P, 3, 2, 2, P))
    return np.ascontiguousarray(m).astype(np.float32).reshape(P, -1)


def flow_masks():
    f = np.arange(P)
    tri = (f[:, None] <= f[None, :]).astype(np.float32)
    head_sum = (f[:, None] // FD == np.arange(P // FD)[None, :]).astype(np.float32)
    block = (f[:, None] // FD == f[None, :] // FD).astype(np.float32)
    odd = (f[:, None] // FD % 2).astype(np.float32)
    return np.concatenate([tri, head_sum, block, odd, np.ones((P, P), np.float32)], axis=1)


def head_spread():
    out = np.zeros((2 * FH, 2 * DC, P), np.float32)
    for a in range(2):
        for c in range(DC):
            for f in range(P):
                out[a * FH + c * (P // FD) + f // FD, a * DC + c, f] = 1
    return out


def counts(nt):
    n = (np.arange(nt)[None, :] * P + np.arange(P)[:, None] + 1).astype(np.float32)
    return np.stack([n, 1 / n], axis=1)


def flow_block(nc, x, nt, w, x_dram, x1_dram):
    with ExitStack() as ctx:
        def sb(name, shape, dt=F32):
            return ctx.enter_context(nc.sbuf_tensor("f_" + name, shape, dt))

        def sem(name):
            return ctx.enter_context(nc.semaphore("f_" + name))

        psum = ctx.enter_context(nc.psum_tensor("f_psum", [P, 8, 512], F32))
        G = P // FD
        NP = B * P

        raw = sb("raw", [P, DC, 3 * D])
        wqkv = sb("wqkv", [P, 2, DC, 3 * D], F32R)
        wo = sb("wo", [P, DC, D])
        bqk = sb("bqk", [P, 2, DC])
        bv = sb("bv", [P, D])
        bo = sb("bo", [P, D])
        ident = sb("ident", [P, P])
        consts = sb("consts", [P, 3 * P + G + 1])
        tri = consts[:, 0:P]
        head_sum = consts[:, P:P + G]
        block_of = consts[:, P + G:2 * P + G]
        odd = consts[:, 2 * P + G:2 * P + G + 1]
        ones = consts[:, 2 * P + G + 1:3 * P + G + 1]
        spread = sb("spread", [2 * FH, 2 * DC, P])
        count = sb("count", [P, 2, nt])
        mhalf = sb("mhalf", [P, 2])
        euler = sb("euler", [P, B * FH])

        stats = sb("stats", [P, 2, B, 6])
        mv = sb("mv", [P, 2, B, 2])
        ve = sb("ve", [P, 2, B])
        rstd = sb("rstd", [P, 2, B])
        hn = sb("hn", [P, B, D])
        hT = sb("hT", [P, 2, DC, NP], F32R)
        qk = sb("qk", [P, 2, 2 * DC, B, P])
        qk_back = sb("qk_back", [P, 2 * DC, B, P])
        q_odd = sb("q_odd", [P, DC, B, P])
        cum = sb("cum", [P, 2 * DC, B, P])
        carry = sb("carry", [P, 2, 2 * DC, B])
        wtd = sb("wtd", [P, 2 * DC, B, P])
        prod = sb("prod", [P, 2, 2 * DC, B, P])
        recip = sb("recip", [P, B, 2, FH])
        recip_n = sb("recip_n", [P, B, 2, FH])
        rT = sb("rT", [2 * FH, B, P])
        r_q = sb("r_q", [P, 2, B, FH])
        cons = sb("cons", [P, 2, B, FH])
        alloc = sb("alloc", [P, B, FH])
        fac = sb("fac", [P, B, FH])
        cs = sb("cs", [P, B, FH])
        cs_sum = sb("cs_sum", [P, B, FH])
        rcs = sb("rcs", [P, B, FH])
        comp = sb("comp", [P, B, FH])
        vb = sb("vb", [P, 2, B, D])
        vs = sb("vs", [P, B, D])
        k_tok = sb("k_tok", [P, B, D])
        st = sb("st", [P, B, 4, 512])
        s_new = sb("s_new", [P, B, D])
        state = sb("state", [P, B, D])
        o = sb("o", [P, B, D])
        oT = sb("oT", [P, DC, B, P])
        x1 = sb("x1", [P, B, D])

        names = """in_const w_high w_ready reset stats_in mv_in ve_in rstd_in hn_in hT_ps hT_high
            hT_low qk_ps v_ps qk_sig v_kept cum1 carry1 prod1 sums1 recip1 recip_n1 rT_ps rT_kept
            spread_ps weighted cum2 carry2 prod2 sums2 cons_done alloc_done fac_done cs_done
            cs_cum cs_added rcs_done comp_done vs_done rq_kept kt_ps kt_kept st_ps st_kept o_ps
            o_kept s_ps s_masked s_added qk_copied q_odd_done oT_ps oT_kept wo_ps bo_added x1_done
            stats_x1 mv_x1 ve_x1 rstd_x1 x_normed""".split()
        S = {n: sem(n) for n in names}
        in_x = [sem(f"in_x{b}") for b in range(B)]
        out_x1 = sem("out_x1")

        def run(step):
            def go(eng):
                step(0, True, False, False)
                step(1, True, True, False)
                with eng.Fori(2, nt) as t:
                    step(t, True, True, True)
                step(nt, False, True, True)
                step(nt + 1, False, False, True)
            return go

        block = ctx.enter_context(nc.Block())
        NCONST = 16 * 12

        def plain(eng):
            eng.wait_ge(S["in_const"], NCONST)

        @block.sync
        def _(sp):
            sp.dma_start(x[:, 0, 0, :], x_dram[0, 0:P]).then_inc(in_x[0], 16)
            sp.dma_start(x[:, 1, 0, :], x_dram[1, 0:P]).then_inc(in_x[1], 16)
            n = S["in_const"]
            for j, m in enumerate(("Wq", "Wk", "Wv")):
                sp.dma_start(raw[:, :, j * D:(j + 1) * D], w[m].rearrange("(c p) n -> p c n", p=P)).then_inc(n, 16)
            sp.dma_start(ident[:], w["ident"]).then_inc(n, 16)
            for j, m in enumerate(("bq", "bk")):
                sp.dma_start(bqk[:, j], w[m].rearrange("(c p) -> p c", p=P), allow_slow_non_contiguous=True).then_inc(n, 16)
            sp.dma_start(bv[:], w["bv"].rearrange("(a d) -> a d", a=1).partition_broadcast(P)).then_inc(n, 16)
            sp.dma_start(bo[:], w["bo"].rearrange("(a d) -> a d", a=1).partition_broadcast(P)).then_inc(n, 16)
            sp.dma_start(consts[:], w["flow_masks"]).then_inc(n, 16)
            sp.dma_start(spread[:], w["head_spread"]).then_inc(n, 16)
            sp.dma_start(count[:], w["counts"]).then_inc(n, 16)
            sp.dma_start(wo[:], w["Wo"].rearrange("(c p) n -> p c n", p=P)).then_inc(n, 16)

            with sp.Fori(1, nt) as t:
                for b in range(B):
                    plain(sp)
                    sp.wait_ge(in_x[b], 16 * t)
                    sp.dma_start(x[:, b, t, :], x_dram[b, bass.ds(t * P, P)]).then_inc(in_x[b], 16)
            with sp.Fori(0, nt) as t:
                plain(sp)
                sp.wait_ge(S["x1_done"], t + 1)
                sp.dma_start(x1_dram[:, bass.ds(t * P, P), :].rearrange("b p d -> p b d"), x1[:]).then_inc(out_x1, 16)
            sp.wait_ge(out_x1, 16 * nt)

        @block.tensor
        def _(pe):
            def hT_stage(t):
                pe.wait_ge(S["hn_in"], t + 1)
                for c in range(DC):
                    for b in range(B):
                        mm = nc.tensor.transpose(psum[:, 7, (c * B + b) * P:(c * B + b + 1) * P], hn[:, b, c * P:(c + 1) * P], ident[:])
                mm.then_inc(S["hT_ps"], 1)

            def qk_stage(t):
                for g in range(2 * DC):
                    n = 0
                    for c in range(DC):
                        for m, a in ((0, 0), (0, 1), (1, 0)):
                            mm = nc.tensor.matmul(psum[:, 4 + g // 2, (g % 2) * NP:(g % 2 + 1) * NP], wqkv[:, m, c, g * P:(g + 1) * P],
                                                  hT[:, a, c, :], start=(n == 0), stop=(n == 5))
                            n += 1
                mm.then_inc(S["qk_ps"], 1)

            def v_stage(t):
                for b in range(B):
                    n = 0
                    for c in range(DC):
                        for a, m in ((0, 0), (0, 1), (1, 0)):
                            mm = nc.tensor.matmul(psum[:, 6, b * D:(b + 1) * D], hT[:, a, c, b * P:(b + 1) * P], wqkv[:, m, c, 2 * D:3 * D],
                                                  start=(n == 0), stop=(n == 5))
                            n += 1
                mm.then_inc(S["v_ps"], 1)

            def head_sums(t, i, bank, ready, made):
                pe.wait_ge(S[ready], t + 1)
                for b in range(B):
                    for g in range(2 * DC):
                        n = (b * 2 * DC + g) * G
                        mm = nc.tensor.matmul(psum[:, bank, n:n + G], prod[:, i, g, b, :], head_sum, start=True, stop=True)
                mm.then_inc(S[made], 1)

            def rT_stage(t):
                pe.wait_ge(S["recip_n1"], t + 1)
                for b in range(B):
                    mm = nc.tensor.transpose(psum[0:2 * FH, 6, b * P:(b + 1) * P], recip_n[:, b].rearrange("p a h -> p (a h)"), ident[:])
                mm.then_inc(S["rT_ps"], 1)

            def spread_stage(t):
                pe.wait_ge(S["rT_kept"], t + 1)
                for g in range(2 * DC):
                    mm = nc.tensor.matmul(psum[:, 4 + g // 2, (g % 2) * NP:(g % 2 + 1) * NP], spread[:, g, :],
                                          rT[:].rearrange("p b n -> p (b n)"), start=True, stop=True)
                mm.then_inc(S["spread_ps"], 1)

            def scores(t, b):
                for k in range(4):
                    for r in range(4):
                        c, par = k // 2, k % 2
                        rows = slice(32 * r, 32 * r + (32 if par else 16))
                        q = q_odd[rows, c, b, :] if par else qk_back[rows, c, b, :]
                        mm = nc.tensor.matmul(psum[:, r, k * P:(k + 1) * P], qk_back[rows, DC + c, b, :], q, start=True, stop=True)
                mm.then_inc(S["st_ps"], 1)

            def kt_stage(t):
                for b in range(B):
                    for c in range(DC):
                        mm = nc.tensor.transpose(psum[:, 7, (b * DC + c) * P:(b * DC + c + 1) * P], qk_back[:, DC + c, b, :], ident[:])
                mm.then_inc(S["kt_ps"], 1)

            def cs_stage(t):
                pe.wait_ge(S["cs_done"], t + 1)
                out = psum[:, 5, 0:B * FH]
                nc.tensor.matmul(out, tri, cs[:].rearrange("p b h -> p (b h)"), start=True, stop=False)
                pe.wait_ge(S["cs_added"], t + 2)
                nc.tensor.matmul(out, ones, cs_sum[:].rearrange("p b h -> p (b h)"), start=False, stop=True).then_inc(S["cs_cum"], 1)

            def values(t, b):
                bank = 7 if b == 0 else 1
                pe.wait_ge(S["s_added"], t + 1)
                for c in range(DC):
                    nc.tensor.matmul(psum[:, bank, c * P:(c + 1) * P], qk_back[:, c, b, :], state[:, b, c * P:(c + 1) * P],
                                     start=(c == 0), stop=False, skip_group_check=True)
                pe.wait_ge(S["st_kept"], 2 * t + b + 1)
                pe.wait_ge(S["vs_done"], t + 1)
                for r in range(4):
                    for k in range(4):
                        h = (k // 2) * G + 2 * r + k % 2
                        cols = h * FD
                        mm = nc.tensor.matmul(psum[:, bank, cols:cols + FD], st[:, b, r, k * P:(k + 1) * P], vs[:, b, h * FD:(h + 1) * FD],
                                              start=False, stop=True, skip_group_check=True)
                mm.then_inc(S["o_ps"], 1)

            def state_stage(t):
                for b in range(B):
                    for c in range(DC):
                        cols = slice(c * P, (c + 1) * P)
                        mm = nc.tensor.matmul(psum[:, 2, b * D + c * P:b * D + (c + 1) * P], k_tok[:, b, cols], vs[:, b, cols], start=True, stop=True)
                mm.then_inc(S["s_ps"], 1)

            def oT_stage(t):
                pe.wait_ge(S["o_kept"], 2 * t + 2)
                for c in range(DC):
                    for b in range(B):
                        mm = nc.tensor.transpose(psum[:, 3, (c * B + b) * P:(c * B + b + 1) * P], o[:, b, c * P:(c + 1) * P], ident[:])
                mm.then_inc(S["oT_ps"], 1)

            def wo_stage(t):
                pe.wait_ge(S["oT_kept"], t + 1)
                for b in range(B):
                    for c in range(DC):
                        mm = nc.tensor.matmul(psum[:, 6, b * D:(b + 1) * D], oT[:, c, b, :], wo[:, c, :], start=(c == 0), stop=(c == DC - 1))
                mm.then_inc(S["wo_ps"], 1)

            pe.wait_ge(S["in_const"], NCONST)
            pe.wait_ge(S["w_ready"], 1)

            def step(t, front, middle, back):
                v, u = t - 1, t - 2
                if middle:
                    pe.wait_ge(S["v_kept"], v + 1)
                if back:
                    pe.wait_ge(S["x1_done"], u)
                    pe.wait_ge(S["qk_sig"], t if front else nt)
                if middle:
                    rT_stage(v)
                if back:
                    cs_stage(u)
                if front:
                    hT_stage(t)
                if back:
                    pe.wait_ge(S["qk_copied"], u + 1)
                    pe.wait_ge(S["q_odd_done"], u + 1)
                    pe.wait_ge(S["cons_done"], u + 1)
                    scores(u, 0)
                if middle:
                    pe.wait_ge(S["qk_sig"], v + 1)
                    pe.wait_ge(S["recip1"], v + 1)
                    if back:
                        pe.wait_ge(S["rcs_done"], u + 1)
                    spread_stage(v)
                if front:
                    pe.wait_ge(S["hT_low"], t + 1)
                if back:
                    kt_stage(u)
                if front:
                    v_stage(t)
                if back:
                    pe.wait_ge(S["st_kept"], 2 * u + 1)
                    scores(u, 1)
                if front:
                    if middle:
                        pe.wait_ge(S["weighted"], v + 1)
                    qk_stage(t)
                if back:
                    pe.wait_ge(S["kt_kept"], u + 1)
                    values(u, 0)
                    pe.wait_ge(S["st_kept"], 2 * u + 2)
                if middle:
                    head_sums(v, 1, 0, "prod2", "sums2")
                if back:
                    values(u, 1)
                    state_stage(u)
                if front:
                    head_sums(t, 0, 4, "prod1", "sums1")
                if back:
                    oT_stage(u)
                    if front:
                        pe.wait_ge(S["v_kept"], t + 1)
                    wo_stage(u)

            run(step)(pe)

        @block.scalar
        def _(act):
            act.wait_ge(S["in_const"], NCONST)
            nc.scalar.copy(wqkv[:, 0].rearrange("p c n -> p (c n)"), raw[:].rearrange("p c n -> p (c n)")).then_inc(S["w_high"], 1)

            def step(t, front, middle, back):
                v, u = t - 1, t - 2
                if middle:
                    act.wait_ge(S["rT_ps"], v + 1)
                    nc.scalar.copy(rT[:].rearrange("p b n -> p (b n)"), psum[0:2 * FH, 6, 0:NP]).then_inc(S["rT_kept"], 1)
                if front:
                    act.wait_ge(S["hT_ps"], t + 1)
                    if middle:
                        act.wait_ge(S["qk_ps"], t)
                    nc.scalar.copy(hT[:, 0].rearrange("p c n -> p (c n)"), psum[:, 7, :]).then_inc(S["hT_high"], 1)
                if back:
                    act.wait_ge(S["kt_ps"], u + 1)
                    nc.scalar.copy(k_tok[:].rearrange("p b n -> p (b n)"), psum[:, 7, :]).then_inc(S["kt_kept"], 1)
                if front:
                    act.wait_ge(S["qk_ps"], t + 1)
                    if back:
                        act.wait_ge(S["prod2"], u + 1)
                        act.wait_ge(S["qk_copied"], u + 1)
                    for g in range(2 * DC):
                        a = nc.scalar.activation(qk[:, t % 2, g].rearrange("p b n -> p (b n)"), psum[:, 4 + g // 2, (g % 2) * NP:(g % 2 + 1) * NP],
                                                 ACT.Sigmoid, bias=bqk[:, g // DC, g % DC:g % DC + 1], scale=1.0)
                    a.then_inc(S["qk_sig"], 1)
                if middle:
                    act.wait_ge(S["cons_done"], v + 1)
                    if back:
                        act.wait_ge(S["fac_done"], v)
                    nc.scalar.activation(alloc[:], cons[:, 0], ACT.Sigmoid).then_inc(S["alloc_done"], 1)
                    act.wait_ge(S["qk_sig"], v + 1)
                    if back:
                        act.wait_ge(S["o_ps"], 2 * u + 2)
                        act.wait_ge(S["q_odd_done"], v)
                    nc.scalar.copy(qk_back[:].rearrange("p g b n -> p (g b n)"), qk[:, v % 2].rearrange("p g b n -> p (g b n)")).then_inc(S["qk_copied"], 1)
                if back:
                    act.wait_ge(S["oT_ps"], u + 1)
                    nc.scalar.copy(oT[:].rearrange("p c b n -> p (c b n)"), psum[:, 3, :]).then_inc(S["oT_kept"], 1)

            run(step)(act)

        @block.vector
        def _(dve):
            def chain(ins, name, n):
                ins.then_inc(S[name], 1)
                dve.wait_ge(S[name], n)

            def norm_stats(src, b, i, tag, n):
                nc.vector.bn_stats(stats[:, i, b], src).then_inc(S["stats_" + tag], 1)

            def norm_in(t):
                for b in range(B):
                    plain(dve)
                    dve.wait_ge(in_x[b], 16 * (t + 1))
                    a = nc.vector.bn_stats(stats[:, 0, b], x[:, b, t, :])
                a.then_inc(S["stats_in"], 1)
                norm_rest("in", 0, t)
                for b in range(B):
                    a = nc.vector.tensor_scalar(hn[:, b], x[:, b, t, :], mv[:, 0, b, 0:1], rstd[:, 0, b:b + 1], ALU.subtract, ALU.mult)
                a.then_inc(S["hn_in"], 1)

            def norm_rest(tag, i, t):
                plain(dve)
                dve.wait_ge(S["stats_" + tag], t + 1)
                for b in range(B):
                    a = nc.vector.bn_aggr(mv[:, i, b], stats[:, i, b])
                a.then_inc(S["mv_" + tag], 1)
                dve.wait_ge(S["mv_" + tag], t + 1)
                nc.vector.tensor_scalar(ve[:, i], mv[:, i, :, 1], LN_EPS, None, ALU.add).then_inc(S["ve_" + tag], 1)
                dve.wait_ge(S["rstd_" + tag], t + 1)

            def scans(t, i, src, name):
                dve.wait_ge(S["reset"], 4)
                for g in range(2 * DC):
                    for b in range(B):
                        a = nc.vector.tensor_tensor_scan(cum[:, g, b, :], ones, src[:, g, b, :], carry[:, i, g, b:b + 1], ALU.mult, ALU.add)
                a.then_inc(S[name], 1)
                dve.wait_ge(S[name], t + 1)
                nc.vector.tensor_copy(carry[:, i], cum[:, :, :, P - 1]).then_inc(S["carry1" if i == 0 else "carry2"], 1)

            def products(t, i, qkt, name):
                for a in range(2):
                    f = lambda v, n: v[:, n * DC:(n + 1) * DC].rearrange("p c b n -> p (c b n)")
                    ins = nc.vector.scalar_tensor_tensor(f(prod[:, i], a), f(qkt, a), FLOW_EPS, f(cum, 1 - a), ALU.add, ALU.mult)
                ins.then_inc(S[name], 1)

            dve.wait_ge(S["w_high"], 1)
            nc.vector.tensor_tensor(wqkv[:, 1].rearrange("p c n -> p (c n)"), raw[:].rearrange("p c n -> p (c n)"),
                                    wqkv[:, 0].rearrange("p c n -> p (c n)").bitcast(F32), ALU.subtract).then_inc(S["w_ready"], 1)
            nc.vector.memset(carry[:], FLOW_EPS).then_inc(S["reset"], 1)
            norm_in(0)

            def mask_scores(u, b):
                dve.wait_ge(S["st_ps"], 2 * u + b + 1)
                nc.vector.tensor_tensor(st[:, b].rearrange("p r (k i) -> p (r k) i", k=4), psum[:, 0:4, :].rearrange("p r (k i) -> p (r k) i", k=4),
                                        tri.rearrange("p (o i) -> p o i", o=1).broadcast_to((P, 16, P)), ALU.mult).then_inc(S["st_kept"], 1)

            def keep_o(u, b):
                if b == 0:
                    dve.wait_ge(S["fac_done"], u + 1)
                    if not (isinstance(u, int) and u == 0):
                        dve.wait_ge(S["oT_ps"], u)
                dve.wait_ge(S["o_ps"], 2 * u + b + 1)
                nc.vector.tensor_tensor(o[:, b].rearrange("p (h d) -> p h d", d=FD), psum[:, 7 if b == 0 else 1, 0:D].rearrange("p (h d) -> p h d", d=FD),
                                        fac[:, b].rearrange("p (h o) -> p h o", o=1).broadcast_to((P, FH, FD)), ALU.mult).then_inc(S["o_kept"], 1)

            def step(t, front, middle, back, more):
                v, u = t - 1, t - 2
                if front:
                    dve.wait_ge(S["hT_high"], t + 1)
                    nc.vector.tensor_tensor(hT[:, 1].rearrange("p c n -> p (c n)"), psum[:, 7, :],
                                            hT[:, 0].rearrange("p c n -> p (c n)").bitcast(F32), ALU.subtract).then_inc(S["hT_low"], 1)
                if back:
                    dve.wait_ge(S["cs_cum"], u + 1)
                    nc.vector.reciprocal(rcs[:].rearrange("p b h -> p (b h)"), psum[:, 5, 0:B * FH]).then_inc(S["rcs_done"], 1)
                    dve.wait_ge(S["rcs_done"], u + 1)
                    dve.wait_ge(S["vs_done"], u)
                    nc.vector.scalar_tensor_tensor(comp[:], cs[:], count[:, 0, bass.ds(u, 1)], rcs[:], ALU.mult, ALU.mult).then_inc(S["comp_done"], 1)
                    mask_scores(u, 0)
                if middle:
                    dve.wait_ge(S["spread_ps"], v + 1)
                    dve.wait_ge(S["qk_sig"], v + 1)
                    nc.vector.tensor_tensor(wtd[:].rearrange("p g b n -> p (g b n)"), psum[:, 4:6, :].rearrange("p a n -> p (a n)"),
                                            qk[:, v % 2].rearrange("p g b n -> p (g b n)"), ALU.mult).then_inc(S["weighted"], 1)
                    dve.wait_ge(S["weighted"], v + 1)
                    dve.wait_ge(S["prod1"], v + 1)
                    dve.wait_ge(S["carry1"], v + 1)
                    if back:
                        dve.wait_ge(S["carry2"], v)
                    scans(v, 1, wtd, "cum2")
                    if back:
                        dve.wait_ge(S["sums2"], v)
                    products(v, 1, qk[:, v % 2], "prod2")
                if front:
                    dve.wait_ge(S["v_ps"], t + 1)
                    if back:
                        dve.wait_ge(S["vs_done"], u + 1)
                    nc.vector.tensor_tensor(vb[:, t % 2], psum[:, 6, :].rearrange("p (b d) -> p b d", b=B),
                                            bv[:].rearrange("p (o d) -> p o d", o=1).broadcast_to((P, B, D)), ALU.add).then_inc(S["v_kept"], 1)
                if back:
                    mask_scores(u, 1)
                if more:
                    norm_in(t + 1)
                if back:
                    keep_o(u, 0)
                if front:
                    dve.wait_ge(S["qk_sig"], t + 1)
                    if middle:
                        dve.wait_ge(S["carry1"], t)
                        dve.wait_ge(S["prod2"], v + 1)
                        dve.wait_ge(S["carry2"], v + 1)
                        dve.wait_ge(S["sums1"], t)
                    scans(t, 0, qk[:, t % 2], "cum1")
                    products(t, 0, qk[:, t % 2], "prod1")
                if middle:
                    dve.wait_ge(S["sums2"], v + 1)
                    if back:
                        dve.wait_ge(S["alloc_done"], v)
                        dve.wait_ge(S["cs_done"], v)
                    nc.vector.tensor_scalar(cons[:].rearrange("p a b h -> p b a h"), psum[:, 0, 0:2 * B * FH].rearrange("p (b a h) -> p b a h", b=B, a=2),
                                            count[:, 1, bass.ds(v, 1)], None, ALU.mult).then_inc(S["cons_done"], 1)
                if back:
                    keep_o(u, 1)
                    dve.wait_ge(S["s_ps"], u + 1)
                    dve.wait_ge(S["s_added"], u + 1)
                    nc.vector.tensor_tensor(s_new[:].rearrange("p b (c f) -> p (b c) f", f=P), psum[:, 2, :].rearrange("p (a f) -> p a f", f=P),
                                            block_of.rearrange("p (o f) -> p o f", o=1).broadcast_to((P, B * DC, P)), ALU.mult).then_inc(S["s_masked"], 1)
                if front:
                    dve.wait_ge(S["sums1"], t + 1)
                    if middle:
                        dve.wait_ge(S["rT_ps"], t)
                    nc.vector.reciprocal(recip[:].rearrange("p b a h -> p (b a h)"), psum[:, 4, 0:2 * B * FH]).then_inc(S["recip1"], 1)
                    dve.wait_ge(S["recip1"], t + 1)
                    nc.vector.tensor_scalar(recip_n[:].rearrange("p b a h -> p (b a h)"), recip[:].rearrange("p b a h -> p (b a h)"),
                                            count[:, 0, bass.ds(t, 1)], None, ALU.mult).then_inc(S["recip_n1"], 1)
                    nc.vector.tensor_copy(r_q[:, t % 2], recip[:, :, 0, :]).then_inc(S["rq_kept"], 1)
                if middle:
                    dve.wait_ge(S["alloc_done"], v + 1)
                    dve.wait_ge(S["rq_kept"], v + 1)
                    if back:
                        dve.wait_ge(S["o_kept"], 2 * u + 2)
                    nc.vector.tensor_tensor(fac[:], alloc[:], r_q[:, v % 2], ALU.mult).then_inc(S["fac_done"], 1)
                    dve.wait_ge(S["qk_copied"], v + 1)
                    nc.vector.tensor_scalar(q_odd[:].rearrange("p c b n -> p (c b n)"), qk_back[:, 0:DC].rearrange("p c b n -> p (c b n)"),
                                            odd, None, ALU.mult).then_inc(S["q_odd_done"], 1)
                if back:
                    dve.wait_ge(S["wo_ps"], u + 1)
                    dve.wait_ge(S["bo_added"], u + 1)
                    if not (isinstance(t, int) and t <= 2):
                        dve.wait_ge(out_x1, 16 * u)
                    nc.vector.tensor_tensor(x1[:], psum[:, 6, :].rearrange("p (b d) -> p b d", b=B), x[:, :, u, :], ALU.add).then_inc(S["x1_done"], 1)
                    dve.wait_ge(S["x1_done"], u + 1)
                    for b in range(B):
                        a = nc.vector.bn_stats(stats[:, 1, b], x1[:, b])
                    a.then_inc(S["stats_x1"], 1)
                    norm_rest("x1", 1, u)
                    for b in range(B):
                        a = nc.vector.tensor_scalar(x[:, b, u, :], x1[:, b], mv[:, 1, b, 0:1], rstd[:, 1, b:b + 1], ALU.subtract, ALU.mult)
                    a.then_inc(S["x_normed"], 1)

            step(0, True, False, False, True)
            step(1, True, True, False, True)
            with dve.Fori(2, nt - 1) as t:
                step(t, True, True, True, True)
            step(nt - 1, True, True, True, False)
            step(nt, False, True, True, False)
            step(nt + 1, False, False, True, False)

        @block.gpsimd
        def _(pool):
            nc.gpsimd.memset(mhalf[:], -0.5).then_inc(S["reset"], 1)
            nc.gpsimd.memset(euler[:], float(np.e)).then_inc(S["reset"], 1)
            nc.gpsimd.memset(cs[:], 0.0).then_inc(S["reset"], 1)
            nc.gpsimd.memset(cs_sum[:], 0.0).then_inc(S["cs_added"], 1)
            nc.gpsimd.memset(state[:], 0.0).then_inc(S["s_added"], 1)
            pool.wait_ge(S["reset"], 4)
            pool.wait_ge(S["cs_added"], 1)
            pool.wait_ge(S["s_added"], 1)
            pool.wait_ge(S["in_const"], NCONST)

            def rstd_(tag, i, t):
                pool.wait_ge(S["ve_" + tag], t + 1)
                nc.gpsimd.tensor_tensor(rstd[:, i], ve[:, i], mhalf[:], ALU.pow).then_inc(S["rstd_" + tag], 1)

            def step(t, middle, back, more):
                v, u = t - 1, t - 2
                if back:
                    pool.wait_ge(S["comp_done"], u + 1)
                    pool.wait_ge(S["s_ps"], u)
                    pool.wait_ge(S["v_kept"], u + 1)
                    nc.gpsimd.tensor_tensor(vs[:].rearrange("p b (h d) -> p (b h) d", d=FD), vb[:, u % 2].rearrange("p b (h d) -> p (b h) d", d=FD),
                                            comp[:].rearrange("p b (h o) -> p (b h) o", o=1).broadcast_to((P, B * FH, FD)), ALU.mult).then_inc(S["vs_done"], 1)
                    nc.gpsimd.tensor_tensor(x[:, :, u, :], x[:, :, u, :], bo[:].rearrange("p (o d) -> p o d", o=1).broadcast_to((P, B, D)),
                                            ALU.add).then_inc(S["bo_added"], 1)
                if more:
                    rstd_("in", 0, t + 1)
                if middle:
                    pool.wait_ge(S["cons_done"], v + 1)
                    pool.wait_ge(S["cs_cum"], v)
                    pool.wait_ge(S["comp_done"], v)
                    nc.gpsimd.tensor_tensor(cs_sum[:], cs_sum[:], cs[:], ALU.add).then_inc(S["cs_added"], 1)
                    pool.wait_ge(S["cs_added"], v + 2)
                    nc.gpsimd.tensor_tensor(cs[:].rearrange("p b h -> p (b h)"), euler[:], cons[:, 1].rearrange("p b h -> p (b h)"), ALU.pow).then_inc(S["cs_done"], 1)
                if back:
                    pool.wait_ge(S["s_masked"], u + 1)
                    pool.wait_ge(S["o_ps"], 2 * u + 2)
                    nc.gpsimd.tensor_tensor(state[:], state[:], s_new[:], ALU.add).then_inc(S["s_added"], 1)
                    rstd_("x1", 1, u)

            rstd_("in", 0, 0)
            step(0, False, False, True)
            step(1, True, False, True)
            with pool.Fori(2, nt - 1) as t:
                step(t, True, True, True)
            step(nt - 1, True, True, False)
            step(nt, True, True, False)
            step(nt + 1, False, True, False)


def layers_block(nc, x, nt, depth, w):
    with ExitStack() as ctx:
        def sb(name, shape, dt=F32):
            return ctx.enter_context(nc.sbuf_tensor(name, shape, dt))

        def sem(name):
            return ctx.enter_context(nc.semaphore(name))

        psum = ctx.enter_context(nc.psum_tensor("psum", [P, 8, 512], F32))
        sc_ps = psum[:, 0:4, :]

        wqkv = sb("wqkv", [P, 2, DC, 3 * INNER], F32R)
        w1 = sb("w1", [P, 2, DC, 2 * HID], F32R)
        raw = sb("raw", [P, DC, 3 * INNER])
        wo = sb("wo", [P, INNER // P, D])
        w2 = sb("w2", [P, NF, D])
        b1 = sb("b1", [P, 2, NF])
        b2 = sb("b2", [P, D])
        lng = sb("lng", [P, DC])
        lnb = sb("lnb", [P, DC])
        qks = sb("qks", [P, 4, DH])
        tab = sb("tab", [P, nt, 4, DH])
        mask = sb("mask", [P, 3, 512], BF16)
        ident = sb("ident", [P, P])
        ident_bf = sb("ident_bf", [P, P], BF16)

        xst = sb("xst", [P, B, D])
        hT = sb("hT", [P, B, 2, DC, P + 2], F32R)
        t1 = sb("t1", [P, B, 2 * INNER])
        t2 = sb("t2", [P, B, 2 * INNER])
        sq = sb("sq", [P, 2 * INNER])
        ss = sb("ss", [P, B, 2 * HEADS])
        rn = sb("rn", [P, B, 2 * HEADS])
        zeros = sb("zeros", [P, D])
        mhalf = sb("mhalf", [P, 2 * HEADS])
        qT = sb("qT", [P, HEADS // 2, P])
        kT = sb("kT", [P, B, HEADS // 2, 2, P])
        v = sb("v", [P, B, 2, INNER])
        nmax = sb("nmax", [P, HEADS])
        psm = sb("psm", [P, HEADS])
        rsm = sb("rsm", [P, HEADS])
        probs = sb("probs", [P, HEADS, 2, P])
        probsT = sb("probsT", [P, 4, 512])
        o = sb("o", [P, INNER])
        oT = sb("oT", [P, INNER // P, P])
        hs = sb("hs", [P, B, P])
        lastrow = sb("lastrow", [1, B, P])
        stats = sb("stats", [P, B, 12])
        mv = sb("mv", [P, B, 2])
        ve = sb("ve", [P, B])
        rstd = sb("rstd", [P, B])
        hn = sb("hn", [P, B, D])
        h2T = sb("h2T", [P, 2, DC, B * P], F32R)
        gate = sb("gate", [P, 2, B * P])
        hid = sb("hid", [P, NF, B * P])

        in_const = sem("in_const")
        in_wqkv = sem("in_wqkv")
        in_w1 = sem("in_w1")
        in_small = sem("in_small")
        in_tab = sem("in_tab")
        const_ready = sem("const_ready")
        half_ready = sem("half_ready")
        wqkv_ready = sem("wqkv_ready")
        wqkv_high = sem("wqkv_high")
        w1_ready = sem("w1_ready")
        w1_high = sem("w1_high")
        w1_bias_mm = sem("w1_bias_mm")
        b1_ready = sem("b1_ready")
        tab_ready = sem("tab_ready")
        state_reset = sem("state_reset")
        layer_done = sem("layer_done")
        x_staged = sem("x_staged")
        xT_ps = sem("xT_ps")
        col_carried = sem("col_carried")
        hT_high = sem("hT_high")
        hT_low = sem("hT_low")
        qk_ps = sem("qk_ps")
        v_ps = sem("v_ps")
        v_kept = sem("v_kept")
        squares = sem("squares")
        rot_parts = sem("rot_parts")
        sumsq = sem("sumsq")
        sumsq_raw = sem("sumsq_raw")
        rnorm = sem("rnorm")
        rot_sum = sem("rot_sum")
        qk_final = sem("qk_final")
        qkT_ps = sem("qkT_ps")
        qT_kept = sem("qT_kept")
        kT_kept = sem("kT_kept")
        scores_ps = sem("scores_ps")
        max_found = sem("max_found")
        exp_done = sem("exp_done")
        pT_ps = sem("pT_ps")
        pT_act = sem("pT_act")
        pT_dve = sem("pT_dve")
        o_ps = sem("o_ps")
        rsum = sem("rsum")
        o_kept = sem("o_kept")
        oT_ps = sem("oT_ps")
        oT_kept = sem("oT_kept")
        wo_ps = sem("wo_ps")
        x_attn = sem("x_attn")
        row_copied = sem("row_copied")
        in_row = [sem(f"in_row{b}") for b in range(B)]
        in_hs = [sem(f"in_hs{b}") for b in range(B)]
        stats_done = sem("stats_done")
        mv_done = sem("mv_done")
        ve_done = sem("ve_done")
        rstd_done = sem("rstd_done")
        hn_done = sem("hn_done")
        b2_added = sem("b2_added")
        h2T_ps = sem("h2T_ps")
        h2T_high = sem("h2T_high")
        h2T_low = sem("h2T_low")
        up_ps = sem("up_ps")
        gelu_done = sem("gelu_done")
        hid_done = sem("hid_done")
        down_ps = sem("down_ps")
        x_ffn = sem("x_ffn")
        out_sent = sem("out_sent")

        def plain(eng):
            eng.wait_ge(in_const, 32)

        def place(h):
            return (h // 4) * 4 + (h % 2) * 2 + (h // 2) % 2

        def done(l, t, b):
            return l * (B * nt) + t * B + b + 1

        def fdone(l, t):
            return l * nt + t + 1

        def rdone(l, t, r):
            return (l * nt + t) * NF + r + 1

        NSMALL = 10
        HEAD_AT = sorted(range(HEADS), key=place)
        UP_BANK = [5, 4, 6, 5, 4, 6]

        def run(eng, start, step, ffn_tail, end=None):
            with eng.Fori(0, depth) as l:
                start(l)
                step(l, 0, True, False)
                with eng.Fori(1, nt - 1) as t:
                    step(l, t, False, False)
                step(l, nt - 1, False, True)
                ffn_tail(l, nt - 1)
                if end is not None:
                    end(l)

        block = ctx.enter_context(nc.Block())

        @block.sync
        def _(sp):
            sp.dma_start(ident[:], w["ident"]).then_inc(in_const, 16)
            sp.dma_start(probs[:].rearrange("p h s j -> p (h s j)")[:, 0:1536], w["masks"]).then_inc(in_const, 16)

            def load_wqkv(l):
                sp.dma_start(raw[:], w["wqkv"][bass.ds(l, 1)].rearrange("a (c p) n -> p (a c) n", p=P)).then_inc(in_wqkv, 16)

            def load_tab(l):
                sp.dma_start(tab[:], w["tables"].rearrange("(t p) k d -> p t k d", p=P)).then_inc(in_tab, 16)
                for n, s in ((0, "q_scale"), (1, "k_scale")):
                    row = w[s][bass.ds(l, 1)]
                    sp.dma_start(qks[:, n], row.partition_broadcast(P)).then_inc(in_tab, 16)
                    sp.dma_start(qks[:, 2 + n, 0:HALF], row[:, HALF:DH].partition_broadcast(P)).then_inc(in_tab, 16)
                    sp.dma_start(qks[:, 2 + n, HALF:DH], row[:, 0:HALF].partition_broadcast(P)).then_inc(in_tab, 16)

            load_wqkv(0)
            load_tab(0)

            def start(l):
                plain(sp)
                sp.wait_ge(wqkv_ready, l + 1)
                sp.dma_start(raw[:, :, 0:2 * HID], w["w1"][bass.ds(l, 1)].rearrange("a (c p) n -> p (a c) n", p=P)).then_inc(in_w1, 16)
                plain(sp)
                sp.wait_ge(layer_done, l)
                sp.dma_start(b2[:], w["b2"][bass.ds(l, 1)].partition_broadcast(P)).then_inc(in_small, 16)
                sp.dma_start(lng[:], w["ln_g"][bass.ds(l, 1)].rearrange("a (c p) -> p (a c)", p=P), allow_slow_non_contiguous=True).then_inc(in_small, 16)
                sp.dma_start(lnb[:], w["ln_b"][bass.ds(l, 1)].rearrange("a (c p) -> p (a c)", p=P), allow_slow_non_contiguous=True).then_inc(in_small, 16)
                for g in range(2):
                    row = w["b1"][bass.ds(l, 1), g * HID:(g + 1) * HID]
                    sp.dma_start(b1[0:FS, g, 0:NF - 1], row[:, 0:(NF - 1) * FS].rearrange("a (f p) -> p (a f)", p=FS), allow_slow_non_contiguous=True).then_inc(in_small, 16)
                    sp.dma_start(b1[0:FLAST, g, NF - 1:NF], row[:, (NF - 1) * FS:HID].rearrange("a (f p) -> p (a f)", p=FLAST), allow_slow_non_contiguous=True).then_inc(in_small, 16)
                sp.dma_start(wo[:], w["wo"][bass.ds(l, 1)].rearrange("a (c p) n -> p (a c) n", p=P)).then_inc(in_small, 16)
                sp.dma_start(w2[0:FS, 0:NF - 1, :], w["w2"][bass.ds(l, 1), 0:(NF - 1) * FS].rearrange("a (f p) n -> p (a f) n", p=FS)).then_inc(in_small, 16)
                sp.dma_start(w2[0:FLAST, NF - 1, :], w["w2"][bass.ds(l, 1), (NF - 1) * FS:HID].rearrange("a p n -> (a p) n")).then_inc(in_small, 16)

            def shift(l, t, b):
                n = done(l, t, b)
                n = n if isinstance(n, int) else sp.snap(n)
                plain(sp)
                sp.wait_ge(x_attn, n)
                sp.wait_ge(row_copied, n)
                sp.dma_start(lastrow[0:1, b], x[P - 1:P, b, t, P:D]).then_inc(in_row[b], 16)
                sp.dma_start(hs[1:P, b], x[0:P - 1, b, t, P:D]).then_inc(in_hs[b], 16)

            def step(l, t, first, last):
                if first:
                    plain(sp)
                    sp.wait_ge(w1_ready, l + 1)
                    sp.wait_ge(w1_bias_mm, l + 1)
                    load_wqkv((l + 1) % depth)
                shift(l, t, 0)
                if last:
                    plain(sp)
                    sp.wait_ge(rot_parts, done(l, t, 1))
                    load_tab((l + 1) % depth)
                shift(l, t, 1)

            run(sp, start, step, lambda l, t: None)
            sp.wait_ge(in_wqkv, 16 * (depth + 1))
            sp.wait_ge(in_tab, 16 * 7 * (depth + 1))

        @block.tensor
        def _(pe):
            def transposed_x(l, t, b, bank):
                pe.wait_ge(x_staged, done(l, t, b))
                for c in range(DC):
                    mm = nc.tensor.transpose(psum[:, bank, c * P:(c + 1) * P], xst[:, b, c * P:(c + 1) * P], ident[:])
                mm.then_inc(xT_ps, 1)

            def project(b, j, bank):
                n = 0
                for c in range(DC):
                    for a, m in ((0, 0), (0, 1), (1, 0)):
                        mm = nc.tensor.matmul(psum[:, bank, :], hT[:, b, a, c, 1 - c:1 - c + P],
                                              wqkv[:, m, c, j * INNER:(j + 1) * INNER], start=(n == 0), stop=(n == 5))
                        n += 1
                return mm

            def qk(l, t, b, bank):
                pe.wait_ge(hT_low, done(l, t, b))
                project(b, 0, bank)
                project(b, 1, bank + 1).then_inc(qk_ps, 1)

            def vproj(l, t, b, bank):
                project(b, 2, bank).then_inc(v_ps, 1)

            def qkT(l, t, b, bank):
                pe.wait_ge(qk_final, done(l, t, b))
                for n in range(HEADS):
                    mm = nc.tensor.transpose(psum[:, bank + n // 4, (n % 4) * P:(n % 4 + 1) * P], t1[:, b, n * P:(n + 1) * P], ident[:])
                mm.then_inc(qkT_ps, 1)

            def scores(l, t, b, kind):
                pe.wait_ge(qT_kept, done(l, t, b))
                pe.wait_ge(kT_kept, done(l, t, b))
                for half in range(2):
                    for k in range(2):
                        nc.tensor.matmul(psum[:, 2 * half + k, :], ident_bf[:], mask[:, kind, :], start=True, stop=True)
                    for h in range(4 * half, 4 * half + 4):
                        r = (h % 2) * DH
                        n = place(h)
                        mm = nc.tensor.matmul(psum[:, n // 2, (n % 2) * 256:(n % 2 + 1) * 256], qT[r:r + DH, h // 2, :],
                                              kT[r:r + DH, b, h // 2], start=False, stop=True, skip_group_check=True)
                    mm.then_inc(scores_ps, 1)

            def probsT_(l, t, b):
                pe.wait_ge(exp_done, 2 * done(l, t, b) - 1)
                for n in range(2 * HEADS):
                    if n == 8:
                        pe.wait_ge(exp_done, 2 * done(l, t, b))
                    mm = nc.tensor.transpose(psum[:, n // 4, (n % 4) * P:(n % 4 + 1) * P], probs[:, n // 2, n % 2, :], ident[:])
                    if n == 7:
                        mm.then_inc(pT_ps, 1)
                mm.then_inc(pT_ps, 1)

            def values(l, t, b, bank):
                pe.wait_ge(pT_act, done(l, t, b))
                pe.wait_ge(pT_dve, done(l, t, b))
                pe.wait_ge(v_kept, done(l, t, b))
                for h in range(HEADS):
                    for s in range(2):
                        n = 2 * place(h) + s
                        mm = nc.tensor.matmul(psum[:, bank, h * DH:(h + 1) * DH], probsT[:, n // 4, (n % 4) * P:(n % 4 + 1) * P],
                                              v[:, b, s, h * DH:(h + 1) * DH], start=(s == 0), stop=(s == 1))
                mm.then_inc(o_ps, 1)

            def transposed_o(l, t, b, bank):
                pe.wait_ge(o_kept, done(l, t, b))
                for c in range(INNER // P):
                    mm = nc.tensor.transpose(psum[:, bank, c * P:(c + 1) * P], o[:, c * P:(c + 1) * P], ident[:])
                mm.then_inc(oT_ps, 1)

            def out_proj(l, t, b, bank):
                pe.wait_ge(oT_kept, done(l, t, b))
                for c in range(INNER // P):
                    mm = nc.tensor.matmul(psum[:, bank, 0:D], oT[:, c, :], wo[:, c, :], start=(c == 0), stop=(c == INNER // P - 1))
                mm.then_inc(wo_ps, 1)

            def transposed_h(l, t):
                pe.wait_ge(hn_done, done(l, t, 1))
                for c in range(DC):
                    for b in range(B):
                        mm = nc.tensor.transpose(psum[:, 4, (c * B + b) * P:(c * B + b + 1) * P], hn[:, b, c * P:(c + 1) * P], ident[:])
                mm.then_inc(h2T_ps, 1)

            def up(l, t, r):
                n = FC[r]
                for g in range(2):
                    k = 0
                    for c in range(DC):
                        for m, a in ((0, 0), (0, 1), (1, 0)):
                            f0 = g * HID + r * FS
                            mm = nc.tensor.matmul(psum[0:n, UP_BANK[r], g * 256:(g + 1) * 256], w1[:, m, c, f0:f0 + n],
                                                  h2T[:, a, c, :], start=(k == 0), stop=(k == 5))
                            k += 1
                mm.then_inc(up_ps, 1)

            def down(l, t):
                pe.wait_ge(hid_done, rdone(l, t, NF - 1))
                for b in range(B):
                    for f in range(NF):
                        n = FC[f]
                        mm = nc.tensor.matmul(psum[:, 5, b * D:(b + 1) * D], hid[0:n, f, b * P:(b + 1) * P], w2[0:n, f, :],
                                              start=(f == 0), stop=(f == NF - 1))
                mm.then_inc(down_ps, 1)

            def start(l):
                pe.wait_ge(wqkv_ready, l + 1)
                pe.wait_ge(const_ready, 2)
                pe.wait_ge(layer_done, l)
                transposed_x(l, 0, 0, 4)
                qk(l, 0, 0, 0)
                vproj(l, 0, 0, 4)
                transposed_x(l, 0, 1, 5)
                qk(l, 0, 1, 6)
                vproj(l, 0, 1, 5)
                qkT(l, 0, 0, 0)

            def ups(l, t, rounds):
                for r in rounds:
                    if r >= 3:
                        pe.wait_ge(hid_done, rdone(l, t, r - 3))
                    up(l, t, r)

            def step(l, t, first, last):
                if not last:
                    if first:
                        pe.wait_ge(v_kept, done(l, t, 0))
                    transposed_x(l, t + 1, 0, 4)
                scores(l, t, 0, 2 if first else t % 2)
                if not last:
                    pe.wait_ge(hT_low, done(l, t + 1, 0))
                if first:
                    pe.wait_ge(v_kept, done(l, t, 1))
                else:
                    pe.wait_ge(x_attn, done(l, t - 1, 1))
                qkT(l, t, 1, 4)
                if not last:
                    qk(l, t + 1, 0, 6)
                pe.wait_ge(qT_kept, done(l, t, 1))
                pe.wait_ge(kT_kept, done(l, t, 1))
                if first:
                    pe.wait_ge(in_w1, 16 * (l + 1))
                    pe.wait_ge(in_small, 16 * NSMALL * (l + 1))
                    for g in range(2):
                        for f in range(NF):
                            for c in range(DC):
                                f0 = g * HID + f * FS
                                mm = nc.tensor.matmul(psum[0:FC[f], 4, g * NF + f:g * NF + f + 1], raw[:, c, f0:f0 + FC[f]],
                                                      lnb[:, c:c + 1], start=(c == 0), stop=(c == DC - 1))
                    mm.then_inc(w1_bias_mm, 1)
                else:
                    transposed_h(l, t - 1)
                    pe.wait_ge(h2T_low, fdone(l, t - 1))
                    ups(l, t - 1, (0, 1))
                probsT_(l, t, 0)
                if not last:
                    pe.wait_ge(rot_parts, done(l, t + 1, 0))
                    pe.wait_ge(squares, done(l, t + 1, 0))
                if not first:
                    ups(l, t - 1, (2,))
                values(l, t, 0, 7)
                if not first:
                    ups(l, t - 1, (3, 4, 5))
                scores(l, t, 1, 2 if first else t % 2)
                transposed_o(l, t, 0, 7)
                if not last:
                    if first:
                        pe.wait_ge(b1_ready, l + 1)
                    else:
                        pe.wait_ge(hid_done, rdone(l, t - 1, 4))
                    vproj(l, t + 1, 0, 4)
                out_proj(l, t, 0, 7)
                if not last:
                    if not first:
                        pe.wait_ge(hid_done, rdone(l, t - 1, 5))
                    transposed_x(l, t + 1, 1, 6)
                if not first:
                    down(l, t - 1)
                probsT_(l, t, 1)
                if not last:
                    pe.wait_ge(x_attn, done(l, t, 0))
                    qk(l, t + 1, 1, 6)
                    pe.wait_ge(v_kept, done(l, t + 1, 0))
                values(l, t, 1, 4)
                if not first:
                    pe.wait_ge(x_ffn, fdone(l, t - 1))
                if not last:
                    vproj(l, t + 1, 1, 5)
                    qkT(l, t + 1, 0, 0)
                transposed_o(l, t, 1, 4)
                if not last:
                    pe.wait_ge(v_kept, done(l, t + 1, 1))
                out_proj(l, t, 1, 5)

            def ffn_tail(l, t):
                pe.wait_ge(x_attn, done(l, t, 1))
                transposed_h(l, t)
                pe.wait_ge(h2T_low, fdone(l, t))
                ups(l, t, range(NF))
                down(l, t)

            run(pe, start, step, ffn_tail)

        @block.scalar
        def _(act):
            act.wait_ge(in_const, 32)
            nc.scalar.copy(ident_bf[:], ident[:]).then_inc(const_ready, 1)
            nc.scalar.copy(mask[:].rearrange("p k n -> p (k n)"), probs[:].rearrange("p h s j -> p (h s j)")[:, 0:1536]).then_inc(const_ready, 1)

            def high(l, t, b, bank):
                act.wait_ge(xT_ps, done(l, t, b))
                act.wait_ge(col_carried, done(l, t, b))
                nc.scalar.copy(hT[:, b, 0, :, 1:P + 1], psum[:, bank, 0:D].rearrange("p (c n) -> p c n", c=DC)).then_inc(hT_high, 1)

            def square(l, t, b, bank):
                act.wait_ge(qk_ps, done(l, t, b))
                if not (isinstance(t, int) and t == 0 and b == 0):
                    act.wait_ge(sumsq_raw, done(l, t, b) - 1)
                nc.scalar.activation(sq[:], psum[:, bank:bank + 2, :].rearrange("p a n -> p (a n)"), ACT.Square).then_inc(squares, 1)

            def keep_v(l, t, b, bank):
                act.wait_ge(v_ps, done(l, t, b))
                if not (isinstance(t, int) and t == 0):
                    act.wait_ge(o_ps, done(l, t - 1, b))
                nc.scalar.copy(v[:, b, t % 2, :], psum[:, bank, :]).then_inc(v_kept, 1)

            def keep_qT(l, t, b, bank):
                act.wait_ge(qkT_ps, done(l, t, b))
                nc.scalar.copy(qT[:].rearrange("p c n -> p (c n)"), psum[:, bank, :]).then_inc(qT_kept, 1)

            def exps(l, t, b, half):
                act.wait_ge(max_found, 2 * done(l, t, b) - 1 + half)
                if half == 0 and not (isinstance(t, int) and t == 0 and b == 0):
                    act.wait_ge(rsum, done(l, t, b) - 1)
                for n in range(4 * half, 4 * half + 4):
                    h = HEAD_AT[n]
                    a = nc.scalar.activation(probs[:, n].rearrange("p s j -> p (s j)"), psum[:, n // 2, (n % 2) * 256:(n % 2 + 1) * 256],
                                             ACT.Exp, bias=nmax[:, n:n + 1], scale=1.0, accum_out=psm[:, h:h + 1])
                a.then_inc(exp_done, 1)

            def keep_pT(l, t, b):
                act.wait_ge(pT_ps, 2 * done(l, t, b) - 1)
                nc.scalar.copy(probsT[:, 0:2].rearrange("p a n -> p (a n)"), psum[:, 0:2, :].rearrange("p a n -> p (a n)")).then_inc(pT_act, 1)

            def keep_oT(l, t, b, bank):
                act.wait_ge(oT_ps, done(l, t, b))
                nc.scalar.copy(oT[:].rearrange("p c n -> p (c n)"), psum[:, bank, :]).then_inc(oT_kept, 1)

            def high2(l, t):
                act.wait_ge(h2T_ps, fdone(l, t))
                nc.scalar.copy(h2T[:, 0].rearrange("p c n -> p (c n)"), psum[:, 4, :]).then_inc(h2T_high, 1)

            def gelu(l, t, r):
                act.wait_ge(up_ps, rdone(l, t, r))
                n = FC[r]
                if r >= 2:
                    act.wait_ge(hid_done, rdone(l, t, r - 2))
                nc.scalar.activation(gate[0:n, r % 2, :], psum[0:n, UP_BANK[r], 256:512], ACT.Gelu, bias=b1[0:n, 1, r:r + 1]).then_inc(gelu_done, 1)

            def start(l):
                act.wait_ge(state_reset, l + 1)
                high(l, 0, 0, 4)
                square(l, 0, 0, 0)
                keep_v(l, 0, 0, 4)
                high(l, 0, 1, 5)
                square(l, 0, 1, 6)
                keep_v(l, 0, 1, 5)
                keep_qT(l, 0, 0, 0)

            def split_wqkv(n):
                act.wait_ge(in_wqkv, 16 * n)
                nc.scalar.copy(wqkv[:, 0].rearrange("p c n -> p (c n)"), raw[:].rearrange("p c n -> p (c n)")).then_inc(wqkv_high, 1)

            def step(l, t, first, last):
                if not last:
                    high(l, t + 1, 0, 4)
                exps(l, t, 0, 0)
                keep_qT(l, t, 1, 4)
                exps(l, t, 0, 1)
                if not last:
                    square(l, t + 1, 0, 6)
                if first:
                    act.wait_ge(in_w1, 16 * (l + 1))
                    act.wait_ge(in_small, 16 * NSMALL * (l + 1))
                    for c in range(DC):
                        nc.scalar.activation(w1[:, 0, c, :], raw[:, c, 0:2 * HID], ACT.Copy, scale=lng[:, c:c + 1]).then_inc(w1_high, 1)
                else:
                    high2(l, t - 1)
                    gelu(l, t - 1, 0)
                    gelu(l, t - 1, 1)
                keep_pT(l, t, 0)
                if not first:
                    for r in range(2, NF):
                        gelu(l, t - 1, r)
                if last:
                    act.wait_ge(v_ps, done(l, t, 1))
                    split_wqkv(l + 2)
                exps(l, t, 1, 0)
                keep_oT(l, t, 0, 7)
                exps(l, t, 1, 1)
                if not last:
                    keep_v(l, t + 1, 0, 4)
                    high(l, t + 1, 1, 6)
                keep_pT(l, t, 1)
                if not last:
                    square(l, t + 1, 1, 6)
                    keep_v(l, t + 1, 1, 5)
                    keep_qT(l, t + 1, 0, 0)
                keep_oT(l, t, 1, 4)

            def ffn_tail(l, t):
                high2(l, t)
                for r in range(NF):
                    gelu(l, t, r)

            split_wqkv(1)
            run(act, start, step, ffn_tail)

        @block.vector
        def _(dve):
            def low(l, t, b, bank):
                dve.wait_ge(hT_high, done(l, t, b))
                nc.vector.tensor_tensor(hT[:, b, 1, :, 1:P + 1], psum[:, bank, 0:D].rearrange("p (c n) -> p c n", c=DC),
                                        hT[:, b, 0, :, 1:P + 1].bitcast(F32), ALU.subtract).then_inc(hT_low, 1)

            def rotate(l, t, b, bank):
                dve.wait_ge(squares, done(l, t, b))
                q = psum[:, bank:bank + 2, :].rearrange("p a (h d) -> p a h d", h=HEADS)
                o1 = t1[:, b].rearrange("p (a h d) -> p a h d", a=2, h=HEADS)
                o2 = t2[:, b].rearrange("p (a h d) -> p a h d", a=2, h=HEADS)
                ta = tab[:, t, 0:2].rearrange("p a (o d) -> p a o d", o=1).broadcast_to((P, 2, HEADS, DH))
                tb = tab[:, t, 2:4].rearrange("p a (o d) -> p a o d", o=1).broadcast_to((P, 2, HEADS, DH))
                nc.vector.tensor_tensor(o1, q, ta, ALU.mult)
                nc.vector.tensor_tensor(o2[:, :, :, 0:HALF], q[:, :, :, HALF:DH], tb[:, :, :, 0:HALF], ALU.mult)
                nc.vector.tensor_tensor(o2[:, :, :, HALF:DH], q[:, :, :, 0:HALF], tb[:, :, :, HALF:DH], ALU.mult).then_inc(rot_parts, 1)

            def sum_squares(l, t, b):
                dve.wait_ge(squares, done(l, t, b))
                nc.vector.tensor_reduce(ss[:, b], sq[:].rearrange("p (h d) -> p h d", d=DH), AX.X, ALU.add).then_inc(sumsq_raw, 1)
                dve.wait_ge(sumsq_raw, done(l, t, b))
                nc.vector.tensor_scalar(ss[:, b], ss[:, b], 1e-24, None, ALU.max).then_inc(sumsq, 1)

            def scale_qk(l, t, b):
                dve.wait_ge(rot_parts, done(l, t, b))
                nc.vector.tensor_tensor(t1[:, b], t1[:, b], t2[:, b], ALU.add).then_inc(rot_sum, 1)
                dve.wait_ge(rnorm, done(l, t, b))
                dve.wait_ge(rot_sum, done(l, t, b))
                v1 = t1[:, b].rearrange("p (h d) -> p h d", d=DH)
                rb = rn[:, b].rearrange("p (h o) -> p h o", o=1).broadcast_to((P, 2 * HEADS, DH))
                nc.vector.tensor_tensor(v1, v1, rb, ALU.mult).then_inc(qk_final, 1)

            def keep_kT(l, t, b, bank):
                dve.wait_ge(qkT_ps, done(l, t, b))
                nc.vector.tensor_copy(kT[:, b, :, t % 2, :], psum[:, bank, :].rearrange("p (c n) -> p c n", n=P)).then_inc(kT_kept, 1)

            def maxima(l, t, b, half):
                dve.wait_ge(scores_ps, 2 * done(l, t, b) - 1 + half)
                nc.vector.tensor_reduce(nmax[:, 4 * half:4 * half + 4], sc_ps[:, 2 * half:2 * half + 2].rearrange("p k (h j) -> p (k h) j", h=2),
                                        AX.X, ALU.max, negate=True).then_inc(max_found, 1)

            def keep_pT(l, t, b):
                dve.wait_ge(pT_ps, 2 * done(l, t, b))
                nc.vector.tensor_copy(probsT[:, 2:4].rearrange("p a n -> p (a n)"), psum[:, 2:4, :].rearrange("p a n -> p (a n)")).then_inc(pT_dve, 1)

            def normalise_o(l, t, b, bank):
                dve.wait_ge(exp_done, 2 * done(l, t, b))
                nc.vector.reciprocal(rsm[:], psm[:]).then_inc(rsum, 1)
                dve.wait_ge(rsum, done(l, t, b))
                dve.wait_ge(o_ps, done(l, t, b))
                rb = rsm[:].rearrange("p (h o) -> p h o", o=1).broadcast_to((P, HEADS, DH))
                nc.vector.tensor_tensor(o[:].rearrange("p (h d) -> p h d", d=DH), psum[:, bank, :].rearrange("p (h d) -> p h d", d=DH), rb,
                                        ALU.mult).then_inc(o_kept, 1)

            def add_attn(l, t, b, bank):
                dve.wait_ge(wo_ps, done(l, t, b))
                nc.vector.tensor_tensor(x[:, b, t, :], psum[:, bank, 0:D], x[:, b, t, :], ALU.add).then_inc(x_attn, 1)

            def ln_stats(l, t, b):
                plain(dve)
                dve.wait_ge(x_attn, done(l, t, b))
                nc.vector.bn_stats(stats[:, b, 0:6], x[:, b, t, 0:P])
                dve.wait_ge(in_hs[b], 16 * fdone(l, t))
                dve.wait_ge(row_copied, done(l, t, b))
                nc.vector.bn_stats(stats[:, b, 6:12], hs[:, b]).then_inc(stats_done, 1)
                plain(dve)
                dve.wait_ge(stats_done, done(l, t, b))
                nc.vector.bn_aggr(mv[:, b], stats[:, b]).then_inc(mv_done, 1)
                dve.wait_ge(mv_done, done(l, t, b))
                nc.vector.tensor_scalar(ve[:, b:b + 1], mv[:, b, 1:2], LN_EPS, None, ALU.add).then_inc(ve_done, 1)

            def ln_apply(l, t, b):
                dve.wait_ge(rstd_done, done(l, t, b))
                nc.vector.tensor_scalar(hn[:, b, 0:P], x[:, b, t, 0:P], mv[:, b, 0:1], rstd[:, b:b + 1], ALU.subtract, ALU.mult)
                nc.vector.tensor_scalar(hn[:, b, P:D], hs[:, b], mv[:, b, 0:1], rstd[:, b:b + 1], ALU.subtract, ALU.mult).then_inc(hn_done, 1)

            def low2(l, t):
                dve.wait_ge(h2T_high, fdone(l, t))
                nc.vector.tensor_tensor(h2T[:, 1].rearrange("p c n -> p (c n)"), psum[:, 4, :],
                                        h2T[:, 0].rearrange("p c n -> p (c n)").bitcast(F32), ALU.subtract).then_inc(h2T_low, 1)

            def gated(l, t, r):
                dve.wait_ge(gelu_done, rdone(l, t, r))
                n = FC[r]
                nc.vector.scalar_tensor_tensor(hid[0:n, r, :], psum[0:n, UP_BANK[r], 0:256], b1[0:n, 0, r:r + 1], gate[0:n, r % 2, :],
                                               ALU.add, ALU.mult).then_inc(hid_done, 1)

            def add_ffn(l, t):
                dve.wait_ge(down_ps, fdone(l, t))
                dve.wait_ge(b2_added, done(l, t, 1))
                nc.vector.tensor_tensor(x[:, :, t, :], psum[:, 5, :].rearrange("p (b d) -> p b d", b=B), x[:, :, t, :], ALU.add).then_inc(x_ffn, 1)

            def split_wqkv(n):
                dve.wait_ge(wqkv_high, n)
                nc.vector.tensor_tensor(wqkv[:, 1].rearrange("p c n -> p (c n)"), raw[:].rearrange("p c n -> p (c n)"),
                                        wqkv[:, 0].rearrange("p c n -> p (c n)").bitcast(F32), ALU.subtract).then_inc(wqkv_ready, 1)

            def scale_tables(n):
                dve.wait_ge(in_tab, 16 * 7 * n)
                for k in range(4):
                    tb = tab[:, :, k, :]
                    nc.vector.tensor_tensor(tb, tb, qks[:, k:k + 1, :].broadcast_to((P, nt, DH)), ALU.mult).then_inc(tab_ready, 1)

            split_wqkv(1)
            scale_tables(1)

            def start(l):
                dve.wait_ge(tab_ready, 4 * (l + 1))
                low(l, 0, 0, 4)
                sum_squares(l, 0, 0)
                rotate(l, 0, 0, 0)
                low(l, 0, 1, 5)
                scale_qk(l, 0, 0)
                sum_squares(l, 0, 1)
                rotate(l, 0, 1, 6)
                keep_kT(l, 0, 0, 1)
                scale_qk(l, 0, 1)

            def step(l, t, first, last):
                if not last:
                    low(l, t + 1, 0, 4)
                maxima(l, t, 0, 0)
                maxima(l, t, 0, 1)
                keep_kT(l, t, 1, 5)
                if not first:
                    ln_stats(l, t - 1, 1)
                    ln_apply(l, t - 1, 1)
                if not last:
                    sum_squares(l, t + 1, 0)
                if first:
                    dve.wait_ge(w1_high, DC * (l + 1))
                    for c in range(DC):
                        a = nc.vector.scalar_tensor_tensor(w1[:, 1, c, :], raw[:, c, 0:2 * HID], lng[:, c:c + 1], w1[:, 0, c, :].bitcast(F32),
                                                           ALU.mult, ALU.subtract)
                    a.then_inc(w1_ready, 1)
                    dve.wait_ge(w1_bias_mm, l + 1)
                    b1v = b1[:].rearrange("p g f -> p (g f)")
                    for g in range(2):
                        nc.vector.tensor_tensor(b1[0:FS, g, 0:NF - 1], psum[0:FS, 4, g * NF:g * NF + NF - 1], b1[0:FS, g, 0:NF - 1], ALU.add)
                        a = nc.vector.tensor_tensor(b1[0:FLAST, g, NF - 1:NF], psum[0:FLAST, 4, g * NF + NF - 1:g * NF + NF],
                                                    b1[0:FLAST, g, NF - 1:NF], ALU.add)
                    a.then_inc(b1_ready, 1)
                else:
                    low2(l, t - 1)
                if not last:
                    rotate(l, t + 1, 0, 6)
                if not first:
                    gated(l, t - 1, 0)
                keep_pT(l, t, 0)
                if not first:
                    gated(l, t - 1, 1)
                    gated(l, t - 1, 2)
                normalise_o(l, t, 0, 7)
                if not last:
                    scale_qk(l, t + 1, 0)
                if not first:
                    for r in range(3, NF):
                        gated(l, t - 1, r)
                maxima(l, t, 1, 0)
                maxima(l, t, 1, 1)
                add_attn(l, t, 0, 7)
                if not last:
                    low(l, t + 1, 1, 6)
                keep_pT(l, t, 1)
                if not first:
                    add_ffn(l, t - 1)
                ln_stats(l, t, 0)
                normalise_o(l, t, 1, 4)
                if not last:
                    sum_squares(l, t + 1, 1)
                ln_apply(l, t, 0)
                if not last:
                    rotate(l, t + 1, 1, 6)
                    keep_kT(l, t + 1, 0, 1)
                if last:
                    split_wqkv(l + 2)
                add_attn(l, t, 1, 5)
                if not last:
                    scale_qk(l, t + 1, 1)

            def ffn_tail(l, t):
                scale_tables(l + 2)
                ln_stats(l, t, 1)
                ln_apply(l, t, 1)
                low2(l, t)
                for r in range(NF):
                    gated(l, t, r)
                add_ffn(l, t)
                dve.wait_ge(x_ffn, fdone(l, t))
                nc.vector.memset(rsm[:], 0.0).then_inc(layer_done, 1)

            run(dve, start, step, ffn_tail)

        @block.gpsimd
        def _(pool):
            nc.gpsimd.memset(mhalf[:], -0.5).then_inc(half_ready, 1)
            nc.gpsimd.memset(zeros[:], 0.0).then_inc(half_ready, 1)
            pool.wait_ge(half_ready, 2)

            def stage(l, t, b, first):
                if not first:
                    pool.wait_ge(xT_ps, done(l, t - 1, b))
                nc.gpsimd.tensor_tensor(xst[:, b], x[:, b, t, :], zeros[:], ALU.add).then_inc(x_staged, 1)
                if not first:
                    pool.wait_ge(v_ps, done(l, t - 1, b))
                    pool.wait_ge(hT_low, done(l, t - 1, b))
                nc.gpsimd.tensor_tensor(hT[:, b, :, 1, 0:1], hT[:, b, :, 1, P:P + 1].bitcast(F32),
                                        zeros[:, 0:2].rearrange("p (a o) -> p a o", o=1), ALU.add).then_inc(col_carried, 1)

            def qk_norm(l, t, b):
                pool.wait_ge(sumsq, done(l, t, b))
                nc.gpsimd.tensor_tensor(rn[:, b], ss[:, b], mhalf[:], ALU.pow).then_inc(rnorm, 1)

            def row(l, t, b, first):
                if not first:
                    pool.wait_ge(hn_done, done(l, t - 1, b))
                    pool.wait_ge(in_row[b], 16 * fdone(l, t - 1))
                nc.gpsimd.tensor_tensor(hs[0:1, b], lastrow[0:1, b], zeros[0:1, 0:P], ALU.add).then_inc(row_copied, 1)

            def ln_rstd(l, t, b):
                pool.wait_ge(ve_done, done(l, t, b))
                nc.gpsimd.tensor_tensor(rstd[:, b:b + 1], ve[:, b:b + 1], mhalf[:, 0:1], ALU.pow).then_inc(rstd_done, 1)

            def add_b2(l, t, b):
                pool.wait_ge(hn_done, done(l, t, b))
                pool.wait_ge(in_row[b], 16 * fdone(l, t))
                nc.gpsimd.tensor_tensor(x[:, b, t, :], x[:, b, t, :], b2[:], ALU.add).then_inc(b2_added, 1)

            def start(l):
                plain(pool)
                pool.wait_ge(layer_done, l)
                nc.gpsimd.memset(hT[:, :, :, 1, P:P + 1].bitcast(F32), 0.0)
                nc.gpsimd.memset(lastrow[:], 0.0)
                nc.gpsimd.memset(kT[:, :, :, 1, :], 0.0)
                nc.gpsimd.memset(v[:, :, 1, :], 0.0).then_inc(state_reset, 1)
                pool.wait_ge(state_reset, l + 1)
                stage(l, 0, 0, True)
                stage(l, 0, 1, True)
                qk_norm(l, 0, 0)

            def step(l, t, first, last):
                if not last:
                    stage(l, t + 1, 0, False)
                qk_norm(l, t, 1)
                if not first:
                    ln_rstd(l, t - 1, 1)
                row(l, t, 0, first)
                row(l, t, 1, first)
                if not last:
                    qk_norm(l, t + 1, 0)
                if not first:
                    add_b2(l, t - 1, 1)
                if not last:
                    stage(l, t + 1, 1, False)
                ln_rstd(l, t, 0)
                add_b2(l, t, 0)

            def ffn_tail(l, t):
                ln_rstd(l, t, 1)
                add_b2(l, t, 1)

            run(pool, start, step, ffn_tail)


def sum_block(nc, x, nt, x1_dram, out_dram):
    with ExitStack() as ctx:
        step = 2
        pieces = [(b, t) for t in range(0, nt, step) for b in range(B)]
        x1 = ctx.enter_context(nc.sbuf_tensor("s_x1", [P, B, nt, D], F32))
        loaded = [ctx.enter_context(nc.semaphore(f"s_loaded{i}")) for i in range(len(pieces))]
        summed = ctx.enter_context(nc.semaphore("s_summed"))
        stored = ctx.enter_context(nc.semaphore("s_stored"))
        block = ctx.enter_context(nc.Block())

        def rows(dram, b, t):
            return dram[b, t * P:(t + step) * P].rearrange("(t p) d -> p t d", p=P)

        @block.sync
        def _(sp):
            for i, (b, t) in enumerate(pieces):
                sp.dma_start(x1[:, b, t:t + step], rows(x1_dram, b, t)).then_inc(loaded[i], 16)

        @block.vector
        def _(dve):
            for i, (b, t) in enumerate(pieces):
                dve.wait_ge(loaded[i], 16)
                xs = x[:, b, t:t + step]
                nc.vector.tensor_tensor(xs, xs, x1[:, b, t:t + step], ALU.add).then_inc(summed, 1)

        @block.scalar
        def _(act):
            for i, (b, t) in enumerate(pieces):
                act.wait_ge(summed, i + 1)
                act.dma_start(rows(out_dram, b, t), x[:, b, t:t + step]).then_inc(stored, 16)
            act.wait_ge(stored, 16 * len(pieces))


def build_program(nc, ins, out):
    _, n, _ = ins["x"].shape
    nt = n // P
    depth = ins["wqkv"].shape[0]
    x1_dram = nc.dram_tensor("x1_scratch", (B, n, D), F32).ap()
    with ExitStack() as ctx:
        x = ctx.enter_context(nc.sbuf_tensor("x", [P, B, nt, D], F32))
        flow_block(nc, x, nt, ins, ins["x"], x1_dram)
        layers_block(nc, x, nt, depth, ins)
        sum_block(nc, x, nt, x1_dram, out)


_ATTN = ["x", "Wq", "bq", "Wk", "bk", "Wv", "bv", "Wo", "bo"]
_FFN = ["wqkv", "q_scale", "k_scale", "wo", "ln_g", "ln_b", "w1", "b1", "w2", "b2"]


def kernel(**inputs):
    import concourse.bacc as bacc
    from concourse.bass_utils import run_bass_kernel_spmd

    arrays = {n: np.ascontiguousarray(inputs["L0_attn_" + n]) for n in _ATTN}
    arrays |= {n: np.ascontiguousarray(inputs["L0_ffn_" + n]) for n in _FFN}
    n = arrays["x"].shape[1]
    arrays |= {
        "ident": np.eye(P, dtype=np.float32),
        "tables": position_tables(n),
        "masks": window_masks(),
        "flow_masks": flow_masks(),
        "head_spread": head_spread(),
        "counts": counts(n // P),
    }
    nc = bacc.Bacc("TRN2", target_bir_lowering=False, num_devices=1)
    ins = {k: nc.dram_tensor(f"in_{k}", a.shape, mybir.dt.from_np(a.dtype), kind="ExternalInput").ap() for k, a in arrays.items()}
    out = nc.dram_tensor("out", arrays["x"].shape, F32, kind="ExternalOutput").ap()
    build_program(nc, ins, out)
    r = run_bass_kernel_spmd(nc, [{f"in_{k}": a for k, a in arrays.items()}], core_ids=[0])
    return r.results[0]["out"]
```

```python
from contextlib import ExitStack

import concourse.bass as bass
import numpy as np
from concourse import mybir

F32 = mybir.dt.float32
F32R = mybir.dt.float32r
BF16 = mybir.dt.bfloat16
ALU = mybir.AluOpType
ACT = mybir.ActivationFunctionType
AX = mybir.AxisListType

P = 128
D = 256
DC = D // P
B = 2
HEADS = 8
DH = 64
INNER = HEADS * DH
HALF = DH // 2
HID = int(D * 4 * 2 / 3)
NF = 6
FS = -(-HID // NF)
FLAST = HID - (NF - 1) * FS
FC = [FS] * (NF - 1) + [FLAST]
WINDOW = 128
QK_SCALE = 8.0
LN_EPS = 1e-5
FH = 16
FD = D // FH
FLOW_EPS = 1e-6
NEG = -3.0e38


def position_tables(n):
    f = np.float32
    half = np.arange(0, DH, 2, dtype=f)
    inv_freq = (f(1.0) / f(10000.0) ** (half / f(DH))).astype(f)
    t = np.arange(n, dtype=f)
    fr = t[:, None] * inv_freq[None, :]
    base = (half + f(0.4 * DH)) / f(1.4 * DH)
    power = (t - f(n // 2)) / f(WINDOW // 2)
    scale = base[None, :] ** power[:, None]
    cos, sin = np.cos(fr), np.sin(fr)
    out = np.empty((n, 4, 2, HALF), f)
    for kind, s in ((0, scale * f(QK_SCALE)), (1, f(1.0) / scale)):
        out[:, kind, 0] = out[:, kind, 1] = cos * s
        out[:, 2 + kind, 0] = -sin * s
        out[:, 2 + kind, 1] = sin * s
    return out.reshape(n, 4, DH)


def window_masks():
    i = np.arange(P)[:, None]
    j = np.arange(P)[None, :]
    own = np.where(j <= i, 0.0, NEG)
    front = np.where(j >= i, 0.0, NEG)
    none = np.full((P, P), NEG)
    one = np.stack([np.stack([own, front]), np.stack([front, own]), np.stack([own, none])])
    m = np.broadcast_to(one.transpose(2, 0, 1, 3)[:, :, None], (P, 3, 2, 2, P))
    return np.ascontiguousarray(m).astype(np.float32).reshape(P, -1)


def flow_masks():
    f = np.arange(P)
    tri = (f[:, None] <= f[None, :]).astype(np.float32)
    head_sum = (f[:, None] // FD == np.arange(P // FD)[None, :]).astype(np.float32)
    block = (f[:, None] // FD == f[None, :] // FD).astype(np.float32)
    odd = (f[:, None] // FD % 2).astype(np.float32)
    return np.concatenate([tri, head_sum, block, odd, np.ones((P, P), np.float32)], axis=1)


def head_spread():
    out = np.zeros((3 * FH, 3 * DC, P), np.float32)
    for a in range(3):
        for c in range(DC):
            for f in range(P):
                out[a * FH + c * (P // FD) + f // FD, a * DC + c, f] = 1
    return out


def counts(nt):
    n = (np.arange(nt)[None, :] * P + np.arange(P)[:, None] + 1).astype(np.float32)
    return np.stack([n, 1 / n], axis=1)


class Shared:

    def __init__(self, nc, ctx, nt, w):
        def sb(name, shape, dt=F32):
            return ctx.enter_context(nc.sbuf_tensor(name, shape, dt))

        self.nc, self.nt, self.w = nc, nt, w
        self.wqkv = sb("wqkv", [P, 2, DC, 3 * INNER], F32R)
        self.raw = sb("raw", [P, DC, 3 * INNER])
        self.tab = sb("tab", [P, nt, 4, DH])
        self.qks = sb("qks", [P, 4, DH])
        self.ident = sb("ident", [P, P])
        self.ident_bf = sb("ident_bf", [P, P], BF16)
        self.mask = sb("mask", [P, 3, 512], BF16)
        self.in_wqkv, self.in_tab, self.in_mask, self.mask_ready, self.wqkv_high, self.wqkv_ready, self.tab_ready = (
            ctx.enter_context(nc.semaphore(n))
            for n in ("in_wqkv", "in_tab", "in_mask", "mask_ready", "wqkv_high", "wqkv_ready", "tab_ready"))

    def load_mask(self, sp, place):
        sp.dma_start(place, self.w["masks"]).then_inc(self.in_mask, 16)

    def round_mask(self, act, place):
        act.wait_ge(self.in_mask, 16)
        self.nc.scalar.copy(self.ident_bf[:], self.ident[:]).then_inc(self.mask_ready, 1)
        self.nc.scalar.copy(self.mask[:].rearrange("p k n -> p (k n)"), place).then_inc(self.mask_ready, 1)

    def load_wqkv(self, sp, l):
        src = self.w["wqkv"][bass.ds(l, 1)].rearrange("a (c p) n -> p (a c) n", p=P)
        sp.dma_start(self.raw[:], src).then_inc(self.in_wqkv, 16)

    def load_tab(self, sp, l):
        sp.dma_start(self.tab[:], self.w["tables"].rearrange("(t p) k d -> p t k d", p=P)).then_inc(self.in_tab, 16)
        for n, s in ((0, "q_scale"), (1, "k_scale")):
            row = self.w[s][bass.ds(l, 1)]
            sp.dma_start(self.qks[:, n], row.partition_broadcast(P)).then_inc(self.in_tab, 16)
            sp.dma_start(self.qks[:, 2 + n, 0:HALF], row[:, HALF:DH].partition_broadcast(P)).then_inc(self.in_tab, 16)
            sp.dma_start(self.qks[:, 2 + n, HALF:DH], row[:, 0:HALF].partition_broadcast(P)).then_inc(self.in_tab, 16)

    def split_high(self, act, n):
        act.wait_ge(self.in_wqkv, 16 * n)
        self.nc.scalar.copy(self.wqkv[:, 0].rearrange("p c n -> p (c n)"), self.raw[:].rearrange("p c n -> p (c n)")).then_inc(self.wqkv_high, 1)

    def split_low(self, dve, n):
        dve.wait_ge(self.wqkv_high, n)
        self.nc.vector.tensor_tensor(self.wqkv[:, 1].rearrange("p c n -> p (c n)"), self.raw[:].rearrange("p c n -> p (c n)"),
                                     self.wqkv[:, 0].rearrange("p c n -> p (c n)").bitcast(F32), ALU.subtract).then_inc(self.wqkv_ready, 1)

    def scale_tables(self, dve, n):
        dve.wait_ge(self.in_tab, 16 * 7 * n)
        for k in range(4):
            tb = self.tab[:, :, k, :]
            self.nc.vector.tensor_tensor(tb, tb, self.qks[:, k:k + 1, :].broadcast_to((P, self.nt, DH)), ALU.mult).then_inc(self.tab_ready, 1)
        dve.wait_ge(self.tab_ready, 4 * n)


def flow_block(nc, x, nt, w, x_dram, x1_dram, shared):
    with ExitStack() as ctx:
        def sb(name, shape, dt=F32):
            return ctx.enter_context(nc.sbuf_tensor("f_" + name, shape, dt))

        def sem(name):
            return ctx.enter_context(nc.semaphore("f_" + name))

        psum = ctx.enter_context(nc.psum_tensor("f_psum", [P, 8, 512], F32))
        G = P // FD
        NP = B * P

        raw = sb("raw", [P, DC, 3 * D])
        wqkv = sb("wqkv", [P, 2, DC, 3 * D], F32R)
        wo = sb("wo", [P, DC, D])
        bqk = sb("bqk", [P, 2, DC])
        bv = sb("bv", [P, D])
        bo = sb("bo", [P, D])
        ident = shared.ident
        consts = sb("consts", [P, 3 * P + G + 1])
        tri = consts[:, 0:P]
        head_sum = consts[:, P:P + G]
        block_of = consts[:, P + G:2 * P + G]
        odd = consts[:, 2 * P + G:2 * P + G + 1]
        ones = consts[:, 2 * P + G + 1:3 * P + G + 1]
        spread = sb("spread", [3 * FH, 3 * DC, P])
        count = sb("count", [P, 2, nt])
        mhalf = sb("mhalf", [P, 2])
        euler = sb("euler", [P, B * FH])

        stats = sb("stats", [P, 2, B, 6])
        mv = sb("mv", [P, 2, B, 2])
        ve = sb("ve", [P, 2, B])
        rstd = sb("rstd", [P, 2, B])
        hn = sb("hn", [P, B, D])
        hT = sb("hT", [P, 2, DC, NP], F32R)
        qk = sb("qk", [P, 2, 2 * DC, B, P])
        qk_back = sb("qk_back", [P, 2 * DC, B, P])
        q_odd = sb("q_odd", [P, DC, B, P])
        cum = sb("cum", [P, 2 * DC, B, P])
        carry = sb("carry", [P, 2, 2 * DC, B])
        wtd = sb("wtd", [P, 2 * DC, B, P])
        prod = sb("prod", [P, 2, 2 * DC, B, P])
        recip = sb("recip", [P, B, 2, FH])
        nums = sb("nums", [P, B, 3, FH])
        recip_n = nums[:, :, 0:2, :]
        fac = nums[:, :, 2, :]
        rT = sb("rT", [3 * FH, B, P])
        r_q = sb("r_q", [P, 2, B, FH])
        cons = sb("cons", [P, 2, B, FH])
        alloc = sb("alloc", [P, B, FH])
        fac_spread = sb("fac_spread", [P, DC, B, P])
        cs = sb("cs", [P, B, FH])
        cs_sum = sb("cs_sum", [P, B, FH])
        rcs = sb("rcs", [P, B, FH])
        comp = sb("comp", [P, B, FH])
        vb = sb("vb", [P, 2, B, D])
        vs = sb("vs", [P, B, DC, G, P + FD])
        k_tok = sb("k_tok", [P, B, D])
        st = sb("st", [P, B, 4, 512])
        s_new = sb("s_new", [P, B, D])
        state = sb("state", [P, B, D])
        oT = sb("oT", [P, DC, B, P])
        x1 = sb("x1", [P, B, D])

        names = """in_const in_raw w_high w_ready reset stats_in mv_in ve_in rstd_in hn_in hT_ps hT_high
            hT_low qk_ps v_ps qk_sig v_kept cum1 carry1 prod1 sums1 recip1 recip_n1 rT_ps rT_kept
            spread_ps weighted cum2 carry2 prod2 sums2 cons_done alloc_done fac_done cs_done
            cs_cum cs_added rcs_done comp_done vs_done rq_kept kt_ps kt_kept st_ps st_kept o_ps
            o_kept s_ps s_masked s_added qk_copied q_odd_done fac_ps fac_spread wo_ps bo_added x1_done
            stats_x1 mv_x1 ve_x1 rstd_x1 x_normed""".split()
        S = {n: sem(n) for n in names}
        in_x = [sem(f"in_x{b}") for b in range(B)]
        out_x1 = sem("out_x1")

        def run(step):
            def go(eng):
                step(0, True, False, False)
                step(1, True, True, False)
                with eng.Fori(2, nt) as t:
                    step(t, True, True, True)
                step(nt, False, True, True)
                step(nt + 1, False, False, True)
            return go

        block = ctx.enter_context(nc.Block())
        NCONST = 16 * 9

        def plain(eng):
            eng.wait_ge(S["in_const"], NCONST)

        @block.sync
        def _(sp):
            sp.dma_start(x[:, 0, 0, :], x_dram[0, 0:P]).then_inc(in_x[0], 16)
            sp.dma_start(x[:, 1, 0, :], x_dram[1, 0:P]).then_inc(in_x[1], 16)
            n = S["in_const"]
            sp.dma_start(ident[:], w["ident"]).then_inc(n, 16)
            for j, m in enumerate(("bq", "bk")):
                sp.dma_start(bqk[:, j], w[m].rearrange("(c p) -> p c", p=P), allow_slow_non_contiguous=True).then_inc(n, 16)
            sp.dma_start(bv[:], w["bv"].rearrange("(a d) -> a d", a=1).partition_broadcast(P)).then_inc(n, 16)
            sp.dma_start(bo[:], w["bo"].rearrange("(a d) -> a d", a=1).partition_broadcast(P)).then_inc(n, 16)
            sp.dma_start(consts[:], w["flow_masks"]).then_inc(n, 16)
            sp.dma_start(spread[:], w["head_spread"]).then_inc(n, 16)
            sp.dma_start(count[:], w["counts"]).then_inc(n, 16)

            shared.load_wqkv(sp, 0)
            shared.load_tab(sp, 0)

            with sp.Fori(1, nt) as t:
                for b in range(B):
                    plain(sp)
                    sp.wait_ge(in_x[b], 16 * t)
                    sp.dma_start(x[:, b, t, :], x_dram[b, bass.ds(t * P, P)]).then_inc(in_x[b], 16)
            sp.wait_ge(S["w_ready"], 1)
            shared.load_mask(sp, raw[:].rearrange("p c n -> p (c n)"))
            with sp.Fori(0, nt) as t:
                plain(sp)
                sp.wait_ge(S["x1_done"], t + 1)
                sp.dma_start(x1_dram[:, bass.ds(t * P, P), :].rearrange("b p d -> p b d"), x1[:]).then_inc(out_x1, 16)
            sp.wait_ge(out_x1, 16 * nt)

        @block.tensor
        def _(pe):
            def hT_stage(t):
                pe.wait_ge(S["hn_in"], t + 1)
                for c in range(DC):
                    for b in range(B):
                        mm = nc.tensor.transpose(psum[:, 7, (c * B + b) * P:(c * B + b + 1) * P], hn[:, b, c * P:(c + 1) * P], ident[:])
                mm.then_inc(S["hT_ps"], 1)

            def qk_stage(half):
                for g in range(DC * half, DC * half + DC):
                    n = 0
                    for c in range(DC):
                        for m, a in ((0, 0), (0, 1), (1, 0)):
                            mm = nc.tensor.matmul(psum[:, 4 + g // 2, (g % 2) * NP:(g % 2 + 1) * NP], wqkv[:, m, c, g * P:(g + 1) * P],
                                                  hT[:, a, c, :], start=(n == 0), stop=(n == 5))
                            n += 1
                if half == 1:
                    mm.then_inc(S["qk_ps"], 1)

            def v_stage(t):
                for b in range(B):
                    n = 0
                    for c in range(DC):
                        for a, m in ((0, 0), (0, 1), (1, 0)):
                            mm = nc.tensor.matmul(psum[:, 6, b * D:(b + 1) * D], hT[:, a, c, b * P:(b + 1) * P], wqkv[:, m, c, 2 * D:3 * D],
                                                  start=(n == 0), stop=(n == 5))
                            n += 1
                mm.then_inc(S["v_ps"], 1)

            def head_sums(t, i, bank, ready, made):
                pe.wait_ge(S[ready], t + 1)
                for b in range(B):
                    for g in range(2 * DC):
                        n = (b * 2 * DC + g) * G
                        mm = nc.tensor.matmul(psum[:, bank, n:n + G], prod[:, i, g, b, :], head_sum, start=True, stop=True)
                mm.then_inc(S[made], 1)

            def rT_stage():
                for b in range(B):
                    mm = nc.tensor.transpose(psum[0:3 * FH, 4, b * P:(b + 1) * P], nums[:, b].rearrange("p a h -> p (a h)"), ident[:])
                mm.then_inc(S["rT_ps"], 1)

            def spread_stage(groups, made):
                for g in groups:
                    bank = 4 + g // 2 if g < 2 * DC else 7
                    mm = nc.tensor.matmul(psum[:, bank, (g % 2) * NP:(g % 2 + 1) * NP], spread[:, g, :],
                                          rT[:].rearrange("p b n -> p (b n)"), start=True, stop=True)
                mm.then_inc(S[made], 1)

            def scores(b, half):
                for k in range(2 * half, 2 * half + 2):
                    for r in range(4):
                        c, par = k // 2, k % 2
                        rows = slice(32 * r, 32 * r + (32 if par else 16))
                        q = q_odd[rows, c, b, :] if par else qk_back[rows, c, b, :]
                        mm = nc.tensor.matmul(psum[:, r, k * P:(k + 1) * P], qk_back[rows, DC + c, b, :], q, start=True, stop=True)
                if half == 1:
                    mm.then_inc(S["st_ps"], 1)

            def kt_stage(t):
                for b in range(B):
                    for c in range(DC):
                        mm = nc.tensor.transpose(psum[:, 7, (b * DC + c) * P:(b * DC + c + 1) * P], qk_back[:, DC + c, b, :], ident[:])
                mm.then_inc(S["kt_ps"], 1)

            def cs_stage(t):
                pe.wait_ge(S["cs_done"], t + 1)
                out = psum[:, 5, 0:B * FH]
                nc.tensor.matmul(out, tri, cs[:].rearrange("p b h -> p (b h)"), start=True, stop=False)
                pe.wait_ge(S["cs_added"], t + 2)
                nc.tensor.matmul(out, ones, cs_sum[:].rearrange("p b h -> p (b h)"), start=False, stop=True).then_inc(S["cs_cum"], 1)

            def values(t, b):
                bank = 7 if b == 0 else 1
                pe.wait_ge(S["s_added"], t + 1)
                for c in range(DC):
                    nc.tensor.matmul(psum[:, bank, c * P:(c + 1) * P], state[:, b, c * P:(c + 1) * P], qk_back[:, c, b, :],
                                     start=(c == 0), stop=False, skip_group_check=True)
                pe.wait_ge(S["st_kept"], 2 * t + b + 1)
                pe.wait_ge(S["vs_done"], t + 1)
                for c in range(DC):
                    for j in range(G):
                        r, k = j // 2, 2 * c + j % 2
                        padded = vs[:, b, c].rearrange("p j d -> p (j d)")[:, j * P:(j + 1) * P]
                        mm = nc.tensor.matmul(psum[:, bank, c * P:(c + 1) * P], padded, st[:, b, r, k * P:(k + 1) * P],
                                              start=False, stop=True, skip_group_check=True)
                mm.then_inc(S["o_ps"], 1)

            def state_stage(t):
                for b in range(B):
                    for c in range(DC):
                        mm = nc.tensor.matmul(psum[:, 2, b * D + c * P:b * D + (c + 1) * P], k_tok[:, b, c * P:(c + 1) * P], vs[:, b, c, :, 0:FD],
                                              start=True, stop=True)
                mm.then_inc(S["s_ps"], 1)

            def wo_stage(t):
                pe.wait_ge(S["o_kept"], 2 * t + 2)
                for b in range(B):
                    for c in range(DC):
                        mm = nc.tensor.matmul(psum[:, 6, b * D:(b + 1) * D], oT[:, c, b, :], wo[:, c, :], start=(c == 0), stop=(c == DC - 1))
                mm.then_inc(S["wo_ps"], 1)

            pe.wait_ge(S["in_const"], NCONST)
            pe.wait_ge(S["w_ready"], 1)

            def step(t, front, middle, back):
                v, u = t - 1, t - 2
                if front:
                    hT_stage(t)
                if back:
                    pe.wait_ge(S["qk_copied"], u + 1)
                    pe.wait_ge(S["q_odd_done"], u + 1)
                    pe.wait_ge(S["cons_done"], u + 1)
                    pe.wait_ge(S["s_masked"], u)
                    scores(0, 0)
                    pe.wait_ge(S["x1_done"], u)
                if front:
                    if middle:
                        pe.wait_ge(S["v_kept"], v + 1)
                    pe.wait_ge(S["hT_low"], t + 1)
                    v_stage(t)
                if back:
                    scores(0, 1)
                if middle:
                    pe.wait_ge(S["recip_n1"], v + 1)
                if back:
                    pe.wait_ge(S["fac_done"], u + 1)
                    pe.wait_ge(S["qk_sig"], t if front else nt)
                    cs_stage(u)
                if middle or back:
                    rT_stage()
                if back:
                    kt_stage(u)
                if middle:
                    pe.wait_ge(S["qk_sig"], v + 1)
                    if back:
                        pe.wait_ge(S["rcs_done"], u + 1)
                if middle or back:
                    pe.wait_ge(S["rT_kept"], t)
                if middle:
                    spread_stage(range(2 * DC), "spread_ps")
                if back:
                    pe.wait_ge(S["kt_kept"], u + 1)
                    spread_stage(range(2 * DC, 3 * DC), "fac_ps")
                if back:
                    pe.wait_ge(S["st_kept"], 2 * u + 1)
                    scores(1, 0)
                if front:
                    if middle:
                        pe.wait_ge(S["weighted"], v + 1)
                    qk_stage(0)
                if back:
                    scores(1, 1)
                if front:
                    qk_stage(1)
                if back:
                    pe.wait_ge(S["fac_spread"], u + 1)
                    values(u, 0)
                    pe.wait_ge(S["st_kept"], 2 * u + 2)
                if middle:
                    head_sums(v, 1, 0, "prod2", "sums2")
                if back:
                    values(u, 1)
                    state_stage(u)
                if front:
                    head_sums(t, 0, 4, "prod1", "sums1")
                if back:
                    if front:
                        pe.wait_ge(S["v_kept"], t + 1)
                    wo_stage(u)

            run(step)(pe)

        @block.scalar
        def _(act):
            for j, m in enumerate(("Wq", "Wk", "Wv")):
                act.dma_start(raw[:, :, j * D:(j + 1) * D], w[m].rearrange("(c p) n -> p c n", p=P)).then_inc(S["in_raw"], 16)
            act.dma_start(wo[:], w["Wo"].rearrange("(c p) n -> p c n", p=P)).then_inc(S["in_const"], 16)
            act.wait_ge(S["in_raw"], 48)
            nc.scalar.copy(wqkv[:, 0].rearrange("p c n -> p (c n)"), raw[:].rearrange("p c n -> p (c n)")).then_inc(S["w_high"], 1)
            act.wait_ge(S["in_const"], NCONST)

            def step(t, front, middle, back):
                v, u = t - 1, t - 2
                if front:
                    act.wait_ge(S["hT_ps"], t + 1)
                    if middle:
                        act.wait_ge(S["qk_ps"], t)
                    nc.scalar.copy(hT[:, 0].rearrange("p c n -> p (c n)"), psum[:, 7, :]).then_inc(S["hT_high"], 1)
                if middle or back:
                    act.wait_ge(S["rT_ps"], t)
                    nc.scalar.copy(rT[:].rearrange("p b n -> p (b n)"), psum[0:3 * FH, 4, 0:NP]).then_inc(S["rT_kept"], 1)
                if back:
                    act.wait_ge(S["kt_ps"], u + 1)
                    nc.scalar.copy(k_tok[:].rearrange("p b n -> p (b n)"), psum[:, 7, :]).then_inc(S["kt_kept"], 1)
                    act.wait_ge(S["fac_ps"], u + 1)
                    act.wait_ge(S["o_kept"], 2 * u)
                    nc.scalar.copy(fac_spread[:].rearrange("p c b n -> p (c b n)"), psum[:, 7, :]).then_inc(S["fac_spread"], 1)
                if front:
                    act.wait_ge(S["qk_ps"], t + 1)
                    if back:
                        act.wait_ge(S["prod2"], u + 1)
                        act.wait_ge(S["qk_copied"], u + 1)
                    for g in range(2 * DC):
                        a = nc.scalar.activation(qk[:, t % 2, g].rearrange("p b n -> p (b n)"), psum[:, 4 + g // 2, (g % 2) * NP:(g % 2 + 1) * NP],
                                                 ACT.Sigmoid, bias=bqk[:, g // DC, g % DC:g % DC + 1], scale=1.0)
                    a.then_inc(S["qk_sig"], 1)
                if middle:
                    act.wait_ge(S["cons_done"], v + 1)
                    if back:
                        act.wait_ge(S["fac_done"], v)
                    nc.scalar.activation(alloc[:], cons[:, 0], ACT.Sigmoid).then_inc(S["alloc_done"], 1)
                    act.wait_ge(S["qk_sig"], v + 1)
                    if back:
                        act.wait_ge(S["o_ps"], 2 * u + 2)
                        act.wait_ge(S["q_odd_done"], v)
                    nc.scalar.copy(qk_back[:].rearrange("p g b n -> p (g b n)"), qk[:, v % 2].rearrange("p g b n -> p (g b n)")).then_inc(S["qk_copied"], 1)
            def with_weights(t, front, middle, back):
                if back and not middle:
                    shared.round_mask(act, raw[:].rearrange("p c n -> p (c n)"))
                    shared.split_high(act, 1)
                step(t, front, middle, back)

            run(with_weights)(act)

        @block.vector
        def _(dve):
            def norm_in(t):
                for b in range(B):
                    plain(dve)
                    dve.wait_ge(in_x[b], 16 * (t + 1))
                    a = nc.vector.bn_stats(stats[:, 0, b], x[:, b, t, :])
                a.then_inc(S["stats_in"], 1)
                norm_rest("in", 0, t)
                for b in range(B):
                    a = nc.vector.tensor_scalar(hn[:, b], x[:, b, t, :], mv[:, 0, b, 0:1], rstd[:, 0, b:b + 1], ALU.subtract, ALU.mult)
                a.then_inc(S["hn_in"], 1)

            def norm_rest(tag, i, t):
                plain(dve)
                dve.wait_ge(S["stats_" + tag], t + 1)
                for b in range(B):
                    a = nc.vector.bn_aggr(mv[:, i, b], stats[:, i, b])
                a.then_inc(S["mv_" + tag], 1)
                dve.wait_ge(S["mv_" + tag], t + 1)
                nc.vector.tensor_scalar(ve[:, i], mv[:, i, :, 1], LN_EPS, None, ALU.add).then_inc(S["ve_" + tag], 1)
                dve.wait_ge(S["rstd_" + tag], t + 1)

            def scans(t, i, src, name):
                dve.wait_ge(S["reset"], 6)
                for g in range(2 * DC):
                    for b in range(B):
                        a = nc.vector.tensor_tensor_scan(cum[:, g, b, :], ones, src[:, g, b, :], carry[:, i, g, b:b + 1], ALU.mult, ALU.add)
                a.then_inc(S[name], 1)
                dve.wait_ge(S[name], t + 1)
                nc.vector.tensor_copy(carry[:, i], cum[:, :, :, P - 1]).then_inc(S["carry1" if i == 0 else "carry2"], 1)

            def products(t, i, qkt, name):
                for a in range(2):
                    f = lambda v, n: v[:, n * DC:(n + 1) * DC].rearrange("p c b n -> p (c b n)")
                    ins = nc.vector.scalar_tensor_tensor(f(prod[:, i], a), f(qkt, a), FLOW_EPS, f(cum, 1 - a), ALU.add, ALU.mult)
                ins.then_inc(S[name], 1)

            nc.vector.memset(carry[:], FLOW_EPS).then_inc(S["reset"], 1)
            norm_in(0)
            dve.wait_ge(S["w_high"], 1)
            nc.vector.tensor_tensor(wqkv[:, 1].rearrange("p c n -> p (c n)"), raw[:].rearrange("p c n -> p (c n)"),
                                    wqkv[:, 0].rearrange("p c n -> p (c n)").bitcast(F32), ALU.subtract).then_inc(S["w_ready"], 1)

            def mask_scores(u, b):
                dve.wait_ge(S["st_ps"], 2 * u + b + 1)
                nc.vector.tensor_tensor(st[:, b].rearrange("p r (k i) -> p (r k) i", k=4), psum[:, 0:4, :].rearrange("p r (k i) -> p (r k) i", k=4),
                                        tri.rearrange("p (o i) -> p o i", o=1).broadcast_to((P, 16, P)), ALU.mult).then_inc(S["st_kept"], 1)

            def keep_o(u, b):
                dve.wait_ge(S["fac_spread"], u + 1)
                dve.wait_ge(S["wo_ps"], u)
                dve.wait_ge(S["o_ps"], 2 * u + b + 1)
                nc.vector.tensor_tensor(oT[:, :, b, :], psum[:, 7 if b == 0 else 1, 0:D].rearrange("p (c n) -> p c n", c=DC),
                                        fac_spread[:, :, b, :], ALU.mult).then_inc(S["o_kept"], 1)

            def low(t):
                dve.wait_ge(S["hT_high"], t + 1)
                nc.vector.tensor_tensor(hT[:, 1].rearrange("p c n -> p (c n)"), psum[:, 7, :],
                                        hT[:, 0].rearrange("p c n -> p (c n)").bitcast(F32), ALU.subtract).then_inc(S["hT_low"], 1)

            def step(t, front, middle, back, more):
                v, u = t - 1, t - 2
                if back:
                    dve.wait_ge(S["cs_cum"], u + 1)
                    nc.vector.reciprocal(rcs[:].rearrange("p b h -> p (b h)"), psum[:, 5, 0:B * FH]).then_inc(S["rcs_done"], 1)
                    dve.wait_ge(S["rcs_done"], u + 1)
                    dve.wait_ge(S["vs_done"], u)
                    nc.vector.scalar_tensor_tensor(comp[:], cs[:], count[:, 0, bass.ds(u, 1)], rcs[:], ALU.mult, ALU.mult).then_inc(S["comp_done"], 1)
                    mask_scores(u, 0)
                if middle:
                    dve.wait_ge(S["spread_ps"], v + 1)
                    dve.wait_ge(S["qk_sig"], v + 1)
                    nc.vector.tensor_tensor(wtd[:].rearrange("p g b n -> p (g b n)"), psum[:, 4:6, :].rearrange("p a n -> p (a n)"),
                                            qk[:, v % 2].rearrange("p g b n -> p (g b n)"), ALU.mult).then_inc(S["weighted"], 1)
                    dve.wait_ge(S["weighted"], v + 1)
                    dve.wait_ge(S["prod1"], v + 1)
                    dve.wait_ge(S["carry1"], v + 1)
                    if back:
                        dve.wait_ge(S["carry2"], v)
                    scans(v, 1, wtd, "cum2")
                    if back:
                        dve.wait_ge(S["sums2"], v)
                    products(v, 1, qk[:, v % 2], "prod2")
                if front:
                    dve.wait_ge(S["v_ps"], t + 1)
                    if back:
                        dve.wait_ge(S["vs_done"], u + 1)
                    nc.vector.tensor_tensor(vb[:, t % 2], psum[:, 6, :].rearrange("p (b d) -> p b d", b=B),
                                            bv[:].rearrange("p (o d) -> p o d", o=1).broadcast_to((P, B, D)), ALU.add).then_inc(S["v_kept"], 1)
                if back:
                    mask_scores(u, 1)
                if more:
                    norm_in(t + 1)
                if back:
                    keep_o(u, 0)
                if front:
                    dve.wait_ge(S["qk_sig"], t + 1)
                    if middle:
                        dve.wait_ge(S["carry1"], t)
                        dve.wait_ge(S["prod2"], v + 1)
                        dve.wait_ge(S["carry2"], v + 1)
                        dve.wait_ge(S["sums1"], t)
                    scans(t, 0, qk[:, t % 2], "cum1")
                    products(t, 0, qk[:, t % 2], "prod1")
                if middle:
                    dve.wait_ge(S["sums2"], v + 1)
                    if back:
                        dve.wait_ge(S["alloc_done"], v)
                        dve.wait_ge(S["cs_done"], v)
                    nc.vector.tensor_scalar(cons[:].rearrange("p a b h -> p b a h"), psum[:, 0, 0:2 * B * FH].rearrange("p (b a h) -> p b a h", b=B, a=2),
                                            count[:, 1, bass.ds(v, 1)], None, ALU.mult).then_inc(S["cons_done"], 1)
                if back:
                    keep_o(u, 1)
                    dve.wait_ge(S["s_ps"], u + 1)
                    dve.wait_ge(S["s_added"], u + 1)
                    nc.vector.tensor_tensor(s_new[:].rearrange("p b (c f) -> p (b c) f", f=P), psum[:, 2, :].rearrange("p (a f) -> p a f", f=P),
                                            block_of.rearrange("p (o f) -> p o f", o=1).broadcast_to((P, B * DC, P)), ALU.mult).then_inc(S["s_masked"], 1)
                if front:
                    dve.wait_ge(S["sums1"], t + 1)
                    if middle:
                        dve.wait_ge(S["rT_ps"], t)
                    nc.vector.reciprocal(recip[:].rearrange("p b a h -> p (b a h)"), psum[:, 4, 0:2 * B * FH]).then_inc(S["recip1"], 1)
                    dve.wait_ge(S["recip1"], t + 1)
                    nc.vector.tensor_scalar(recip_n.rearrange("p b a h -> p b (a h)"), recip[:].rearrange("p b a h -> p b (a h)"),
                                            count[:, 0, bass.ds(t, 1)], None, ALU.mult).then_inc(S["recip_n1"], 1)
                    nc.vector.tensor_copy(r_q[:, t % 2], recip[:, :, 0, :]).then_inc(S["rq_kept"], 1)
                if middle:
                    dve.wait_ge(S["alloc_done"], v + 1)
                    dve.wait_ge(S["rq_kept"], v + 1)
                    dve.wait_ge(S["rT_ps"], t)
                    nc.vector.tensor_tensor(fac, alloc[:], r_q[:, v % 2], ALU.mult).then_inc(S["fac_done"], 1)
                    dve.wait_ge(S["qk_copied"], v + 1)
                    nc.vector.tensor_scalar(q_odd[:].rearrange("p c b n -> p (c b n)"), qk_back[:, 0:DC].rearrange("p c b n -> p (c b n)"),
                                            odd, None, ALU.mult).then_inc(S["q_odd_done"], 1)
                if back:
                    dve.wait_ge(S["wo_ps"], u + 1)
                    dve.wait_ge(S["bo_added"], u + 1)
                    if not (isinstance(t, int) and t <= 2):
                        dve.wait_ge(out_x1, 16 * u)
                    nc.vector.tensor_tensor(x1[:], psum[:, 6, :].rearrange("p (b d) -> p b d", b=B), x[:, :, u, :], ALU.add).then_inc(S["x1_done"], 1)
                if more:
                    low(t + 1)
                if back:
                    dve.wait_ge(S["x1_done"], u + 1)
                    for b in range(B):
                        a = nc.vector.bn_stats(stats[:, 1, b], x1[:, b])
                    a.then_inc(S["stats_x1"], 1)
                    norm_rest("x1", 1, u)
                    for b in range(B):
                        a = nc.vector.tensor_scalar(x[:, b, u, :], x1[:, b], mv[:, 1, b, 0:1], rstd[:, 1, b:b + 1], ALU.subtract, ALU.mult)
                    a.then_inc(S["x_normed"], 1)

            low(0)
            step(0, True, False, False, True)
            step(1, True, True, False, True)
            with dve.Fori(2, nt - 1) as t:
                step(t, True, True, True, True)
            step(nt - 1, True, True, True, False)
            step(nt, False, True, True, False)
            shared.split_low(dve, 1)
            shared.scale_tables(dve, 1)
            step(nt + 1, False, False, True, False)

        @block.gpsimd
        def _(pool):
            nc.gpsimd.memset(mhalf[:], -0.5).then_inc(S["reset"], 1)
            nc.gpsimd.memset(euler[:], float(np.e)).then_inc(S["reset"], 1)
            nc.gpsimd.memset(cs[:], 0.0).then_inc(S["reset"], 1)
            nc.gpsimd.memset(vs[:], 0.0).then_inc(S["reset"], 1)
            nc.gpsimd.memset(nums[:], 0.0).then_inc(S["reset"], 1)
            nc.gpsimd.memset(cs_sum[:], 0.0).then_inc(S["cs_added"], 1)
            nc.gpsimd.memset(state[:], 0.0).then_inc(S["s_added"], 1)
            pool.wait_ge(S["reset"], 6)
            pool.wait_ge(S["cs_added"], 1)
            pool.wait_ge(S["s_added"], 1)
            pool.wait_ge(S["in_const"], NCONST)

            def rstd_(tag, i, t):
                pool.wait_ge(S["ve_" + tag], t + 1)
                nc.gpsimd.tensor_tensor(rstd[:, i], ve[:, i], mhalf[:], ALU.pow).then_inc(S["rstd_" + tag], 1)

            def step(t, middle, back, more):
                v, u = t - 1, t - 2
                if back:
                    pool.wait_ge(S["comp_done"], u + 1)
                    pool.wait_ge(S["s_ps"], u)
                    pool.wait_ge(S["v_kept"], u + 1)
                    nc.gpsimd.tensor_tensor(vs[:].rearrange("p b c j n -> p (b c j) n")[:, :, 0:FD], vb[:, u % 2].rearrange("p b (h d) -> p (b h) d", d=FD),
                                            comp[:].rearrange("p b (h o) -> p (b h) o", o=1).broadcast_to((P, B * FH, FD)), ALU.mult).then_inc(S["vs_done"], 1)
                    nc.gpsimd.tensor_tensor(x[:, :, u, :], x[:, :, u, :], bo[:].rearrange("p (o d) -> p o d", o=1).broadcast_to((P, B, D)),
                                            ALU.add).then_inc(S["bo_added"], 1)
                if more:
                    rstd_("in", 0, t + 1)
                if middle:
                    pool.wait_ge(S["cons_done"], v + 1)
                    pool.wait_ge(S["cs_cum"], v)
                    pool.wait_ge(S["comp_done"], v)
                    nc.gpsimd.tensor_tensor(cs_sum[:], cs_sum[:], cs[:], ALU.add).then_inc(S["cs_added"], 1)
                    pool.wait_ge(S["cs_added"], v + 2)
                    nc.gpsimd.tensor_tensor(cs[:].rearrange("p b h -> p (b h)"), euler[:], cons[:, 1].rearrange("p b h -> p (b h)"), ALU.pow).then_inc(S["cs_done"], 1)
                if back:
                    pool.wait_ge(S["s_masked"], u + 1)
                    pool.wait_ge(S["o_ps"], 2 * u + 2)
                    nc.gpsimd.tensor_tensor(state[:], state[:], s_new[:], ALU.add).then_inc(S["s_added"], 1)
                    rstd_("x1", 1, u)

            rstd_("in", 0, 0)
            step(0, False, False, True)
            step(1, True, False, True)
            with pool.Fori(2, nt - 1) as t:
                step(t, True, True, True)
            step(nt - 1, True, True, False)
            step(nt, True, True, False)
            step(nt + 1, False, True, False)


def layers_block(nc, x, nt, depth, w, shared, x1_dram, out_dram):
    with ExitStack() as ctx:
        def sb(name, shape, dt=F32):
            return ctx.enter_context(nc.sbuf_tensor(name, shape, dt))

        def sem(name):
            return ctx.enter_context(nc.semaphore(name))

        psum = ctx.enter_context(nc.psum_tensor("psum", [P, 8, 512], F32))
        sc_ps = psum[:, 0:4, :]

        wqkv, raw, tab = shared.wqkv, shared.raw, shared.tab
        w1 = sb("w1", [P, 2, DC, 2 * HID], F32R)
        wo = sb("wo", [P, INNER // P, D])
        w2 = sb("w2", [P, NF, D])
        b1 = sb("b1", [P, 2, NF])
        b2 = sb("b2", [P, D])
        lng = sb("lng", [P, DC])
        lnb = sb("lnb", [P, DC])
        mask, ident, ident_bf = shared.mask, shared.ident, shared.ident_bf

        xst = sb("xst", [P, B, D])
        hT = sb("hT", [P, B, 2, DC, P + 2], F32R)
        t1 = sb("t1", [P, B, 2 * INNER])
        t2 = sb("t2", [P, 2 * INNER])
        sq = sb("sq", [P, 2 * INNER])
        ss = sb("ss", [P, B, 2 * HEADS])
        rn = sb("rn", [P, B, 2 * HEADS])
        zeros = sb("zeros", [P, D])
        mhalf = sb("mhalf", [P, 2 * HEADS])
        qT = sb("qT", [P, HEADS // 2, P])
        kT = sb("kT", [P, B, HEADS // 2, 2, P])
        v = sb("v", [P, B, 2, INNER])
        nmax = sb("nmax", [P, HEADS])
        psm = sb("psm", [P, HEADS])
        rsm = sb("rsm", [P, HEADS])
        probs = sb("probs", [P, HEADS, 2, P])
        probsT = sb("probsT", [P, 4, 512])
        o = sb("o", [P, INNER])
        oT = sb("oT", [P, INNER // P, P])
        hs = sb("hs", [P, B, P])
        lastrow = sb("lastrow", [1, B, P])
        stats = sb("stats", [P, B, 12])
        mv = sb("mv", [P, B, 2])
        ve = sb("ve", [P, B])
        rstd = sb("rstd", [P, B])
        hn = sb("hn", [P, B, D])
        h2T = sb("h2T", [P, 2, DC, B * P], F32R)
        gate = sb("gate", [P, 2, B * P])
        hid = sb("hid", [P, NF, B * P])
        x1t = sb("x1t", [P, B, D])

        in_wqkv, wqkv_ready = shared.in_wqkv, shared.wqkv_ready
        in_w1 = sem("in_w1")
        in_wo = sem("in_wo")
        in_small = sem("in_small")
        half_ready = sem("half_ready")
        w1_ready = sem("w1_ready")
        w1_high = sem("w1_high")
        w1_bias_mm = sem("w1_bias_mm")
        b1_ready = sem("b1_ready")
        state_reset = sem("state_reset")
        x_staged = sem("x_staged")
        xT_ps = sem("xT_ps")
        col_carried = sem("col_carried")
        hT_high = sem("hT_high")
        hT_low = sem("hT_low")
        qk_ps = sem("qk_ps")
        v_ps = sem("v_ps")
        v_kept = sem("v_kept")
        squares = sem("squares")
        rot_parts = sem("rot_parts")
        sumsq = sem("sumsq")
        sumsq_raw = sem("sumsq_raw")
        rnorm = sem("rnorm")
        rot_sum = sem("rot_sum")
        qk_final = sem("qk_final")
        qkT_ps = sem("qkT_ps")
        qT_kept = sem("qT_kept")
        kT_kept = sem("kT_kept")
        scores_ps = sem("scores_ps")
        max_found = sem("max_found")
        exp_done = sem("exp_done")
        pT_ps = sem("pT_ps")
        pT_act = sem("pT_act")
        pT_dve = sem("pT_dve")
        o_ps = sem("o_ps")
        rsum = sem("rsum")
        o_kept = sem("o_kept")
        oT_ps = sem("oT_ps")
        oT_kept = sem("oT_kept")
        wo_ps = sem("wo_ps")
        x_attn = sem("x_attn")
        row_copied = sem("row_copied")
        in_row = [sem(f"in_row{b}") for b in range(B)]
        in_hs = [sem(f"in_hs{b}") for b in range(B)]
        stats_done = sem("stats_done")
        mv_done = sem("mv_done")
        ve_done = sem("ve_done")
        rstd_done = sem("rstd_done")
        hn_done = sem("hn_done")
        b2_added = sem("b2_added")
        h2T_ps = sem("h2T_ps")
        h2T_high = sem("h2T_high")
        h2T_low = sem("h2T_low")
        up_ps = sem("up_ps")
        gelu_done = sem("gelu_done")
        hid_done = sem("hid_done")
        down_ps = sem("down_ps")
        x_ffn = sem("x_ffn")
        in_x1 = sem("in_x1")
        x1_added = sem("x1_added")
        out_sent = sem("out_sent")

        def plain(eng):
            eng.wait_ge(in_wqkv, 16)

        def place(h):
            return (h // 4) * 4 + (h % 2) * 2 + (h // 2) % 2

        def done(l, t, b):
            return l * (B * nt) + t * B + b + 1

        def fdone(l, t):
            return l * nt + t + 1

        def rdone(l, t, r):
            return (l * nt + t) * NF + r + 1

        NSMALL = 9
        HEAD_AT = sorted(range(HEADS), key=place)
        UP_BANK = [5, 4, 6, 5, 4, 6]

        def at(t):
            return t % nt if isinstance(t, int) else t

        def run(eng, start, step, ffn_tail):
            start()
            step(0, 0, first=True, last=False, edge=True, final=False)
            with eng.Fori(0, depth - 1) as l:
                with eng.Fori(1, nt - 1) as t:
                    step(l, t, first=False, last=False, edge=False, final=False)
                step(l, nt - 1, first=False, last=False, edge=False, final=False)
                step(l + 1, 0, first=False, last=False, edge=True, final=False)
            with eng.Fori(1, nt - 1) as t:
                step(depth - 1, t, first=False, last=False, edge=False, final=True)
            step(depth - 1, nt - 1, first=False, last=True, edge=False, final=True)
            ffn_tail(depth - 1, nt - 1)

        assert nt % 2 == 0 and nt > 2 and depth > 1

        block = ctx.enter_context(nc.Block())

        @block.sync
        def _(sp):
            def load_w1(l):
                plain(sp)
                sp.wait_ge(wqkv_ready, l + 1)
                sp.dma_start(raw[:, :, 0:2 * HID], w["w1"][bass.ds(l, 1)].rearrange("a (c p) n -> p (a c) n", p=P)).then_inc(in_w1, 16)
                sp.dma_start(lng[:], w["ln_g"][bass.ds(l, 1)].rearrange("a (c p) -> p (a c)", p=P), allow_slow_non_contiguous=True).then_inc(in_small, 16)
                sp.dma_start(lnb[:], w["ln_b"][bass.ds(l, 1)].rearrange("a (c p) -> p (a c)", p=P), allow_slow_non_contiguous=True).then_inc(in_small, 16)

            def load_wo(l):
                sp.dma_start(wo[:], w["wo"][bass.ds(l, 1)].rearrange("a (c p) n -> p (a c) n", p=P)).then_inc(in_wo, 16)

            def load_ffn(l):
                sp.dma_start(b2[:], w["b2"][bass.ds(l, 1)].partition_broadcast(P)).then_inc(in_small, 16)
                for g in range(2):
                    row = w["b1"][bass.ds(l, 1), g * HID:(g + 1) * HID]
                    sp.dma_start(b1[0:FS, g, 0:NF - 1], row[:, 0:(NF - 1) * FS].rearrange("a (f p) -> p (a f)", p=FS), allow_slow_non_contiguous=True).then_inc(in_small, 16)
                    sp.dma_start(b1[0:FLAST, g, NF - 1:NF], row[:, (NF - 1) * FS:HID].rearrange("a (f p) -> p (a f)", p=FLAST), allow_slow_non_contiguous=True).then_inc(in_small, 16)
                sp.dma_start(w2[0:FS, 0:NF - 1, :], w["w2"][bass.ds(l, 1), 0:(NF - 1) * FS].rearrange("a (f p) n -> p (a f) n", p=FS)).then_inc(in_small, 16)
                sp.dma_start(w2[0:FLAST, NF - 1, :], w["w2"][bass.ds(l, 1), (NF - 1) * FS:HID].rearrange("a p n -> (a p) n")).then_inc(in_small, 16)

            def start():
                load_wo(0)
                load_ffn(0)

            def shift(l, t, b):
                n = done(l, t, b)
                n = n if isinstance(n, int) else sp.snap(n)
                plain(sp)
                sp.wait_ge(x_attn, n)
                sp.wait_ge(row_copied, n)
                sp.dma_start(lastrow[0:1, b], x[P - 1:P, b, at(t), P:D]).then_inc(in_row[b], 16)
                sp.dma_start(hs[1:P, b], x[0:P - 1, b, at(t), P:D]).then_inc(in_hs[b], 16)

            def step(l, t, first, last, edge, final):
                if edge:
                    load_w1(l)
                if edge and not first:
                    plain(sp)
                    sp.wait_ge(wo_ps, done(l, t - 1, 1))
                    load_wo(l)
                if not last and isinstance(t, int) and t == nt - 1:
                    plain(sp)
                    sp.wait_ge(rot_parts, done(l, t, 1))
                    shared.load_tab(sp, l + 1)
                if final:
                    load_x1(t - 1)
                shift(l, t, 0)
                if edge and not first:
                    plain(sp)
                    sp.wait_ge(down_ps, fdone(l, t - 1))
                    sp.wait_ge(b2_added, done(l, t - 1, 1))
                    load_ffn(l)
                if final:
                    store(t - 1)
                shift(l, t, 1)
                if edge:
                    plain(sp)
                    sp.wait_ge(w1_ready, l + 1)
                    sp.wait_ge(w1_bias_mm, l + 1)
                    shared.load_wqkv(sp, (l + 1) % depth)

            def ffn_tail(l, t):
                load_x1(t)
                store(t)
                sp.wait_ge(out_sent, 16 * nt)

            def load_x1(t):
                plain(sp)
                sp.wait_ge(x1_added, t)
                sp.dma_start(x1t[:], x1_dram[:, bass.ds(t * P, P), :].rearrange("b p d -> p b d")).then_inc(in_x1, 16)

            def store(t):
                plain(sp)
                sp.wait_ge(x1_added, t + 1)
                sp.dma_start(out_dram[:, bass.ds(t * P, P), :].rearrange("b p d -> p b d"), x[:, :, t, :]).then_inc(out_sent, 16)

            run(sp, start, step, ffn_tail)
            sp.wait_ge(in_wqkv, 16 * (depth + 1))

        @block.tensor
        def _(pe):
            def transposed_x(l, t, b, bank):
                pe.wait_ge(x_staged, done(l, t, b))
                for c in range(DC):
                    mm = nc.tensor.transpose(psum[:, bank, c * P:(c + 1) * P], xst[:, b, c * P:(c + 1) * P], ident[:])
                mm.then_inc(xT_ps, 1)

            def project(b, j, bank):
                n = 0
                for c in range(DC):
                    for a, m in ((0, 0), (0, 1), (1, 0)):
                        mm = nc.tensor.matmul(psum[:, bank, :], hT[:, b, a, c, 1 - c:1 - c + P],
                                              wqkv[:, m, c, j * INNER:(j + 1) * INNER], start=(n == 0), stop=(n == 5))
                        n += 1
                return mm

            def qk(l, t, b, bank):
                pe.wait_ge(hT_low, done(l, t, b))
                project(b, 0, bank)
                project(b, 1, bank + 1).then_inc(qk_ps, 1)

            def vproj(l, t, b, bank):
                project(b, 2, bank).then_inc(v_ps, 1)

            def qkT(l, t, b, bank):
                pe.wait_ge(qk_final, done(l, t, b))
                for n in range(HEADS):
                    mm = nc.tensor.transpose(psum[:, bank + n // 4, (n % 4) * P:(n % 4 + 1) * P], t1[:, b, n * P:(n + 1) * P], ident[:])
                mm.then_inc(qkT_ps, 1)

            def scores(l, t, b, kind):
                pe.wait_ge(qT_kept, done(l, t, b))
                pe.wait_ge(kT_kept, done(l, t, b))
                for half in range(2):
                    for k in range(2):
                        nc.tensor.matmul(psum[:, 2 * half + k, :], ident_bf[:], mask[:, kind, :], start=True, stop=True)
                    for h in range(4 * half, 4 * half + 4):
                        r = (h % 2) * DH
                        n = place(h)
                        mm = nc.tensor.matmul(psum[:, n // 2, (n % 2) * 256:(n % 2 + 1) * 256], qT[r:r + DH, h // 2, :],
                                              kT[r:r + DH, b, h // 2], start=False, stop=True, skip_group_check=True)
                    mm.then_inc(scores_ps, 1)

            def probsT_(l, t, b, half):
                pe.wait_ge(exp_done, 2 * done(l, t, b) - 1 + half)
                for n in range(HEADS * half, HEADS * half + HEADS):
                    mm = nc.tensor.transpose(psum[:, n // 4, (n % 4) * P:(n % 4 + 1) * P], probs[:, n // 2, n % 2, :], ident[:])
                mm.then_inc(pT_ps, 1)

            def values(l, t, b, bank):
                pe.wait_ge(pT_act, done(l, t, b))
                pe.wait_ge(pT_dve, done(l, t, b))
                pe.wait_ge(v_kept, done(l, t, b))
                for h in range(HEADS):
                    for s in range(2):
                        n = 2 * place(h) + s
                        mm = nc.tensor.matmul(psum[:, bank, h * DH:(h + 1) * DH], probsT[:, n // 4, (n % 4) * P:(n % 4 + 1) * P],
                                              v[:, b, s, h * DH:(h + 1) * DH], start=(s == 0), stop=(s == 1))
                mm.then_inc(o_ps, 1)

            def transposed_o(l, t, b, bank):
                pe.wait_ge(o_kept, done(l, t, b))
                for c in range(INNER // P):
                    mm = nc.tensor.transpose(psum[:, bank, c * P:(c + 1) * P], o[:, c * P:(c + 1) * P], ident[:])
                mm.then_inc(oT_ps, 1)

            def out_proj(l, t, b, bank):
                pe.wait_ge(oT_kept, done(l, t, b))
                for c in range(INNER // P):
                    mm = nc.tensor.matmul(psum[:, bank, 0:D], oT[:, c, :], wo[:, c, :], start=(c == 0), stop=(c == INNER // P - 1))
                mm.then_inc(wo_ps, 1)

            def transposed_h(l, t):
                pe.wait_ge(hn_done, done(l, t, 1))
                for c in range(DC):
                    for b in range(B):
                        mm = nc.tensor.transpose(psum[:, 4, (c * B + b) * P:(c * B + b + 1) * P], hn[:, b, c * P:(c + 1) * P], ident[:])
                mm.then_inc(h2T_ps, 1)

            def up(l, t, r):
                n = FC[r]
                for g in range(2):
                    k = 0
                    for c in range(DC):
                        for m, a in ((0, 0), (0, 1), (1, 0)):
                            f0 = g * HID + r * FS
                            mm = nc.tensor.matmul(psum[0:n, UP_BANK[r], g * 256:(g + 1) * 256], w1[:, m, c, f0:f0 + n],
                                                  h2T[:, a, c, :], start=(k == 0), stop=(k == 5))
                            k += 1
                mm.then_inc(up_ps, 1)

            def down(l, t, b):
                if b == 0:
                    pe.wait_ge(hid_done, rdone(l, t, NF - 1))
                for f in range(NF):
                    n = FC[f]
                    mm = nc.tensor.matmul(psum[:, 5, b * D:(b + 1) * D], hid[0:n, f, b * P:(b + 1) * P], w2[0:n, f, :],
                                          start=(f == 0), stop=(f == NF - 1))
                if b == B - 1:
                    mm.then_inc(down_ps, 1)

            def start():
                l = 0
                pe.wait_ge(wqkv_ready, 1)
                pe.wait_ge(shared.mask_ready, 2)
                transposed_x(l, 0, 0, 4)
                qk(l, 0, 0, 0)
                vproj(l, 0, 0, 4)
                transposed_x(l, 0, 1, 5)
                qk(l, 0, 1, 6)
                vproj(l, 0, 1, 5)
                qkT(l, 0, 0, 0)
                pe.wait_ge(state_reset, 1)

            def ups(l, t, rounds):
                for r in rounds:
                    if r >= 3:
                        pe.wait_ge(hid_done, rdone(l, t, r - 3))
                    up(l, t, r)

            def step(l, t, first, last, edge, final):
                if not last:
                    if first:
                        pe.wait_ge(v_kept, done(l, t, 0))
                    transposed_x(l, t + 1, 0, 4)
                scores(l, t, 0, 2 if edge else t % 2)
                if not last:
                    pe.wait_ge(hT_low, done(l, t + 1, 0))
                if first:
                    pe.wait_ge(v_kept, done(l, t, 1))
                else:
                    pe.wait_ge(x_attn, done(l, t - 1, 1))
                qkT(l, t, 1, 4)
                if not last:
                    if isinstance(t, int) and t == nt - 1:
                        pe.wait_ge(wqkv_ready, l + 2)
                    qk(l, t + 1, 0, 6)
                pe.wait_ge(qT_kept, done(l, t, 1))
                pe.wait_ge(kT_kept, done(l, t, 1))
                probsT_(l, t, 0, 0)
                if not first:
                    transposed_h(l, t - 1)
                probsT_(l, t, 0, 1)
                if not first:
                    pe.wait_ge(h2T_low, fdone(l, t - 1))
                    ups(l, t - 1, (0, 1))
                if not last:
                    pe.wait_ge(rot_parts, done(l, t + 1, 0))
                    pe.wait_ge(squares, done(l, t + 1, 0))
                if not first:
                    ups(l, t - 1, (2,))
                values(l, t, 0, 7)
                if not first:
                    ups(l, t - 1, (3, 4, 5))
                scores(l, t, 1, 2 if edge else t % 2)
                transposed_o(l, t, 0, 7)
                if not last:
                    if not first:
                        pe.wait_ge(hid_done, rdone(l, t - 1, 4))
                    vproj(l, t + 1, 0, 4)
                if not last:
                    if not first:
                        pe.wait_ge(hid_done, rdone(l, t - 1, 5))
                    transposed_x(l, t + 1, 1, 6)
                if edge:
                    pe.wait_ge(in_wo, 16 * (l + 1))
                out_proj(l, t, 0, 7)
                if not first:
                    down(l, t - 1, 0)
                if not last:
                    pe.wait_ge(x_attn, done(l, t, 0))
                    qk(l, t + 1, 1, 6)
                if not first:
                    down(l, t - 1, 1)
                probsT_(l, t, 1, 0)
                probsT_(l, t, 1, 1)
                if not first:
                    pe.wait_ge(x_ffn, fdone(l, t - 1))
                if not last:
                    vproj(l, t + 1, 1, 5)
                    pe.wait_ge(v_kept, done(l, t + 1, 0))
                values(l, t, 1, 4)
                transposed_o(l, t, 1, 4)
                if not last:
                    qkT(l, t + 1, 0, 0)
                    pe.wait_ge(v_kept, done(l, t + 1, 1))
                out_proj(l, t, 1, 5)
                if edge:
                    pe.wait_ge(in_w1, 16 * (l + 1))
                    pe.wait_ge(in_small, 16 * NSMALL * (l + 1))
                    for g in range(2):
                        for f in range(NF):
                            for c in range(DC):
                                f0 = g * HID + f * FS
                                mm = nc.tensor.matmul(psum[0:FC[f], 4, g * NF + f:g * NF + f + 1], raw[:, c, f0:f0 + FC[f]],
                                                      lnb[:, c:c + 1], start=(c == 0), stop=(c == DC - 1))
                    mm.then_inc(w1_bias_mm, 1)
                    pe.wait_ge(b1_ready, l + 1)
                    pe.wait_ge(w1_ready, l + 1)

            def ffn_tail(l, t):
                pe.wait_ge(x_attn, done(l, t, 1))
                transposed_h(l, t)
                pe.wait_ge(h2T_low, fdone(l, t))
                ups(l, t, range(NF))
                down(l, t, 0)
                down(l, t, 1)

            run(pe, start, step, ffn_tail)

        @block.scalar
        def _(act):
            def high(l, t, b, bank):
                act.wait_ge(xT_ps, done(l, t, b))
                act.wait_ge(col_carried, done(l, t, b))
                nc.scalar.copy(hT[:, b, 0, :, 1:P + 1], psum[:, bank, 0:D].rearrange("p (c n) -> p c n", c=DC)).then_inc(hT_high, 1)

            def square(l, t, b, bank):
                act.wait_ge(rot_parts, done(l, t, b))
                before = done(l, t, b) - 1
                if not (isinstance(before, int) and before == 0):
                    act.wait_ge(sumsq_raw, before)
                nc.scalar.activation(sq[:], psum[:, bank:bank + 2, :].rearrange("p a n -> p (a n)"), ACT.Square).then_inc(squares, 1)

            def keep_v(l, t, b, bank):
                act.wait_ge(v_ps, done(l, t, b))
                if not (isinstance(t, int) and t == 0):
                    act.wait_ge(o_ps, done(l, t - 1, b))
                nc.scalar.copy(v[:, b, t % 2, :], psum[:, bank, :]).then_inc(v_kept, 1)

            def keep_qT(l, t, b, bank):
                act.wait_ge(qkT_ps, done(l, t, b))
                nc.scalar.copy(qT[:].rearrange("p c n -> p (c n)"), psum[:, bank, :]).then_inc(qT_kept, 1)

            def exps(l, t, b, half):
                act.wait_ge(max_found, 2 * done(l, t, b) - 1 + half)
                before = done(l, t, b) - 1
                if half == 0 and not (isinstance(before, int) and before == 0):
                    act.wait_ge(rsum, before)
                for n in range(4 * half, 4 * half + 4):
                    h = HEAD_AT[n]
                    a = nc.scalar.activation(probs[:, n].rearrange("p s j -> p (s j)"), psum[:, n // 2, (n % 2) * 256:(n % 2 + 1) * 256],
                                             ACT.Exp, bias=nmax[:, n:n + 1], scale=1.0, accum_out=psm[:, h:h + 1])
                a.then_inc(exp_done, 1)

            def keep_pT(l, t, b):
                act.wait_ge(pT_ps, 2 * done(l, t, b) - 1)
                nc.scalar.copy(probsT[:, 0:2].rearrange("p a n -> p (a n)"), psum[:, 0:2, :].rearrange("p a n -> p (a n)"))
                act.wait_ge(pT_ps, 2 * done(l, t, b))
                nc.scalar.copy(probsT[:, 2], psum[:, 2, :]).then_inc(pT_act, 1)

            def keep_oT(l, t, b, bank):
                act.wait_ge(oT_ps, done(l, t, b))
                nc.scalar.copy(oT[:].rearrange("p c n -> p (c n)"), psum[:, bank, :]).then_inc(oT_kept, 1)

            def high2(l, t):
                act.wait_ge(h2T_ps, fdone(l, t))
                nc.scalar.copy(h2T[:, 0].rearrange("p c n -> p (c n)"), psum[:, 4, :]).then_inc(h2T_high, 1)

            def gelu(l, t, r):
                act.wait_ge(up_ps, rdone(l, t, r))
                n = FC[r]
                if r >= 2:
                    act.wait_ge(hid_done, rdone(l, t, r - 2))
                nc.scalar.activation(gate[0:n, r % 2, :], psum[0:n, UP_BANK[r], 256:512], ACT.Gelu, bias=b1[0:n, 1, r:r + 1]).then_inc(gelu_done, 1)

            def start():
                l = 0
                high(l, 0, 0, 4)
                square(l, 0, 0, 0)
                keep_v(l, 0, 0, 4)
                high(l, 0, 1, 5)
                square(l, 0, 1, 6)
                keep_v(l, 0, 1, 5)
                keep_qT(l, 0, 0, 0)

            def step(l, t, first, last, edge, final):
                if not last:
                    high(l, t + 1, 0, 4)
                    if isinstance(t, int) and t == nt - 1:
                        act.wait_ge(v_ps, done(l, t, 1))
                        shared.split_high(act, l + 2)
                exps(l, t, 0, 0)
                keep_qT(l, t, 1, 4)
                exps(l, t, 0, 1)
                if not first:
                    high2(l, t - 1)
                if not last:
                    square(l, t + 1, 0, 6)
                keep_pT(l, t, 0)
                if not first:
                    for r in range(NF):
                        gelu(l, t - 1, r)
                exps(l, t, 1, 0)
                keep_oT(l, t, 0, 7)
                exps(l, t, 1, 1)
                if not last:
                    keep_v(l, t + 1, 0, 4)
                    high(l, t + 1, 1, 6)
                    square(l, t + 1, 1, 6)
                keep_pT(l, t, 1)
                if edge:
                    if not first:
                        act.wait_ge(up_ps, rdone(l, t - 1, NF - 1))
                    act.wait_ge(in_w1, 16 * (l + 1))
                    act.wait_ge(in_small, 16 * NSMALL * (l + 1))
                    for c in range(DC):
                        nc.scalar.activation(w1[:, 0, c, :], raw[:, c, 0:2 * HID], ACT.Copy, scale=lng[:, c:c + 1]).then_inc(w1_high, 1)
                if not last:
                    keep_v(l, t + 1, 1, 5)
                keep_oT(l, t, 1, 4)
                if not last:
                    keep_qT(l, t + 1, 0, 0)

            def ffn_tail(l, t):
                high2(l, t)
                for r in range(NF):
                    gelu(l, t, r)

            run(act, start, step, ffn_tail)

        @block.vector
        def _(dve):
            def low(l, t, b, bank):
                dve.wait_ge(hT_high, done(l, t, b))
                nc.vector.tensor_tensor(hT[:, b, 1, :, 1:P + 1], psum[:, bank, 0:D].rearrange("p (c n) -> p c n", c=DC),
                                        hT[:, b, 0, :, 1:P + 1].bitcast(F32), ALU.subtract).then_inc(hT_low, 1)

            def rotate_same(l, t, b, bank):
                dve.wait_ge(qk_ps, done(l, t, b))
                q = psum[:, bank:bank + 2, :].rearrange("p a (h d) -> p a h d", h=HEADS)
                o1 = t1[:, b].rearrange("p (a h d) -> p a h d", a=2, h=HEADS)
                ta = tab[:, at(t), 0:2].rearrange("p a (o d) -> p a o d", o=1).broadcast_to((P, 2, HEADS, DH))
                nc.vector.tensor_tensor(o1, q, ta, ALU.mult)

            def rotate_swapped(l, t, b, bank):
                before = done(l, t, b) - 1
                if not (isinstance(before, int) and before == 0):
                    dve.wait_ge(rot_sum, before)
                q = psum[:, bank:bank + 2, :].rearrange("p a (h d) -> p a h d", h=HEADS)
                o2 = t2[:].rearrange("p (a h d) -> p a h d", a=2, h=HEADS)
                tb = tab[:, at(t), 2:4].rearrange("p a (o d) -> p a o d", o=1).broadcast_to((P, 2, HEADS, DH))
                nc.vector.tensor_tensor(o2[:, :, :, 0:HALF], q[:, :, :, HALF:DH], tb[:, :, :, 0:HALF], ALU.mult)
                nc.vector.tensor_tensor(o2[:, :, :, HALF:DH], q[:, :, :, 0:HALF], tb[:, :, :, HALF:DH], ALU.mult).then_inc(rot_parts, 1)

            def rotate(l, t, b, bank):
                rotate_same(l, t, b, bank)
                rotate_swapped(l, t, b, bank)

            def sum_squares(l, t, b):
                dve.wait_ge(squares, done(l, t, b))
                nc.vector.tensor_reduce(ss[:, b], sq[:].rearrange("p (h d) -> p h d", d=DH), AX.X, ALU.add).then_inc(sumsq_raw, 1)
                dve.wait_ge(sumsq_raw, done(l, t, b))
                nc.vector.tensor_scalar(ss[:, b], ss[:, b], 1e-24, None, ALU.max).then_inc(sumsq, 1)

            def add_rotated(l, t, b):
                dve.wait_ge(rot_parts, done(l, t, b))
                nc.vector.tensor_tensor(t1[:, b], t1[:, b], t2[:], ALU.add).then_inc(rot_sum, 1)

            def scale_qk(l, t, b):
                dve.wait_ge(rnorm, done(l, t, b))
                dve.wait_ge(rot_sum, done(l, t, b))
                v1 = t1[:, b].rearrange("p (h d) -> p h d", d=DH)
                rb = rn[:, b].rearrange("p (h o) -> p h o", o=1).broadcast_to((P, 2 * HEADS, DH))
                nc.vector.tensor_tensor(v1, v1, rb, ALU.mult).then_inc(qk_final, 1)

            def keep_kT(l, t, b, bank):
                dve.wait_ge(qkT_ps, done(l, t, b))
                nc.vector.tensor_copy(kT[:, b, :, t % 2, :], psum[:, bank, :].rearrange("p (c n) -> p c n", n=P)).then_inc(kT_kept, 1)

            def maxima(l, t, b, half):
                dve.wait_ge(scores_ps, 2 * done(l, t, b) - 1 + half)
                nc.vector.tensor_reduce(nmax[:, 4 * half:4 * half + 4], sc_ps[:, 2 * half:2 * half + 2].rearrange("p k (h j) -> p (k h) j", h=2),
                                        AX.X, ALU.max, negate=True).then_inc(max_found, 1)

            def keep_pT(l, t, b):
                dve.wait_ge(pT_ps, 2 * done(l, t, b))
                nc.vector.tensor_copy(probsT[:, 3], psum[:, 3, :]).then_inc(pT_dve, 1)

            def normalise_o(l, t, b, bank):
                dve.wait_ge(exp_done, 2 * done(l, t, b))
                nc.vector.reciprocal(rsm[:], psm[:]).then_inc(rsum, 1)
                dve.wait_ge(rsum, done(l, t, b))
                dve.wait_ge(o_ps, done(l, t, b))
                rb = rsm[:].rearrange("p (h o) -> p h o", o=1).broadcast_to((P, HEADS, DH))
                nc.vector.tensor_tensor(o[:].rearrange("p (h d) -> p h d", d=DH), psum[:, bank, :].rearrange("p (h d) -> p h d", d=DH), rb,
                                        ALU.mult).then_inc(o_kept, 1)

            def add_attn(l, t, b, bank):
                dve.wait_ge(wo_ps, done(l, t, b))
                nc.vector.tensor_tensor(x[:, b, at(t), :], psum[:, bank, 0:D], x[:, b, at(t), :], ALU.add).then_inc(x_attn, 1)

            def ln_stats(l, t, b):
                plain(dve)
                dve.wait_ge(x_attn, done(l, t, b))
                nc.vector.bn_stats(stats[:, b, 0:6], x[:, b, at(t), 0:P])
                dve.wait_ge(in_hs[b], 16 * fdone(l, t))
                dve.wait_ge(row_copied, done(l, t, b))
                nc.vector.bn_stats(stats[:, b, 6:12], hs[:, b]).then_inc(stats_done, 1)
                plain(dve)
                dve.wait_ge(stats_done, done(l, t, b))
                nc.vector.bn_aggr(mv[:, b], stats[:, b]).then_inc(mv_done, 1)
                dve.wait_ge(mv_done, done(l, t, b))
                nc.vector.tensor_scalar(ve[:, b:b + 1], mv[:, b, 1:2], LN_EPS, None, ALU.add).then_inc(ve_done, 1)

            def ln_apply(l, t, b):
                dve.wait_ge(rstd_done, done(l, t, b))
                nc.vector.tensor_scalar(hn[:, b, 0:P], x[:, b, at(t), 0:P], mv[:, b, 0:1], rstd[:, b:b + 1], ALU.subtract, ALU.mult)
                nc.vector.tensor_scalar(hn[:, b, P:D], hs[:, b], mv[:, b, 0:1], rstd[:, b:b + 1], ALU.subtract, ALU.mult).then_inc(hn_done, 1)

            def low2(l, t):
                dve.wait_ge(h2T_high, fdone(l, t))
                nc.vector.tensor_tensor(h2T[:, 1].rearrange("p c n -> p (c n)"), psum[:, 4, :],
                                        h2T[:, 0].rearrange("p c n -> p (c n)").bitcast(F32), ALU.subtract).then_inc(h2T_low, 1)

            def gated(l, t, r):
                dve.wait_ge(gelu_done, rdone(l, t, r))
                n = FC[r]
                nc.vector.scalar_tensor_tensor(hid[0:n, r, :], psum[0:n, UP_BANK[r], 0:256], b1[0:n, 0, r:r + 1], gate[0:n, r % 2, :],
                                               ALU.add, ALU.mult).then_inc(hid_done, 1)

            def add_ffn(l, t, final):
                if final:
                    dve.wait_ge(in_x1, 16 * (t + 1))
                dve.wait_ge(down_ps, fdone(l, t))
                dve.wait_ge(b2_added, done(l, t, 1))
                nc.vector.tensor_tensor(x[:, :, at(t), :], psum[:, 5, :].rearrange("p (b d) -> p b d", b=B), x[:, :, at(t), :], ALU.add).then_inc(x_ffn, 1)

            def start():
                l = 0
                low(l, 0, 0, 4)
                rotate(l, 0, 0, 0)
                sum_squares(l, 0, 0)
                low(l, 0, 1, 5)
                add_rotated(l, 0, 0)
                scale_qk(l, 0, 0)
                rotate(l, 0, 1, 6)
                sum_squares(l, 0, 1)
                keep_kT(l, 0, 0, 1)
                add_rotated(l, 0, 1)
                scale_qk(l, 0, 1)

            def step(l, t, first, last, edge, final):
                if not last:
                    low(l, t + 1, 0, 4)
                if not last and isinstance(t, int) and t == nt - 1:
                    shared.split_low(dve, l + 2)
                maxima(l, t, 0, 0)
                maxima(l, t, 0, 1)
                keep_kT(l, t, 1, 5)
                if not first:
                    ln_stats(l, t - 1, 1)
                    ln_apply(l, t - 1, 1)
                if not last:
                    if isinstance(t, int) and t == nt - 1:
                        shared.scale_tables(dve, l + 2)
                    rotate_same(l, t + 1, 0, 6)
                if not first:
                    low2(l, t - 1)
                if not last:
                    rotate_swapped(l, t + 1, 0, 6)
                keep_pT(l, t, 0)
                if not last:
                    sum_squares(l, t + 1, 0)
                if not first:
                    gated(l, t - 1, 0)
                    gated(l, t - 1, 1)
                    gated(l, t - 1, 2)
                normalise_o(l, t, 0, 7)
                if not last:
                    add_rotated(l, t + 1, 0)
                    scale_qk(l, t + 1, 0)
                if not first:
                    for r in range(3, NF):
                        gated(l, t - 1, r)
                maxima(l, t, 1, 0)
                maxima(l, t, 1, 1)
                if not last:
                    low(l, t + 1, 1, 6)
                add_attn(l, t, 0, 7)
                if not last:
                    rotate(l, t + 1, 1, 6)
                if not first:
                    add_ffn(l, t - 1, final)
                keep_pT(l, t, 1)
                ln_stats(l, t, 0)
                ln_apply(l, t, 0)
                if not last:
                    sum_squares(l, t + 1, 1)
                normalise_o(l, t, 1, 4)
                if not last:
                    add_rotated(l, t + 1, 1)
                    keep_kT(l, t + 1, 0, 1)
                    scale_qk(l, t + 1, 1)
                add_attn(l, t, 1, 5)
                if edge:
                    dve.wait_ge(w1_high, DC * (l + 1))
                    for c in range(DC):
                        a = nc.vector.scalar_tensor_tensor(w1[:, 1, c, :], raw[:, c, 0:2 * HID], lng[:, c:c + 1], w1[:, 0, c, :].bitcast(F32),
                                                           ALU.mult, ALU.subtract)
                    a.then_inc(w1_ready, 1)
                    dve.wait_ge(w1_bias_mm, l + 1)
                    for g in range(2):
                        nc.vector.tensor_tensor(b1[0:FS, g, 0:NF - 1], psum[0:FS, 4, g * NF:g * NF + NF - 1], b1[0:FS, g, 0:NF - 1], ALU.add)
                        a = nc.vector.tensor_tensor(b1[0:FLAST, g, NF - 1:NF], psum[0:FLAST, 4, g * NF + NF - 1:g * NF + NF],
                                                    b1[0:FLAST, g, NF - 1:NF], ALU.add)
                    a.then_inc(b1_ready, 1)

            def ffn_tail(l, t):
                ln_stats(l, t, 1)
                ln_apply(l, t, 1)
                low2(l, t)
                for r in range(NF):
                    gated(l, t, r)
                add_ffn(l, t, True)

            run(dve, start, step, ffn_tail)

        @block.gpsimd
        def _(pool):
            nc.gpsimd.memset(mhalf[:], -0.5).then_inc(half_ready, 1)
            nc.gpsimd.memset(zeros[:], 0.0).then_inc(half_ready, 1)
            pool.wait_ge(half_ready, 2)

            def stage(l, t, b, first):
                if not first:
                    pool.wait_ge(xT_ps, done(l, t - 1, b))
                nc.gpsimd.tensor_tensor(xst[:, b], x[:, b, at(t), :], zeros[:], ALU.add).then_inc(x_staged, 1)
                if not first:
                    pool.wait_ge(v_ps, done(l, t - 1, b))
                    pool.wait_ge(hT_low, done(l, t - 1, b))
                nothing = zeros[:, 0:2].rearrange("p (a o) -> p a o", o=1)
                carried = nothing if isinstance(t, int) and t % nt == 0 else hT[:, b, :, 1, P:P + 1].bitcast(F32)
                nc.gpsimd.tensor_tensor(hT[:, b, :, 1, 0:1], carried, nothing, ALU.add).then_inc(col_carried, 1)

            def qk_norm(l, t, b):
                pool.wait_ge(sumsq, done(l, t, b))
                nc.gpsimd.tensor_tensor(rn[:, b], ss[:, b], mhalf[:], ALU.pow).then_inc(rnorm, 1)

            def row(l, t, b, first, edge):
                if not first:
                    pool.wait_ge(hn_done, done(l, t - 1, b))
                    pool.wait_ge(in_row[b], 16 * fdone(l, t - 1))
                above = zeros[0:1, 0:P] if edge else lastrow[0:1, b]
                nc.gpsimd.tensor_tensor(hs[0:1, b], above, zeros[0:1, 0:P], ALU.add).then_inc(row_copied, 1)

            def ln_rstd(l, t, b):
                pool.wait_ge(ve_done, done(l, t, b))
                nc.gpsimd.tensor_tensor(rstd[:, b:b + 1], ve[:, b:b + 1], mhalf[:, 0:1], ALU.pow).then_inc(rstd_done, 1)

            def add_b2(l, t, b):
                pool.wait_ge(hn_done, done(l, t, b))
                pool.wait_ge(in_row[b], 16 * fdone(l, t))
                nc.gpsimd.tensor_tensor(x[:, b, at(t), :], x[:, b, at(t), :], b2[:], ALU.add).then_inc(b2_added, 1)

            def add_x1(l, t):
                plain(pool)
                pool.wait_ge(x_ffn, fdone(l, t))
                nc.gpsimd.tensor_tensor(x[:, :, t, :], x[:, :, t, :], x1t[:], ALU.add).then_inc(x1_added, 1)

            def start():
                l = 0
                stage(l, 0, 0, True)
                stage(l, 0, 1, True)
                nc.gpsimd.memset(kT[:, :, :, 1, :], 0.0)
                nc.gpsimd.memset(v[:, :, 1, :], 0.0).then_inc(state_reset, 1)
                qk_norm(l, 0, 0)
                qk_norm(l, 0, 1)

            def step(l, t, first, last, edge, final):
                if not last:
                    stage(l, t + 1, 0, False)
                if not first:
                    ln_rstd(l, t - 1, 1)
                row(l, t, 0, first, edge)
                row(l, t, 1, first, edge)
                if not last:
                    qk_norm(l, t + 1, 0)
                if not first:
                    add_b2(l, t - 1, 1)
                if not last:
                    stage(l, t + 1, 1, False)
                ln_rstd(l, t, 0)
                if not last:
                    qk_norm(l, t + 1, 1)
                if edge:
                    pool.wait_ge(in_small, 16 * NSMALL * (l + 1))
                add_b2(l, t, 0)
                if final:
                    add_x1(l, t - 1)

            def ffn_tail(l, t):
                ln_rstd(l, t, 1)
                add_b2(l, t, 1)
                add_x1(l, t)

            run(pool, start, step, ffn_tail)


def build_program(nc, ins, out):
    _, n, _ = ins["x"].shape
    nt = n // P
    depth = ins["wqkv"].shape[0]
    x1_dram = nc.dram_tensor("x1_scratch", (B, n, D), F32).ap()
    with ExitStack() as ctx:
        x = ctx.enter_context(nc.sbuf_tensor("x", [P, B, nt, D], F32))
        shared = Shared(nc, ctx, nt, ins)
        flow_block(nc, x, nt, ins, ins["x"], x1_dram, shared)
        layers_block(nc, x, nt, depth, ins, shared, x1_dram, out)


_ATTN = ["x", "Wq", "bq", "Wk", "bk", "Wv", "bv", "Wo", "bo"]
_FFN = ["wqkv", "q_scale", "k_scale", "wo", "ln_g", "ln_b", "w1", "b1", "w2", "b2"]


def kernel(**inputs):
    import concourse.bacc as bacc
    from concourse.bass_utils import run_bass_kernel_spmd

    arrays = {n: np.ascontiguousarray(inputs["L0_attn_" + n]) for n in _ATTN}
    arrays |= {n: np.ascontiguousarray(inputs["L0_ffn_" + n]) for n in _FFN}
    n = arrays["x"].shape[1]
    arrays |= {
        "ident": np.eye(P, dtype=np.float32),
        "tables": position_tables(n),
        "masks": window_masks(),
        "flow_masks": flow_masks(),
        "head_spread": head_spread(),
        "counts": counts(n // P),
    }
    nc = bacc.Bacc("TRN2", target_bir_lowering=False, num_devices=1)
    ins = {k: nc.dram_tensor(f"in_{k}", a.shape, mybir.dt.from_np(a.dtype), kind="ExternalInput").ap() for k, a in arrays.items()}
    out = nc.dram_tensor("out", arrays["x"].shape, F32, kind="ExternalOutput").ap()
    build_program(nc, ins, out)
    r = run_bass_kernel_spmd(nc, [{f"in_{k}": a for k, a in arrays.items()}], core_ids=[0])
    return r.results[0]["out"]
```
